# Optimizing a Trainium2 kernel written in Bass

```python
import numpy as np
import jax
import jax.numpy as jnp

def _softmax(x, axis=-1):
    return jax.nn.softmax(x, axis=axis)

def _gelu(x):
    return jax.nn.gelu(x, approximate=True)

def _silu(x):
    return jax.nn.silu(x)

def _sigmoid(x):
    return jax.nn.sigmoid(x)

def _layernorm(x, axis=-1, eps=1e-05):
    m = jnp.mean(x, axis=axis, keepdims=True)
    v = jnp.var(x, axis=axis, keepdims=True)
    return (x - m) / jnp.sqrt(v + eps)

def _scatter_add(tgt, idx, src, axis=0):
    return tgt.at[idx].add(src)

def _segment_sum(src, seg, n):
    return jax.ops.segment_sum(src, seg, n)
kernel_name = 'mk_adaln_d2_jaxref_r8_80685b'

def setup_inputs(seed: int=0):
    np.random.seed(seed)
    _w = jnp.asarray

    def _L0_attn_setup():
        import jax, jax.numpy as jnp
        import numpy as np
        HIDDEN = 128
        N_HEADS = 16
        key = jax.random.key(seed)
        kx, kq, kk, kv = jax.random.split(key, 4)
        b, s, h = (2, 256, HIDDEN)
        scale = 1.0 / np.sqrt(h)
        x = jax.random.normal(kx, (b, s, h), dtype=jnp.float32)
        Wq = jax.random.normal(kq, (h, h), dtype=jnp.float32) * scale
        Wk = jax.random.normal(kk, (h, h), dtype=jnp.float32) * scale
        Wv = jax.random.normal(kv, (h, h), dtype=jnp.float32) * scale
        return {'x': x, 'Wq': Wq, 'Wk': Wk, 'Wv': Wv}
    _L0_attn_in = _L0_attn_setup()

    def _L0_ffn_setup():
        import jax, jax.numpy as jnp
        import numpy as np
        E = 16
        K = 4
        G = 4
        TG = 2
        NS = 2
        H = 128
        I = 176
        SCALE = 1.0

        def _gate(x2d, gate_w, gate_bias):
            T = x2d.shape[0]
            logits = x2d.astype(jnp.float32) @ gate_w.astype(jnp.float32).T
            scores = jax.nn.sigmoid(logits)
            sfc = scores + gate_bias[None, :]
            grp = sfc.reshape(T, G, E // G)
            top2, _ = jax.lax.top_k(grp, 2)
            group_scores = top2.sum(-1)
            _, gidx = jax.lax.top_k(group_scores, TG)
            gmask = jnp.zeros((T, G), sfc.dtype).at[jnp.arange(T)[:, None], gidx].set(1.0)
            smask = jnp.repeat(gmask, E // G, axis=1) > 0
            tmp = jnp.where(smask, sfc, 0.0)
            _, topk_idx = jax.lax.top_k(tmp, K)
            topk_w = jnp.take_along_axis(scores, topk_idx, axis=1)
            topk_w = topk_w / (topk_w.sum(-1, keepdims=True) + 1e-20)
            return (topk_idx, topk_w * SCALE)
        key = jax.random.key(seed)
        ks = jax.random.split(key, 8)
        bound = 1.0 / np.sqrt(H)
        return {'hidden_states': jax.random.normal(ks[0], (1, 128, H), jnp.float32), 'gate_w': jax.random.uniform(ks[1], (E, H), jnp.float32, -bound, bound), 'gate_bias': jnp.zeros((E,), jnp.float32), 'gate_proj': jax.random.normal(ks[2], (E, I, H), jnp.float32) * 0.02, 'up_proj': jax.random.normal(ks[3], (E, I, H), jnp.float32) * 0.02, 'down_proj': jax.random.normal(ks[4], (E, H, I), jnp.float32) * 0.02, 'shared_gate_w': jax.random.normal(ks[5], (I * NS, H), jnp.float32) * 0.02, 'shared_up_w': jax.random.normal(ks[6], (I * NS, H), jnp.float32) * 0.02, 'shared_down_w': jax.random.normal(ks[7], (H, I * NS), jnp.float32) * 0.02}
    _L0_ffn_in = _L0_ffn_setup()
    _L0_c = _w((lambda *s: np.random.randn(*s).astype(np.float32) * 0.05)(4, 128))
    _L0_wmod = _w((lambda *s: np.random.randn(*s).astype(np.float32) * 0.05)(128, 6 * 128) * 128 ** (-0.5))

    def _L1_attn_setup():
        import math
        import jax, jax.numpy as jnp
        import numpy as np
        DIM = 128
        key = jax.random.key(seed)
        ks = jax.random.split(key, 5)
        B, T, d = (4, 512, DIM)
        x = jax.random.normal(ks[0], (B, T, d), dtype=jnp.float32)
        std = 0.02
        Wq = jax.random.normal(ks[1], (d, d), dtype=jnp.float32) * std
        Wk = jax.random.normal(ks[2], (d, d), dtype=jnp.float32) * std
        Wv = jax.random.normal(ks[3], (d, d), dtype=jnp.float32) * std
        Wo = jax.random.normal(ks[4], (d, d), dtype=jnp.float32) * std
        decay_logit = jnp.asarray(3.0, dtype=jnp.float32)
        out_scale = jnp.asarray(0.1, dtype=jnp.float32)
        return {'x': x, 'Wq': Wq, 'Wk': Wk, 'Wv': Wv, 'Wo': Wo, 'decay_logit': decay_logit, 'out_scale': out_scale}
    _L1_attn_in = _L1_attn_setup()

    def _L1_ffn_setup():
        import jax, jax.numpy as jnp
        import numpy as np
        B, S, D = (2, 256, 128)
        E, K, H = (8, 2, 512)
        CAP_FACTOR = 1.0

        def _moe_forward(x, wg, w1, b1, w2, b2):
            Bb, Ss, Dd = x.shape
            T = Bb * Ss
            cap = int(K * CAP_FACTOR * ((T + E - 1) // E))
            xt = x.reshape(T, Dd)
            logits = xt @ wg
            scores = jax.nn.softmax(logits, axis=-1)
            gates_k, idx_k = jax.lax.top_k(scores, K)
            gates_k = gates_k / jnp.sum(gates_k, axis=-1, keepdims=True)
            masks = jax.nn.one_hot(idx_k, E, dtype=jnp.int32)
            m = jnp.transpose(masks, (1, 0, 2)).reshape(K * T, E)
            locs_full = jnp.cumsum(m, axis=0) - 1
            loc = jnp.sum(locs_full * m, axis=-1)
            loc = loc.reshape(K, T).T
            valid = (loc < cap).astype(xt.dtype)
            loc_c = jnp.clip(loc, 0, cap - 1)
            contrib = (xt[:, None, :] * valid[:, :, None]).reshape(T * K, Dd)
            disp = jnp.zeros((E, cap, Dd), xt.dtype)
            disp = disp.at[idx_k.reshape(-1), loc_c.reshape(-1)].add(contrib)
            h = jax.nn.relu(jnp.einsum('ecd,edh->ech', disp, w1) + b1[:, None, :])
            out = jnp.einsum('ech,ehd->ecd', h, w2) + b2[:, None, :]
            gathered = out[idx_k, loc_c]
            y = jnp.einsum('tk,tkd->td', gates_k * valid, gathered)
            return y.reshape(Bb, Ss, Dd)
        key = jax.random.key(seed)
        ks = jax.random.split(key, 6)
        scale_in = 1.0 / np.sqrt(D)
        scale_h = 1.0 / np.sqrt(H)
        return {'x': jax.random.normal(ks[0], (B, S, D), jnp.float32), 'wg': jax.random.normal(ks[1], (D, E), jnp.float32) * scale_in, 'w1': jax.random.normal(ks[2], (E, D, H), jnp.float32) * scale_in, 'b1': jnp.zeros((E, H), jnp.float32), 'w2': jax.random.normal(ks[3], (E, H, D), jnp.float32) * scale_h, 'b2': jnp.zeros((E, D), jnp.float32)}
    _L1_ffn_in = _L1_ffn_setup()
    _L1_c = _w((lambda *s: np.random.randn(*s).astype(np.float32) * 0.05)(4, 128))
    _L1_wmod = _w((lambda *s: np.random.randn(*s).astype(np.float32) * 0.05)(128, 6 * 128) * 128 ** (-0.5))
    _d = {'L0_attn_x': _L0_attn_in['x'], 'L0_attn_Wq': _L0_attn_in['Wq'], 'L0_attn_Wk': _L0_attn_in['Wk'], 'L0_attn_Wv': _L0_attn_in['Wv'], 'L0_ffn_gate_w': _L0_ffn_in['gate_w'], 'L0_ffn_gate_bias': _L0_ffn_in['gate_bias'], 'L0_ffn_gate_proj': _L0_ffn_in['gate_proj'], 'L0_ffn_up_proj': _L0_ffn_in['up_proj'], 'L0_ffn_down_proj': _L0_ffn_in['down_proj'], 'L0_ffn_shared_gate_w': _L0_ffn_in['shared_gate_w'], 'L0_ffn_shared_up_w': _L0_ffn_in['shared_up_w'], 'L0_ffn_shared_down_w': _L0_ffn_in['shared_down_w'], 'L0_c': _L0_c, 'L0_wmod': _L0_wmod, 'L1_attn_Wq': _L1_attn_in['Wq'], 'L1_attn_Wk': _L1_attn_in['Wk'], 'L1_attn_Wv': _L1_attn_in['Wv'], 'L1_attn_Wo': _L1_attn_in['Wo'], 'L1_attn_decay_logit': _L1_attn_in['decay_logit'], 'L1_attn_out_scale': _L1_attn_in['out_scale'], 'L1_ffn_wg': _L1_ffn_in['wg'], 'L1_ffn_w1': _L1_ffn_in['w1'], 'L1_ffn_b1': _L1_ffn_in['b1'], 'L1_ffn_w2': _L1_ffn_in['w2'], 'L1_ffn_b2': _L1_ffn_in['b2'], 'L1_c': _L1_c, 'L1_wmod': _L1_wmod}
    _x0 = _d['L0_attn_x']
    _d['L0_attn_x'] = jax.random.normal(jax.random.fold_in(jax.random.key(seed), 1), (4, 1024, 128), dtype=_x0.dtype)
    del _x0
    return _d

def reference(L0_attn_x, L0_attn_Wq, L0_attn_Wk, L0_attn_Wv, L0_ffn_gate_w, L0_ffn_gate_bias, L0_ffn_gate_proj, L0_ffn_up_proj, L0_ffn_down_proj, L0_ffn_shared_gate_w, L0_ffn_shared_up_w, L0_ffn_shared_down_w, L0_c, L0_wmod, L1_attn_Wq, L1_attn_Wk, L1_attn_Wv, L1_attn_Wo, L1_attn_decay_logit, L1_attn_out_scale, L1_ffn_wg, L1_ffn_w1, L1_ffn_b1, L1_ffn_w2, L1_ffn_b2, L1_c, L1_wmod):

    def _L0_attn_ref(x, Wq, Wk, Wv):
        import jax, jax.numpy as jnp
        import numpy as np
        HIDDEN = 128
        N_HEADS = 16
        b, s, h = x.shape
        n = N_HEADS
        d = h // n
        q = (x @ Wq.T).reshape(b, s, n, d).transpose(0, 2, 1, 3)
        k = (x @ Wk.T).reshape(b, s, n, d).transpose(0, 2, 1, 3)
        v = (x @ Wv.T).reshape(b, s, n, d).transpose(0, 2, 1, 3)
        score = jnp.einsum('bnqd,bnkd->bnqk', q, k)
        prob = jax.nn.softmax(score, axis=-1)
        attn = jnp.einsum('bnqk,bnkd->bnqd', prob, v)
        return attn.transpose(0, 2, 1, 3).reshape(b, s, h)

    def _L0_ffn_ref(hidden_states, gate_w, gate_bias, gate_proj, up_proj, down_proj, shared_gate_w, shared_up_w, shared_down_w):
        import jax, jax.numpy as jnp
        import numpy as np
        E = 16
        K = 4
        G = 4
        TG = 2
        NS = 2
        H = 128
        I = 176
        SCALE = 1.0

        def _gate(x2d, gate_w, gate_bias):
            T = x2d.shape[0]
            logits = x2d.astype(jnp.float32) @ gate_w.astype(jnp.float32).T
            scores = jax.nn.sigmoid(logits)
            sfc = scores + gate_bias[None, :]
            grp = sfc.reshape(T, G, E // G)
            top2, _ = jax.lax.top_k(grp, 2)
            group_scores = top2.sum(-1)
            _, gidx = jax.lax.top_k(group_scores, TG)
            gmask = jnp.zeros((T, G), sfc.dtype).at[jnp.arange(T)[:, None], gidx].set(1.0)
            smask = jnp.repeat(gmask, E // G, axis=1) > 0
            tmp = jnp.where(smask, sfc, 0.0)
            _, topk_idx = jax.lax.top_k(tmp, K)
            topk_w = jnp.take_along_axis(scores, topk_idx, axis=1)
            topk_w = topk_w / (topk_w.sum(-1, keepdims=True) + 1e-20)
            return (topk_idx, topk_w * SCALE)
        orig_shape = hidden_states.shape
        x = hidden_states.reshape(-1, H)
        topk_idx, topk_w = _gate(x, gate_w, gate_bias)
        combine_w = (jax.nn.one_hot(topk_idx, E, dtype=x.dtype) * topk_w[..., None]).sum(1)
        g = jnp.einsum('th,eih->tei', x, gate_proj)
        u = jnp.einsum('th,eih->tei', x, up_proj)
        act = jax.nn.silu(g) * u
        y = jnp.einsum('tei,ehi,te->th', act, down_proj, combine_w)
        sg = x @ shared_gate_w.T
        su = x @ shared_up_w.T
        y = y + jax.nn.silu(sg) * su @ shared_down_w.T
        return y.reshape(orig_shape)

    def _L1_attn_ref(x, Wq, Wk, Wv, Wo, decay_logit, out_scale):
        import math
        import jax, jax.numpy as jnp
        import numpy as np
        DIM = 128
        B, T, d = x.shape
        scale = 1.0 / math.sqrt(d)
        q = x @ Wq.T
        k = x @ Wk.T
        v = x @ Wv.T
        scores = jnp.einsum('btd,bsd->bts', q, k) * scale
        decay = jax.nn.sigmoid(decay_logit)
        pos = jnp.arange(T)
        diff = pos[None, :] - pos[:, None]
        mask = (diff > 0).astype(x.dtype)
        expo = jnp.maximum(diff.astype(x.dtype) - 1.0, 0.0)
        weights = decay ** expo * mask
        scores = scores * weights[None, :, :]
        retrieved = jnp.einsum('bts,bsd->btd', scores, v)
        return retrieved @ Wo.T * out_scale

    def _L1_ffn_ref(x, wg, w1, b1, w2, b2):
        import jax, jax.numpy as jnp
        import numpy as np
        B, S, D = (2, 256, 128)
        E, K, H = (8, 2, 512)
        CAP_FACTOR = 1.0

        def _moe_forward(x, wg, w1, b1, w2, b2):
            Bb, Ss, Dd = x.shape
            T = Bb * Ss
            cap = int(K * CAP_FACTOR * ((T + E - 1) // E))
            xt = x.reshape(T, Dd)
            logits = xt @ wg
            scores = jax.nn.softmax(logits, axis=-1)
            gates_k, idx_k = jax.lax.top_k(scores, K)
            gates_k = gates_k / jnp.sum(gates_k, axis=-1, keepdims=True)
            masks = jax.nn.one_hot(idx_k, E, dtype=jnp.int32)
            m = jnp.transpose(masks, (1, 0, 2)).reshape(K * T, E)
            locs_full = jnp.cumsum(m, axis=0) - 1
            loc = jnp.sum(locs_full * m, axis=-1)
            loc = loc.reshape(K, T).T
            valid = (loc < cap).astype(xt.dtype)
            loc_c = jnp.clip(loc, 0, cap - 1)
            contrib = (xt[:, None, :] * valid[:, :, None]).reshape(T * K, Dd)
            disp = jnp.zeros((E, cap, Dd), xt.dtype)
            disp = disp.at[idx_k.reshape(-1), loc_c.reshape(-1)].add(contrib)
            h = jax.nn.relu(jnp.einsum('ecd,edh->ech', disp, w1) + b1[:, None, :])
            out = jnp.einsum('ech,ehd->ecd', h, w2) + b2[:, None, :]
            gathered = out[idx_k, loc_c]
            y = jnp.einsum('tk,tkd->td', gates_k * valid, gathered)
            return y.reshape(Bb, Ss, Dd)
        return _moe_forward(x, wg, w1, b1, w2, b2)
    x = L0_attn_x
    mod = (_silu(L0_c) @ L0_wmod).reshape(L0_c.shape[0], 6, 1, -1)
    sa, ca, ga, sb, cb, gb = (mod[:, 0], mod[:, 1], mod[:, 2], mod[:, 3], mod[:, 4], mod[:, 5])
    ga = (2 * (ga >= 0) - 1) * jnp.maximum(jnp.abs(ga), 0.25)
    gb = (2 * (gb >= 0) - 1) * jnp.maximum(jnp.abs(gb), 0.25)
    h = _layernorm(x, axis=-1) * (1 + ca) + sa
    x = x + ga * _L0_attn_ref(h, L0_attn_Wq, L0_attn_Wk, L0_attn_Wv)
    h = _layernorm(x, axis=-1) * (1 + cb) + sb
    x = x + gb * _L0_ffn_ref(h, L0_ffn_gate_w, L0_ffn_gate_bias, L0_ffn_gate_proj, L0_ffn_up_proj, L0_ffn_down_proj, L0_ffn_shared_gate_w, L0_ffn_shared_up_w, L0_ffn_shared_down_w)
    mod = (_silu(L1_c) @ L1_wmod).reshape(L1_c.shape[0], 6, 1, -1)
    sa, ca, ga, sb, cb, gb = (mod[:, 0], mod[:, 1], mod[:, 2], mod[:, 3], mod[:, 4], mod[:, 5])
    ga = (2 * (ga >= 0) - 1) * jnp.maximum(jnp.abs(ga), 0.25)
    gb = (2 * (gb >= 0) - 1) * jnp.maximum(jnp.abs(gb), 0.25)
    h = _layernorm(x, axis=-1) * (1 + ca) + sa
    x = x + ga * _L1_attn_ref(h, L1_attn_Wq, L1_attn_Wk, L1_attn_Wv, L1_attn_Wo, L1_attn_decay_logit, L1_attn_out_scale)
    h = _layernorm(x, axis=-1) * (1 + cb) + sb
    x = x + gb * _L1_ffn_ref(h, L1_ffn_wg, L1_ffn_w1, L1_ffn_b1, L1_ffn_w2, L1_ffn_b2)
    return x

_drawn_inputs = setup_inputs


def setup_inputs(seed=0):
    import zlib

    import numpy as np

    out = dict(_drawn_inputs(seed))
    spreads = {'L0_ffn_gate_bias': (0.0, 0.8), 'L1_ffn_b1': (0.0, 0.611), 'L1_ffn_b2': (0.0, 0.427)}
    factors = {'L0_ffn_gate_w': 8.0,
     'L0_ffn_gate_proj': 8.0,
     'L0_ffn_up_proj': 8.0,
     'L0_ffn_down_proj': 8.0,
     'L0_ffn_shared_gate_w': 8.0,
     'L0_ffn_shared_up_w': 8.0,
     'L0_ffn_shared_down_w': 8.0,
     'L1_attn_Wq': 8.0,
     'L1_attn_Wk': 8.0,
     'L1_attn_Wv': 8.0,
     'L1_attn_Wo': 8.0}
    for name, (base, spread) in spreads.items():
        noise = np.random.default_rng([zlib.crc32(name.encode()), seed]).standard_normal(out[name].shape)
        drawn = base * np.exp(spread * noise) if base else spread * noise
        out[name] = jnp.asarray(drawn.astype(out[name].dtype))
    for name, factor in factors.items():
        out[name] = (out[name] * factor).astype(out[name].dtype)
    return out
```

```python
from contextlib import ExitStack

import numpy as np
import concourse.bass as bass
from concourse import mybir

F32 = mybir.dt.float32
BF16 = mybir.dt.bfloat16
U32 = mybir.dt.uint32
ALU = mybir.AluOpType
ACT = mybir.ActivationFunctionType
AX = mybir.AxisListType.X

P = 128
BANK = 512
EPS = 1e-5


class Phase:

    def __init__(self, nc, ctx, names):
        self.nc = nc
        handles = [ctx.enter_context(nc.semaphore(n)) for n in names]
        self.by_name = dict(zip(names, handles))
        nums = [h.num for h in handles]
        assert nums == list(range(nums[0], nums[0] + len(nums)))
        self.nums = range(nums[0], nums[-1] + 1)

    def __getitem__(self, name):
        return self.by_name[name]

    def end(self):
        self.nc.all_engine_barrier(sems_to_clear=self.nums)


class Chain:

    def __init__(self, eng, sem):
        self.eng, self.sem, self.n = eng, sem, 0

    def did(self, ins):
        self.n += 1
        ins.then_inc(self.sem, 1)
        return self.n

    def wait(self):
        self.eng.wait_ge(self.sem, self.n)

    def link(self, ins):
        self.did(ins)
        self.wait()


def adaln_program(nc, t, shape):
    B, T = shape["B"], shape["T"]
    NT = T // P
    TILES = B * NT
    HEADS, HD = 16, P // 16
    GROUPS = 4
    GH = HEADS // GROUPS
    QUAD = P // GH
    PARTS = 3
    TERMS = PARTS * PARTS
    KROWS = TERMS * HD
    SROWS = KROWS + PARTS
    HALF = T // 2
    STEPS = 2 * NT
    assert HALF == BANK and GH * QUAD == P

    with ExitStack() as ctx:
        def sb(name, shp, dt=F32, stack=ctx):
            return stack.enter_context(nc.sbuf_tensor(name, shp, dt))

        def phase(*names):
            return Phase(nc, ctx, names)

        ps = ctx.enter_context(nc.psum_tensor("psum", [P, 8, BANK], F32))

        x_all = sb("x_all", [P, TILES, P])
        ident = sb("ident", [P, P])
        silu_cT = sb("silu_cT", [P, 2, B])
        mod_cols = sb("mod_cols", [P, 2, B, 6])
        ga0_rows = sb("ga0_rows", [P, B, P])
        mod1_rows = sb("mod1_rows", [P, B, 6, P])
        cur_cols = sb("cur_cols", [P, 6])
        xb = sb("xb", [P, NT, P])
        xn = sb("xn", [P, NT, P])
        hT = sb("hT", [P, T])
        stats = sb("stats", [P, NT, 6])
        mv = sb("mv", [P, NT, 2])
        ln = sb("ln", [P, 8, NT])

        q_dram = nc.dram_tensor("q_parts", [B, PARTS, P, T], BF16, kind="Internal").ap()
        k_dram = nc.dram_tensor("k_parts", [B, PARTS, P, T], BF16, kind="Internal").ap()
        v_dram = nc.dram_tensor("v_padded", [B, P, NT, HEADS * QUAD], F32, kind="Internal").ap()

        with ExitStack() as own:
            S = phase("m_in", "m_sig", "m_silu", "m_bc", "m_cols", "m_rows", "m_gate", "m_done")
            cT = sb("cT", [P, 2, B], stack=own)
            sig = sb("sig", [P, 2, B], stack=own)
            silu_bc = sb("silu_bc", [P, 2, B, P], stack=own)
            wmod = sb("wmod", [P, 2, 6 * P], stack=own)
            sgn = sb("sgn", [P, B, P], stack=own)
            sgc = sb("sgc", [P, 2, B, 2], stack=own)
            mag = sb("mag", [P, B, P], stack=own)
            magc = sb("magc", [P, 2, B, 2], stack=own)
            with nc.Block() as block:
                @block.sync
                def _(sp):
                    sp.dma_start(x_all[:], t["x"].rearrange("b (n p) d -> p (b n) d", p=P)).then_inc(S["m_in"], 16)
                    sp.dma_start(ident[:], t["ident"]).then_inc(S["m_in"], 16)
                    for i in range(2):
                        sp.dma_start(cT[:, i, :], t[f"cT{i}"]).then_inc(S["m_in"], 16)
                        sp.dma_start(wmod[:, i, :], t[f"wmod{i}"]).then_inc(S["m_in"], 16)

                @block.scalar
                def _(act):
                    act.wait_ge(S["m_in"], 16 * 6)
                    act.activation(sig[:], cT[:], ACT.Sigmoid).then_inc(S["m_sig"], 1)

                @block.vector
                def _(dve):
                    own_steps = Chain(dve, S["m_done"])

                    def keep_from_zero(g, sign, size):
                        own_steps.did(dve.tensor_scalar(sign, g, 0.0, 2.0, ALU.is_ge, ALU.mult))
                        own_steps.link(dve.scalar_tensor_tensor(size, g, -1.0, g, ALU.mult, ALU.max))
                        own_steps.link(dve.tensor_scalar(size, size, 0.25, None, ALU.max))
                        own_steps.link(dve.scalar_tensor_tensor(g, sign, 1.0, size, ALU.subtract, ALU.mult))

                    dve.wait_ge(S["m_sig"], 1)
                    dve.tensor_tensor(silu_cT[:], cT[:], sig[:], ALU.mult).then_inc(S["m_silu"], 1)
                    dve.wait_ge(S["m_silu"], 1)
                    for i in range(2):
                        dve.tensor_copy(silu_bc[:, i], silu_cT[:, i, :].unsqueeze(2).to_broadcast([P, B, P])) \
                            .then_inc(S["m_bc"], 1)
                    dve.wait_ge(S["m_cols"], 1)
                    own_steps.link(dve.tensor_copy(
                        mod_cols[:], ps[:, 0, 0:2 * 6 * B].rearrange("p (i v b) -> p i b v", i=2, v=6)))
                    for v in (1, 4):
                        own_steps.did(dve.tensor_scalar(mod_cols[:, :, :, v], mod_cols[:, :, :, v], 1.0, None, ALU.add))
                    g = mod_cols[:].rearrange("p i b (w v) -> p i b w v", w=2)[:, :, :, :, 2]
                    keep_from_zero(g.rearrange("p i b w -> p (i b w)"), sgc[:].rearrange("p i b w -> p (i b w)"),
                                   magc[:].rearrange("p i b w -> p (i b w)"))
                    dve.wait_ge(S["m_rows"], 1)
                    own_steps.did(dve.tensor_copy(ga0_rows[:], ps[:, 1, :].rearrange("p (b d) -> p b d", b=B)))
                    own_steps.link(dve.tensor_copy(mod1_rows[:].rearrange("p b v d -> p (b v d)"),
                                                   ps[:, 2:8, :].rearrange("p a n -> p (a n)")))
                    for v in (1, 4):
                        own_steps.did(dve.tensor_scalar(mod1_rows[:, :, v, :], mod1_rows[:, :, v, :], 1.0, None, ALU.add))
                    keep_from_zero(ga0_rows[:], sgn[:], mag[:])
                    for v in (2, 5):
                        keep_from_zero(mod1_rows[:, :, v, :], sgn[:], mag[:])

                @block.tensor
                def _(pe):
                    pe.wait_ge(S["m_silu"], 1)
                    for i in range(2):
                        for v in range(6):
                            o = (i * 6 + v) * B
                            last = pe.matmul(ps[:, 0, o:o + B], wmod[:, i, v * P:(v + 1) * P], silu_cT[:, i, :],
                                             start=True, stop=True)
                    last.then_inc(S["m_cols"], 1)
                    pe.wait_ge(S["m_bc"], 2)
                    for b in range(B):
                        pe.matmul(ps[:, 1, b * P:(b + 1) * P], silu_bc[:, 0, b, :], wmod[:, 0, 2 * P:3 * P],
                                  start=True, stop=True)
                    for b in range(B):
                        for v in range(6):
                            q = b * 6 + v
                            last = pe.matmul(ps[:, 2 + q // 4, (q % 4) * P:(q % 4 + 1) * P], silu_bc[:, 1, b, :],
                                             wmod[:, 1, v * P:(v + 1) * P], start=True, stop=True)
                    last.then_inc(S["m_rows"], 1)
            S.end()

        def norm_vector(dve, S, b, layer):
            c = Chain(dve, S["ln_dve"])
            c.did(dve.tensor_copy(cur_cols[:], mod_cols[:, layer, b, :] if isinstance(b, int) else
                                  mod_cols[:, layer].rearrange("p b v -> p (b v)")[:, bass.ds(b * 6, 6)]))
            c.link(dve.tensor_copy(xb[:], x_all[:, bass.ds(b * NT, NT), :]))
            for n in range(NT):
                c.did(dve.bn_stats(stats[:, n, :], xb[:, n, :]))
            c.wait()
            for n in range(NT):
                c.did(dve.bn_aggr(mv[:, n, :], stats[:, n, :]))
            c.wait()
            dve.tensor_scalar(ln[:, 0, :], mv[:, :, 1], EPS, None, ALU.add).then_inc(S["ln_var"], 1)
            dve.wait_ge(S["ln_std"], 1)
            c.link(dve.reciprocal(ln[:, 2, :], ln[:, 1, :]))
            c.link(dve.tensor_tensor(ln[:, 3, :], ln[:, 2, :], ln[:, 2, :], ALU.mult))
            c.link(dve.tensor_tensor(ln[:, 4, :], ln[:, 3, :], ln[:, 0, :], ALU.mult))
            c.link(dve.tensor_scalar(ln[:, 5, :], ln[:, 4, :], -0.5, 1.5, ALU.mult, ALU.add))
            c.link(dve.tensor_tensor(ln[:, 6, :], ln[:, 5, :], ln[:, 2, :], ALU.mult))
            for n in range(NT):
                dve.tensor_scalar(xn[:, n, :], xb[:, n, :], mv[:, n, 0:1], ln[:, 6, n:n + 1],
                                  ALU.subtract, ALU.mult).then_inc(S["ln_xn"], 1)

        def norm_scalar(act, S, shift, scale):
            act.wait_ge(S["ln_var"], 1)
            act.activation(ln[:, 1, :], ln[:, 0, :], ACT.Sqrt).then_inc(S["ln_std"], 1)
            act.wait_ge(S["ln_xT"], NT)
            act.activation(hT[:], ps[:, 0:2, :].rearrange("p a n -> p (a n)"), ACT.Identity,
                           bias=cur_cols[:, shift:shift + 1], scale=cur_cols[:, scale:scale + 1]) \
                .then_inc(S["ln_hT"], 1)

        def norm_tensor(pe, S):
            for n in range(NT):
                pe.wait_ge(S["ln_xn"], n + 1)
                pe.transpose(ps[:, n // 4, (n % 4) * P:(n % 4 + 1) * P], xn[:, n, :], ident[:]) \
                    .then_inc(S["ln_xT"], 1)

        def batch_phase(prefix, *names):
            S = phase(*[f"{prefix}_{n}" for n in LN], *[f"{prefix}_{n}" for n in names])
            S.by_name = {n[len(prefix) + 1:]: h for n, h in S.by_name.items()}
            return S

        LN = ("ln_dve", "ln_var", "ln_std", "ln_xn", "ln_xT", "ln_hT")

        with ExitStack() as own:
            S = phase("p_in", "p_ones")
            wqkv = sb("wqkv", [P, 3, P], stack=own)
            v_pad = sb("v_pad", [P, NT, HEADS, QUAD], stack=own)
            part = [[sb(f"part{w}{i}", [P, T], BF16, stack=own) for i in range(PARTS)] for w in "qk"]
            rest = [sb(f"rest{w}", [P, T], stack=own) for w in "qk"]
            with nc.Block() as block:
                @block.sync
                def _(sp):
                    for i, w in enumerate(("wq0", "wk0", "wv0")):
                        sp.dma_start(wqkv[:, i, :], t[w]).then_inc(S["p_in"], 16)
                    sp.wait_ge(S["p_in"], 16 * 3)

                @block.vector
                def _(dve):
                    dve.memset(v_pad[:], 0.0).then_inc(S["p_ones"], 1)
                    dve.wait_ge(S["p_ones"], 1)
                    dve.memset(v_pad[:, :, :, HD:HD + 1], 1.0).then_inc(S["p_ones"], 1)
            S.end()

            S = batch_phase("qkv", "q", "k", "v", "high0", "high1", "rest0", "rest1", "mid0", "mid1", "low", "vpad",
                            "stored")
            with nc.Fori(0, B) as b:
                with nc.Block() as block:
                    @block.vector
                    def _(dve):
                        norm_vector(dve, S, b, 0)
                        for w in range(2):
                            dve.wait_ge(S[f"high{w}"], 1)
                            dve.tensor_tensor(rest[w][:], ps[:, 2 + 2 * w:4 + 2 * w, :].rearrange("p a n -> p (a n)"),
                                              part[w][0][:], ALU.subtract).then_inc(S[f"rest{w}"], 1)
                        gate = ga0_rows[:, bass.ds(b, 1), :].to_broadcast([P, 4, P])
                        for c in range(2):
                            dve.wait_ge(S["v"], 4 * (c + 1))
                            dve.tensor_tensor(
                                v_pad[:, 4 * c:4 * c + 4, :, 0:HD],
                                ps[:, 6 + c, :].rearrange("p (n h d) -> p n h d", n=4, d=HD),
                                gate.rearrange("p n (h d) -> p n h d", d=HD), ALU.mult).then_inc(S["vpad"], 1)
                        for w in range(2):
                            dve.wait_ge(S[f"mid{w}"], 1)
                            dve.tensor_tensor(part[w][2][:], rest[w][:], part[w][1][:], ALU.subtract) \
                                .then_inc(S["low"], 1)

                    @block.scalar
                    def _(act):
                        norm_scalar(act, S, 0, 1)
                        for w in range(2):
                            act.wait_ge(S["q" if w == 0 else "k"], 1)
                            act.activation(part[w][0][:], ps[:, 2 + 2 * w:4 + 2 * w, :].rearrange("p a n -> p (a n)"),
                                           ACT.Copy).then_inc(S[f"high{w}"], 1)
                        for w in range(2):
                            act.wait_ge(S[f"rest{w}"], 1)
                            act.activation(part[w][1][:], rest[w][:], ACT.Copy).then_inc(S[f"mid{w}"], 1)

                    @block.tensor
                    def _(pe):
                        norm_tensor(pe, S)
                        pe.wait_ge(S["ln_hT"], 1)
                        for w in range(2):
                            for c in range(2):
                                last = pe.matmul(ps[:, 2 + 2 * w + c, :], wqkv[:, w, :], hT[:, c * BANK:(c + 1) * BANK],
                                                 start=True, stop=True)
                            last.then_inc(S["q" if w == 0 else "k"], 1)
                        for n in range(NT):
                            pe.matmul(ps[:, 6 + n // 4, (n % 4) * P:(n % 4 + 1) * P], hT[:, n * P:(n + 1) * P],
                                      wqkv[:, 2, :], start=True, stop=True).then_inc(S["v"], 1)

                    @block.sync
                    def _(sp):
                        for i, (s, n) in enumerate((("high", 1), ("mid", 1))):
                            for w, dram in enumerate((q_dram, k_dram)):
                                sp.wait_ge(S[f"{s}{w}"], n)
                                sp.dma_start(dram[b, i], part[w][i][:]).then_inc(S["stored"], 16)
                        sp.wait_ge(S["vpad"], 2)
                        sp.dma_start(v_dram[b], v_pad[:].rearrange("p n h d -> p n (h d)")).then_inc(S["stored"], 16)
                        for w, dram in enumerate((q_dram, k_dram)):
                            sp.wait_ge(S["low"], w + 1)
                            sp.dma_start(dram[b, 2], part[w][2][:]).then_inc(S["stored"], 16)
                        sp.wait_ge(S["stored"], 16 * 7)
                S.end()

        with ExitStack() as own:
            S = phase("a_load0", "a_load1", "a_load2", "a_load3", "a_scores", "a_exp", "a_maxmm", "a_max",
                      "a_rowT", "a_neg", "a_negrows", "a_pv", "a_oT", "a_turned", "a_free7", "a_dve")
            q_ops = [sb(f"q_ops{g}", [P, GH, T], BF16, stack=own) for g in range(GROUPS)]
            k_ops = [sb(f"k_ops{g}", [P, GH, T], BF16, stack=own) for g in range(GROUPS)]
            v_ops = [sb(f"v_ops{g}", [P, NT, P], stack=own) for g in range(GROUPS)]
            prob = [sb(f"prob{i}", [P, GH, BANK], stack=own) for i in range(2)]
            row_max = [sb(f"row_max{i}", [P, GH * NT], stack=own) for i in range(2)]
            neg = sb("neg", [GH * NT, P], stack=own)
            neg_rest = sb("neg_rest", [GH * NT, P], stack=own)
            neg_part = [sb(f"neg_part{i}", [GH * NT, P], BF16, stack=own) for i in range(PARTS)]
            oT = sb("oT", [P, 2, BANK], stack=own)
            recip = sb("recip", [P, 4, GH], stack=own)
            head_out = sb("head_out", [P, 4, GH * HD], stack=own)

            def load_unit(sp, b, g):
                sem = S[f"a_load{g}"]
                rows = slice(g * GH * HD, (g + 1) * GH * HD)
                for i in range(PARTS):
                    for j in range(PARTS):
                        r = (i * PARTS + j) * HD
                        sp.dma_start(q_ops[g][r:r + HD],
                                     q_dram[b, i, rows, :].rearrange("(h d) t -> d h t", d=HD)).then_inc(sem, 16)
                        sp.dma_start(k_ops[g][r:r + HD],
                                     k_dram[b, j, rows, :].rearrange("(h d) t -> d h t", d=HD)).then_inc(sem, 16)
                sp.dma_start(v_ops[g][:], v_dram[b, :, :, g * P:(g + 1) * P]).then_inc(sem, 16)

            LOADED = 16 * (2 * TERMS + 1)

            ROWS = GH * NT
            PER_STEP = ROWS // STEPS
            AHEAD = 4 * PER_STEP

            def max_scores(pe, g, i, asked):
                h, n = divmod(i, NT)
                if asked >= 2:
                    pe.wait_ge(S["a_max"], asked - 1)
                for c in range(2):
                    last = pe.matmul(ps[:, 2 + 2 * (i % 2) + c, :], q_ops[g][0:KROWS, h, n * P:(n + 1) * P],
                                     k_ops[g][0:KROWS, h, c * BANK:(c + 1) * BANK], start=True, stop=True)
                last.then_inc(S["a_maxmm"], 1)

            def reduce_max(dve, rows, i, asked):
                dve.wait_ge(S["a_maxmm"], asked + 1)
                dve.tensor_reduce(rows[:, i:i + 1], ps[:, 2 + 2 * (i % 2):4 + 2 * (i % 2), :].rearrange("p a n -> p (a n)"),
                                  axis=AX, op=ALU.max).then_inc(S["a_max"], 1)

            def store_neg(sp, g, count):
                sp.wait_ge(S["a_neg"], count)
                for i in range(PARTS):
                    sp.dma_start(q_ops[g][KROWS + i:KROWS + i + 1].rearrange("p h (n q) -> p (h n) q", q=P),
                                 neg_part[i][:]).then_inc(S["a_negrows"], 16)

            def split_neg(dve, ch):
                ch.link(dve.tensor_copy(neg_part[0][:], neg[:]))
                ch.link(dve.tensor_tensor(neg_rest[:], neg[:], neg_part[0][:], ALU.subtract))
                ch.link(dve.tensor_copy(neg_part[1][:], neg_rest[:]))
                dve.tensor_tensor(neg_part[2][:], neg_rest[:], neg_part[1][:], ALU.subtract).then_inc(S["a_neg"], 1)

            with nc.Block() as block:
                @block.vector
                def _(dve):
                    c = Chain(dve, S["a_dve"])
                    for g in range(GROUPS):
                        c.did(dve.memset(k_ops[g][:], 1.0))
                    for i in range(ROWS):
                        reduce_max(dve, row_max[1], i, i)
                    dve.wait_ge(S["a_rowT"], 1)
                    c.link(dve.tensor_scalar(neg[:], ps[0:ROWS, 7, 0:P], -1.0, None, ALU.mult))
                    split_neg(dve, c)
                    for i in range(AHEAD):
                        reduce_max(dve, row_max[0], i, ROWS + i)

                @block.sync
                def _(sp):
                    sp.wait_ge(S["a_dve"], GROUPS)
                    for g in range(GROUPS - 1):
                        load_unit(sp, 0, g)
                    store_neg(sp, 0, 1)
                    sp.wait_ge(S["a_negrows"], 48)
                    for g in range(GROUPS - 1):
                        sp.wait_ge(S[f"a_load{g}"], LOADED)

                @block.tensor
                def _(pe):
                    pe.wait_ge(S["a_load0"], LOADED)
                    for i in range(ROWS):
                        max_scores(pe, 0, i, i)
                    pe.wait_ge(S["a_max"], ROWS)
                    pe.transpose(ps[0:ROWS, 7, 0:P], row_max[1][:], ident[:]).then_inc(S["a_rowT"], 1)
                    pe.wait_ge(S["a_load1"], LOADED)
                    for i in range(AHEAD):
                        max_scores(pe, 1, i, ROWS + i)
            S.end()

            def attention(b, last_batch):
                stop = ROWS * (GROUPS - 1) if last_batch else ROWS * GROUPS + AHEAD
                to_negate = GROUPS - 1 if last_batch else GROUPS
                turns = []
                for k in range(GROUPS * STEPS):
                    g, s = divmod(k, STEPS)
                    if k % NT == 3 and k > NT:
                        turns.append(("out", (k - 3) // NT - 1))
                    if s == STEPS - 4 and g < to_negate:
                        turns.append(("max", g))
                turns.append(("out", 2 * GROUPS - 1))
                order = {u: i for i, u in enumerate(turns)}

                def asked_for(k):
                    for i in range(AHEAD + k * PER_STEP, AHEAD + (k + 1) * PER_STEP):
                        if i < stop:
                            yield i - AHEAD, i // ROWS, i % ROWS

                with nc.Block() as block:
                    @block.tensor
                    def _(pe):
                        def scores(k, h):
                            g, s = divmod(k, STEPS)
                            c, n = divmod(s, NT)
                            if k or h >= 2:
                                pe.wait_ge(S["a_exp"], 4 * k + h - 1)
                            pe.matmul(ps[:, h % 2, :], k_ops[g][0:SROWS, h, n * P:(n + 1) * P],
                                      q_ops[g][0:SROWS, h, c * BANK:(c + 1) * BANK], start=True, stop=True) \
                                .then_inc(S["a_scores"], 1)

                        def values(k):
                            g, s = divmod(k, STEPS)
                            pe.wait_ge(S["a_exp"], 4 * k + 4)
                            if s % NT == 0 and k:
                                pe.wait_ge(S["a_oT"], k // NT)
                            for h in range(GH):
                                last = pe.matmul(ps[h * QUAD:(h + 1) * QUAD, 6, :], v_ops[g][:, s % NT, h * QUAD:(h + 1) * QUAD],
                                                 prob[k % 2][:, h, :], start=(s % NT == 0), stop=(s % NT == NT - 1))
                            last.then_inc(S["a_pv"], 1)

                        def turn_out(m):
                            pe.wait_ge(S["a_oT"], m + 1)
                            if order["out", m]:
                                pe.wait_ge(S["a_free7"], order["out", m])
                            for i in range(4):
                                last = pe.transpose(ps[:, 7, i * P:(i + 1) * P], oT[:, m % 2, i * P:(i + 1) * P], ident[:])
                            last.then_inc(S["a_turned"], 1)

                        for k in range(GROUPS * STEPS):
                            g, s = divmod(k, STEPS)
                            if s == 0 and g:
                                pe.wait_ge(S["a_negrows"], 48 * g)
                            between = list(asked_for(k)) + [None] * PER_STEP
                            for h in range(GH):
                                scores(k, h)
                                if h % 2 == 0 and between[h // 2]:
                                    i, u, row = between[h // 2]
                                    if u == GROUPS - 2 and row == 0:
                                        pe.wait_ge(S["a_load3"], LOADED)
                                    if u >= GROUPS - 1 and row == 0:
                                        pe.wait_ge(S[f"a_load{u - GROUPS + 1}"], LOADED)
                                    max_scores(pe, (u + 1) % GROUPS, row, i)
                            if k:
                                values(k - 1)
                            if k % NT == 3 and k > NT:
                                turn_out((k - 3) // NT - 1)
                            if s == STEPS - 4 and g < to_negate:
                                pe.wait_ge(S["a_max"], ROWS * (g + 1) - AHEAD)
                                if order["max", g]:
                                    pe.wait_ge(S["a_free7"], order["max", g])
                                pe.transpose(ps[0:ROWS, 7, 0:P], row_max[g % 2][:], ident[:]).then_inc(S["a_rowT"], 1)
                        values(GROUPS * STEPS - 1)
                        turn_out(2 * GROUPS - 1)

                    @block.scalar
                    def _(act):
                        def copy_out(m):
                            act.wait_ge(S["a_pv"], (m + 1) * NT)
                            if m >= 2:
                                act.wait_ge(S["a_turned"], m - 1)
                            act.activation(oT[:, m % 2, :], ps[:, 6, :], ACT.Copy).then_inc(S["a_oT"], 1)

                        for k in range(GROUPS * STEPS):
                            if k >= 2:
                                act.wait_ge(S["a_pv"], k - 1)
                            for h in range(GH):
                                act.wait_ge(S["a_scores"], 4 * k + h + 1)
                                act.activation(prob[k % 2][:, h, :], ps[:, h % 2, :], ACT.Exp).then_inc(S["a_exp"], 1)
                            if k and k % NT == 0:
                                copy_out(k // NT - 1)
                        copy_out(2 * GROUPS - 1)

                    @block.vector
                    def _(dve):
                        ch = Chain(dve, S["a_dve"])

                        def add_out(m):
                            g, c = divmod(m, 2)
                            turned = ps[:, 7, :].rearrange("p (n h d) -> p n h d", n=4, h=GH)
                            dve.wait_ge(S["a_turned"], m + 1)
                            ch.link(dve.reciprocal(recip[:], turned[:, :, :, HD]))
                            dve.tensor_tensor(
                                head_out[:].rearrange("p n (h d) -> p (n h) d", d=HD),
                                ps[:, 7, :].rearrange("p (a d) -> p a d", d=QUAD)[:, :, 0:HD],
                                recip[:].rearrange("p n h -> p (n h)").unsqueeze(2).to_broadcast([P, 4 * GH, HD]),
                                ALU.mult).then_inc(S["a_free7"], 1)
                            dve.wait_ge(S["a_free7"], order["out", m] + 1)
                            dst = x_all[:, bass.ds(b * NT + 4 * c, 4), g * GH * HD:(g + 1) * GH * HD]
                            ch.link(dve.tensor_tensor(dst, dst, head_out[:], ALU.add))

                        for k in range(GROUPS * STEPS):
                            g, s = divmod(k, STEPS)
                            for i, u, row in asked_for(k):
                                reduce_max(dve, row_max[u % 2], row, i)
                            if s == STEPS - 3 and g < to_negate:
                                dve.wait_ge(S["a_rowT"], g + 1)
                                if g:
                                    dve.wait_ge(S["a_negrows"], 48 * g)
                                dve.tensor_scalar(neg[:], ps[0:ROWS, 7, 0:P], -1.0, None, ALU.mult) \
                                    .then_inc(S["a_free7"], 1)
                                dve.wait_ge(S["a_free7"], order["max", g] + 1)
                                split_neg(dve, ch)
                            if k % NT == 4 and k > NT:
                                add_out((k - 4) // NT - 1)
                        add_out(2 * GROUPS - 1)

                    @block.sync
                    def _(sp):
                        load_unit(sp, b, GROUPS - 1)
                        for g in range(GROUPS):
                            if g < to_negate:
                                store_neg(sp, (g + 1) % GROUPS, g + 1)
                            if not last_batch and g < GROUPS - 1:
                                sp.wait_ge(S["a_pv"], STEPS * (g + 1))
                                load_unit(sp, b + 1, g)
                        sp.wait_ge(S["a_negrows"], 48 * to_negate)
                        for g in range(GROUPS):
                            if g == GROUPS - 1 or not last_batch:
                                sp.wait_ge(S[f"a_load{g}"], LOADED)
                S.end()

            with nc.Fori(0, B - 1) as b:
                attention(b, False)
            attention(B - 1, True)

        E0, I = shape["E0"], shape["I"]
        FEATS = E0 * I
        ALL = t["gate0"].shape[1]
        ROUTED = FEATS // P
        FT = -(-ALL // P)
        rows_of = [min(P, ALL - j * P) for j in range(FT)]
        EG = 4
        NG = E0 // EG
        TOP_GROUPS, TOP = 2, 4
        assert FEATS % P == 0
        with ExitStack() as own:
            gate_w = sb("gate_w", [P, ALL], stack=own)
            up_w = sb("up_w", [P, ALL], stack=own)
            down_w = sb("down_w", [P, FT, P], stack=own)
            router = sb("router0", [P, E0], stack=own)
            bias = sb("bias0", [P, E0], stack=own)
            below = sb("below", [P, E0, E0], stack=own)
            owner = sb("owner", [3 * 32, FEATS], BF16, stack=own)
            scores = sb("scores", [P, NT, E0], stack=own)
            biased = sb("biased", [P, NT, E0], stack=own)
            pair_max = sb("pair_max", [P, NT * NG, 2], stack=own)
            pair_sum = sb("pair_sum", [P, NT * NG, 2], stack=own)
            top_a = sb("top_a", [P, NT * NG], stack=own)
            top_b = sb("top_b", [P, NT * NG], stack=own)
            group_score = sb("group_score", [P, NT, NG], stack=own)
            ahead = sb("ahead", [P, NT, E0, E0], stack=own)
            tied = sb("tied", [P, NT, E0, E0], stack=own)
            rank = sb("rank", [P, NT, E0], stack=own)
            chosen = sb("chosen", [P, NT, E0], stack=own)
            masked = sb("masked", [P, NT, E0], stack=own)
            total = sb("total", [P, NT], stack=own)
            inverse = sb("inverse", [P, NT], stack=own)
            combine = sb("combine", [P, NT, E0], stack=own)
            c_rest = sb("c_rest", [E0, T], stack=own)
            c_mid = sb("c_mid", [E0, T], BF16, stack=own)
            c_parts = sb("c_parts", [3 * 32, T], BF16, stack=own)
            gated = [sb(f"gated{i}", [P, BANK], stack=own) for i in range(2)]
            prod = [sb(f"prod{i}", [P, BANK], stack=own) for i in range(2)]
            acts = [sb(f"acts{i}", [P, BANK], stack=own) for i in range(3)]
            yT = sb("yT", [P, 2, BANK], stack=own)

            S = phase("f_w", "f_own", "f_cast")
            with nc.Block() as block:
                with ExitStack() as inner:
                    owner32 = sb("owner32", [3 * 32, FEATS], stack=inner)

                    @block.sync
                    def _(sp):
                        sp.dma_start(owner32[:], t["owner"]).then_inc(S["f_own"], 16)
                        for dst, n in ((router, "router0"), (bias, "bias0"), (below, "below"), (gate_w, "gate0"), (up_w, "up0")):
                            sp.dma_start(dst[:], t[n]).then_inc(S["f_w"], 16)
                        full = ALL // P
                        sp.dma_start(down_w[:, 0:full, :], t["down0"][0:full * P].rearrange("(j p) d -> p j d", p=P)) \
                            .then_inc(S["f_w"], 16)
                        if full < FT:
                            sp.dma_start(down_w[0:rows_of[-1], full, :], t["down0"][full * P:ALL]).then_inc(S["f_w"], 16)
                        sp.wait_ge(S["f_w"], 16 * (6 + (full < FT)))

                    @block.vector
                    def _(dve):
                        dve.memset(c_parts[:], 0.0).then_inc(S["f_cast"], 1)
                        dve.wait_ge(S["f_own"], 16)
                        dve.tensor_copy(owner[:], owner32[:]).then_inc(S["f_cast"], 1)
            S.end()

            S = batch_phase("ffn", "logits", "scores", "combine", "cT", "cparts", "dve", "gate", "up", "silu", "prod",
                            "act", "down", "yT", "turned", "added")
            TILES_ALL = 2 * FT
            with nc.Fori(0, B) as b:
                with nc.Block() as block:
                    @block.tensor
                    def _(pe):
                        norm_tensor(pe, S)
                        pe.wait_ge(S["ln_hT"], 1)
                        for n in range(NT):
                            last = pe.matmul(ps[:, 2, n * E0:(n + 1) * E0], hT[:, n * P:(n + 1) * P], router[:],
                                             start=True, stop=True)
                        last.then_inc(S["logits"], 1)

                        def gate_up(i):
                            c, j = divmod(i, FT)
                            m = rows_of[j]
                            tokens = slice(c * BANK, (c + 1) * BANK)
                            if i >= 2:
                                pe.wait_ge(S["silu"], i - 1)
                            pe.matmul(ps[0:m, i % 2, :], gate_w[:, j * P:j * P + m], hT[:, tokens], start=True, stop=True) \
                                .then_inc(S["gate"], 1)
                            if i >= 2:
                                pe.wait_ge(S["act"], i - 1)
                            last = pe.matmul(ps[0:m, 2 + i % 2, :], up_w[:, j * P:j * P + m], hT[:, tokens],
                                             start=True, stop=True)
                            if j < ROUTED:
                                if i < 2:
                                    pe.wait_ge(S["cparts"], 2)
                                last = pe.matmul(ps[:, 4 + i % 2, :], owner[:, j * P:(j + 1) * P], c_parts[:, tokens],
                                                 start=True, stop=True)
                            last.then_inc(S["up"], 1)

                        def down(i):
                            c, j = divmod(i, FT)
                            m = rows_of[j]
                            pe.wait_ge(S["act"], i + 1)
                            if j == 0 and c:
                                pe.wait_ge(S["yT"], c)
                            pe.matmul(ps[:, 6, :], down_w[0:m, j, :], acts[i % 3][0:m, :], start=(j == 0), stop=(j == FT - 1)) \
                                .then_inc(S["down"], 1)

                        def turn(c):
                            pe.wait_ge(S["yT"], c + 1)
                            if c:
                                pe.wait_ge(S["added"], c)
                            for n in range(4):
                                last = pe.transpose(ps[:, 7, n * P:(n + 1) * P], yT[:, c, n * P:(n + 1) * P], ident[:])
                            last.then_inc(S["turned"], 1)

                        pe.wait_ge(S["combine"], 1)
                        for n in range(NT):
                            last = pe.transpose(ps[0:E0, 6 + n // 4, (n % 4) * P:(n % 4 + 1) * P], combine[:, n, :], ident[:])
                        last.then_inc(S["cT"], 1)
                        for i in range(TILES_ALL + 2):
                            if i < TILES_ALL:
                                gate_up(i)
                            if i >= 2:
                                down(i - 2)
                            if i == FT + 4:
                                turn(0)
                        turn(1)

                    @block.scalar
                    def _(act):
                        norm_scalar(act, S, 3, 4)
                        act.wait_ge(S["logits"], 1)
                        act.activation(scores[:].rearrange("p n e -> p (n e)"), ps[:, 2, 0:NT * E0], ACT.Sigmoid) \
                            .then_inc(S["scores"], 1)

                        def copy_y(c):
                            act.wait_ge(S["down"], FT * (c + 1))
                            act.activation(yT[:, c, :], ps[:, 6, :], ACT.Copy, scale=cur_cols[:, 5:6]).then_inc(S["yT"], 1)

                        for i in range(TILES_ALL):
                            m = rows_of[i % FT]
                            act.wait_ge(S["gate"], i + 1)
                            if i >= 2:
                                act.wait_ge(S["act"], i - 1)
                            act.activation(gated[i % 2][0:m, :], ps[0:m, i % 2, :], ACT.Silu).then_inc(S["silu"], 1)
                            if i == FT + 1:
                                copy_y(0)
                        copy_y(1)

                    @block.vector
                    def _(dve):
                        norm_vector(dve, S, b, 0)
                        ch = Chain(dve, S["dve"])
                        tt, link = dve.tensor_tensor, ch.link

                        def rank_of(out, v, count):
                            a, q = ahead[:, :, 0:count, 0:count], tied[:, :, 0:count, 0:count]
                            other = v.unsqueeze(2).to_broadcast([P, NT, count, count])
                            mine = v.unsqueeze(3).to_broadcast([P, NT, count, count])
                            ch.did(tt(a, other, mine, ALU.is_gt))
                            link(tt(q, other, mine, ALU.is_equal))
                            link(tt(q, q, below[:, 0:count, 0:count].unsqueeze(1).to_broadcast([P, NT, count, count]), ALU.mult))
                            link(tt(a, a, q, ALU.add))
                            link(dve.tensor_reduce(out, a, axis=AX, op=ALU.add))

                        dve.wait_ge(S["scores"], 1)
                        link(tt(biased[:], scores[:], bias[:].unsqueeze(1).to_broadcast([P, NT, E0]), ALU.add))
                        v = biased[:].rearrange("p n (g w v) -> p (n g) w v", g=NG, v=2)
                        ch.did(tt(pair_max[:], v[:, :, :, 0], v[:, :, :, 1], ALU.max))
                        link(tt(pair_sum[:], v[:, :, :, 0], v[:, :, :, 1], ALU.add))
                        ch.did(tt(top_a[:], pair_max[:, :, 0], pair_max[:, :, 1], ALU.add))
                        link(tt(top_b[:], pair_sum[:, :, 0], pair_sum[:, :, 1], ALU.max))
                        link(tt(group_score[:].rearrange("p n g -> p (n g)"), top_a[:], top_b[:], ALU.max))
                        rank_of(rank[:, :, 0:NG], group_score[:], NG)
                        link(dve.tensor_scalar(chosen[:, :, 0:NG], rank[:, :, 0:NG], float(TOP_GROUPS), None, ALU.is_lt))
                        link(tt(masked[:].rearrange("p n (g w) -> p n g w", g=NG), biased[:].rearrange("p n (g w) -> p n g w", g=NG),
                                chosen[:, :, 0:NG].unsqueeze(3).to_broadcast([P, NT, NG, EG]), ALU.mult))
                        rank_of(rank[:], masked[:], E0)
                        link(dve.tensor_scalar(chosen[:], rank[:], float(TOP), None, ALU.is_lt))
                        link(tt(masked[:], scores[:], chosen[:], ALU.mult))
                        link(dve.tensor_reduce(total[:], masked[:], axis=AX, op=ALU.add))
                        link(dve.tensor_scalar(total[:], total[:], 1e-20, None, ALU.add))
                        link(dve.reciprocal(inverse[:], total[:]))
                        tt(combine[:], masked[:], inverse[:].unsqueeze(2).to_broadcast([P, NT, E0]), ALU.mult) \
                            .then_inc(S["combine"], 1)
                        dve.wait_ge(S["cT"], 1)
                        cT_ps = ps[0:E0, 6:8, :].rearrange("p a n -> p (a n)")
                        link(dve.tensor_copy(c_parts[0:E0, :], cT_ps))
                        link(tt(c_rest[:], cT_ps, c_parts[0:E0, :], ALU.subtract))
                        link(dve.tensor_copy(c_mid[:], c_rest[:]))
                        dve.tensor_copy(c_parts[32:32 + E0, :], c_mid[:]).then_inc(S["cparts"], 1)
                        tt(c_parts[64:64 + E0, :], c_rest[:], c_mid[:], ALU.subtract).then_inc(S["cparts"], 1)

                        def add_y(c):
                            dve.wait_ge(S["turned"], c + 1)
                            dst = x_all[:, bass.ds(b * NT + 4 * c, 4), :]
                            tt(dst, dst, ps[:, 7, :].rearrange("p (n d) -> p n d", d=P), ALU.add).then_inc(S["added"], 1)

                        routed = 0
                        for i in range(TILES_ALL):
                            j = i % FT
                            m = rows_of[j]
                            dve.wait_ge(S["silu"], i + 1)
                            dve.wait_ge(S["up"], i + 1)
                            if i >= 3:
                                dve.wait_ge(S["down"], i - 2)
                            if j < ROUTED:
                                tt(prod[i % 2][:], gated[i % 2][:], ps[:, 2 + i % 2, :], ALU.mult).then_inc(S["prod"], 1)
                                routed += 1
                                dve.wait_ge(S["prod"], routed)
                                tt(acts[i % 3][:], prod[i % 2][:], ps[:, 4 + i % 2, :], ALU.mult).then_inc(S["act"], 1)
                            else:
                                tt(acts[i % 3][0:m, :], gated[i % 2][0:m, :], ps[0:m, 2 + i % 2, :], ALU.mult) \
                                    .then_inc(S["act"], 1)
                            if i == FT + 5:
                                add_y(0)
                        add_y(1)
                S.end()

        with ExitStack() as own:
            w1q = sb("w1q", [P, 4, P], stack=own)
            qk_w = sb("qk_w", [P, P], stack=own)
            vo_w = sb("vo_w", [P, P], stack=own)
            decay = sb("decay", [P, 8], stack=own)
            out_scale = sb("out_scale", [P, 1], stack=own)
            distance = sb("distance", [P, P], stack=own)
            later = sb("later", [P, P], stack=own)
            to_end = sb("to_end", [P, P], stack=own)
            from_start = sb("from_start", [P, 1], stack=own)
            powers = sb("powers", [P, P], stack=own)
            mask = sb("mask", [P, P], stack=own)
            end_powers = sb("end_powers", [P, P], stack=own)
            start_powers = sb("start_powers", [P, 1], stack=own)
            chunk_power = sb("chunk_power", [P, 1], stack=own)
            qT = sb("qT", [P, T], stack=own)
            qT_end = sb("qT_end", [P, T], stack=own)
            h_start = sb("h_start", [P, NT, P], stack=own)
            gate_row = sb("gate_row", [P, P], stack=own)
            vals = sb("vals", [P, NT, P], stack=own)
            near = sb("near", [P, NT, P], stack=own)
            state = sb("state", [P, NT, P], stack=own)
            shift_row = sb("shift_row", [P, P], stack=own)

            S = phase("l_in", "l_dve", "l_act", "l_pe", "l_copied")
            with nc.Block() as block:
                @block.sync
                def _(sp):
                    for i, n in enumerate(("wq1", "wk1", "wv1", "wo1")):
                        sp.dma_start(w1q[:, i, :], t[n]).then_inc(S["l_in"], 16)
                    for dst, n in ((decay[:, 0:1], "decay"), (out_scale[:], "out_scale"), (distance[:], "distance"),
                                   (later[:], "later"), (to_end[:], "to_end"), (from_start[:], "from_start")):
                        sp.dma_start(dst, t[n]).then_inc(S["l_in"], 16)
                    sp.wait_ge(S["l_in"], 160)

                @block.tensor
                def _(pe):
                    pe.wait_ge(S["l_in"], 160)
                    pe.matmul(ps[:, 0, 0:P], w1q[:, 0, :], w1q[:, 1, :], start=True, stop=True)
                    pe.matmul(ps[:, 1, 0:P], w1q[:, 2, :], w1q[:, 3, :], start=True, stop=True).then_inc(S["l_pe"], 1)

                @block.vector
                def _(dve):
                    dve.wait_ge(S["l_in"], 160)
                    ch = Chain(dve, S["l_dve"])
                    ch.link(dve.scalar_tensor_tensor(decay[:, 1:2], decay[:, 0:1], -1.0, decay[:, 0:1], ALU.mult, ALU.min))
                    dve.wait_ge(S["l_act"], 2)
                    ch.link(dve.scalar_tensor_tensor(decay[:, 4:5], decay[:, 0:1], 0.0, decay[:, 3:4], ALU.min, ALU.subtract))
                    dve.wait_ge(S["l_act"], 6)
                    ch.did(dve.tensor_tensor(mask[:], powers[:], later[:], ALU.mult))
                    ch.did(dve.tensor_scalar(end_powers[:], end_powers[:], float(np.float32(P) ** -0.5), None, ALU.mult))
                    dve.wait_ge(S["l_pe"], 1)
                    ch.did(dve.tensor_copy(qk_w[:], ps[:, 0, 0:P]))
                    ch.did(dve.tensor_copy(vo_w[:], ps[:, 1, 0:P]))

                @block.scalar
                def _(act):
                    ch = Chain(act, S["l_act"])
                    act.wait_ge(S["l_dve"], 1)
                    ch.link(act.activation(decay[:, 2:3], decay[:, 1:2], ACT.Exp))
                    ch.link(act.activation(decay[:, 3:4], decay[:, 2:3], ACT.Ln, bias=1.0))
                    act.wait_ge(S["l_dve"], 2)
                    log = decay[:, 4:5]
                    ch.did(act.activation(powers[:], distance[:], ACT.Exp, scale=log))
                    ch.did(act.activation(end_powers[:], to_end[:], ACT.Exp, scale=log))
                    ch.did(act.activation(start_powers[:], from_start[:], ACT.Exp, scale=log))
                    ch.did(act.activation(chunk_power[:], log, ACT.Exp, scale=float(P)))
            S.end()

            S = batch_phase("lin", "qT", "qT_sb", "dve", "vals", "vals_sb", "near", "near_sb", "pairs", "states", "y")
            with nc.Fori(0, B) as b:
                with nc.Block() as block:
                    @block.tensor
                    def _(pe):
                        norm_tensor(pe, S)
                        pe.wait_ge(S["ln_hT"], 1)
                        for c in range(2):
                            last = pe.matmul(ps[:, 2 + c, :], qk_w[:], hT[:, c * BANK:(c + 1) * BANK], start=True, stop=True)
                        last.then_inc(S["qT"], 1)
                        for n in range(NT):
                            last = pe.matmul(ps[:, 6 + n // 4, (n % 4) * P:(n % 4 + 1) * P], hT[:, n * P:(n + 1) * P], vo_w[:],
                                             start=True, stop=True)
                        last.then_inc(S["vals"], 1)
                        pe.wait_ge(S["qT_sb"], 1)
                        for n in range(NT):
                            cols = slice(n * P, (n + 1) * P)
                            last = pe.matmul(ps[:, 4 + n // 4, (n % 4) * P:(n % 4 + 1) * P], hT[:, cols], qT[:, cols],
                                             start=True, stop=True)
                        last.then_inc(S["near"], 1)
                        pe.wait_ge(S["vals_sb"], 1)
                        for n in range(NT):
                            last = pe.matmul(ps[:, n // 4, (n % 4) * P:(n % 4 + 1) * P], h_start[:, n, :], vals[:, n, :],
                                             start=True, stop=True)
                        last.then_inc(S["pairs"], 1)
                        pe.wait_ge(S["near_sb"], 1)
                        pe.wait_ge(S["states"], 1)
                        for n in range(NT):
                            out = ps[:, 2 + n // 4, (n % 4) * P:(n % 4 + 1) * P]
                            last = pe.matmul(out, near[:, n, :], vals[:, n, :], start=True, stop=(n == NT - 1))
                            if n < NT - 1:
                                last = pe.matmul(out, qT_end[:, n * P:(n + 1) * P], state[:, n, :], start=False, stop=True)
                        last.then_inc(S["y"], 1)

                    @block.scalar
                    def _(act):
                        norm_scalar(act, S, 0, 1)
                        act.wait_ge(S["qT"], 1)
                        act.activation(qT[:], ps[:, 2:4, :].rearrange("p a n -> p (a n)"), ACT.Copy).then_inc(S["qT_sb"], 1)

                    @block.vector
                    def _(dve):
                        norm_vector(dve, S, b, 1)
                        ch = Chain(dve, S["dve"])
                        tt, link = dve.tensor_tensor, ch.link
                        row = lambda v: mod1_rows[:].rearrange("p b v d -> p (b v) d")[:, bass.ds(b * 6 + v, 1), :]
                        all_tiles = lambda ap: ap.to_broadcast([P, NT, P])
                        dve.wait_ge(S["ln_xn"], NT)
                        ch.did(dve.tensor_scalar(gate_row[:].unsqueeze(1), row(2), out_scale[:], None, ALU.mult))
                        ch.did(dve.tensor_scalar(shift_row[:].unsqueeze(1), row(0), start_powers[:], None, ALU.mult))
                        link(dve.scalar_tensor_tensor(h_start[:], xn[:], start_powers[:], all_tiles(row(1)), ALU.mult, ALU.mult))
                        link(tt(h_start[:], h_start[:], all_tiles(shift_row[:].unsqueeze(1)), ALU.add))
                        dve.wait_ge(S["vals"], 1)
                        tt(vals[:], ps[:, 6:8, :].rearrange("p a (n d) -> p (a n) d", d=P), all_tiles(gate_row[:].unsqueeze(1)),
                           ALU.mult).then_inc(S["vals_sb"], 1)
                        dve.wait_ge(S["qT_sb"], 1)
                        link(tt(qT_end[:].rearrange("p (n q) -> p n q", q=P), qT[:].rearrange("p (n q) -> p n q", q=P),
                                all_tiles(end_powers[:].unsqueeze(1)), ALU.mult))
                        dve.wait_ge(S["near"], 1)
                        tt(near[:], ps[:, 4:6, :].rearrange("p a (n d) -> p (a n) d", d=P), all_tiles(mask[:].unsqueeze(1)),
                           ALU.mult).then_inc(S["near_sb"], 1)
                        dve.wait_ge(S["pairs"], 1)
                        pair = lambda n: ps[:, n // 4, (n % 4) * P:(n % 4 + 1) * P]
                        link(dve.tensor_copy(state[:, NT - 2, :], pair(NT - 1)))
                        for n in range(NT - 2, 0, -1):
                            ins = dve.scalar_tensor_tensor(state[:, n - 1, :], state[:, n, :], chunk_power[:], pair(n),
                                                           ALU.mult, ALU.add)
                            if n > 1:
                                link(ins)
                        ins.then_inc(S["states"], 1)
                        dve.wait_ge(S["y"], 1)
                        dst = x_all[:, bass.ds(b * NT, NT), :]
                        link(tt(dst, dst, ps[:, 2:4, :].rearrange("p a (n d) -> p (a n) d", d=P), ALU.add))
                S.end()

        E1, HID = shape["E1"], shape["HID"]
        HT = HID // P
        K = 2
        TOKENS = B * T
        ROOM = K * (-(-TOKENS // E1))
        SLOTS = E1 * ROOM
        ST = ROOM // P
        CHOICES = K * TILES
        assert ROOM == T and CHOICES * E1 == BANK
        slots_dram = nc.dram_tensor("slots", [SLOTS + K * TOKENS, P], F32, kind="Internal").ap()
        outs_dram = nc.dram_tensor("slot_outs", [SLOTS, P], F32, kind="Internal").ap()
        with ExitStack() as own:
            gates = sb("gates", [P, K, TILES], stack=own)
            from_slot = sb("from_slot", [P, CHOICES], U32, stack=own)

            with ExitStack() as inner:
                router1 = sb("router1", [P, E1], stack=inner)
                h_rows = sb("h_rows", [P, TILES, P], stack=inner)
                logit = sb("logit", [P, TILES, E1], stack=inner)
                zeros = sb("zeros", [P, ST, P], stack=inner)
                before32 = sb("before32", [P, P], stack=inner)
                before = sb("before", [P, P], BF16, stack=inner)
                ones = sb("ones", [P, P], BF16, stack=inner)
                expert_id = sb("expert_id", [P, E1], stack=inner)
                spill = sb("spill", [P, CHOICES], stack=inner)
                priority = sb("priority", [P, E1], stack=inner)
                scan_ones = sb("scan_ones", [P, CHOICES], stack=inner)
                S = phase("r_in", "r_zeroed", "r_dve", "r_first")
                with nc.Block() as block:
                    @block.sync
                    def _(sp):
                        for dst, n in ((router1, "router1"), (before32, "before"), (expert_id, "expert_id"), (spill, "spill")):
                            sp.dma_start(dst[:], t[n]).then_inc(S["r_in"], 16)
                        sp.wait_ge(S["r_first"], 1)
                        for e in range(E1):
                            sp.dma_start(slots_dram[e * ROOM:(e + 1) * ROOM].rearrange("(n p) d -> p n d", p=P), zeros[:]) \
                                .then_inc(S["r_zeroed"], 16)
                        sp.wait_ge(S["r_in"], 64)
                        sp.wait_ge(S["r_zeroed"], 16 * E1)

                    @block.vector
                    def _(dve):
                        dve.memset(zeros[:], 0.0).then_inc(S["r_first"], 1)
                        dve.memset(ones[:], 1.0).then_inc(S["r_dve"], 1)
                        dve.memset(scan_ones[:], 1.0).then_inc(S["r_dve"], 1)
                        dve.wait_ge(S["r_in"], 64)
                        dve.tensor_copy(before[:], before32[:]).then_inc(S["r_dve"], 1)
                        dve.tensor_scalar(priority[:], expert_id[:], -1.0, float(E1), ALU.mult, ALU.add).then_inc(S["r_dve"], 1)
                S.end()

                S = batch_phase("rt", "logits", "dve")
                with nc.Fori(0, B) as b:
                    with nc.Block() as block:
                        @block.tensor
                        def _(pe):
                            norm_tensor(pe, S)
                            pe.wait_ge(S["ln_hT"], 1)
                            for n in range(NT):
                                last = pe.matmul(ps[:, 2, n * E1:(n + 1) * E1], hT[:, n * P:(n + 1) * P], router1[:],
                                                 start=True, stop=True)
                            last.then_inc(S["logits"], 1)

                        @block.scalar
                        def _(act):
                            norm_scalar(act, S, 3, 4)

                        @block.vector
                        def _(dve):
                            norm_vector(dve, S, b, 1)
                            ch = Chain(dve, S["dve"])
                            row = lambda v: mod1_rows[:].rearrange("p b v d -> p (b v) d")[:, bass.ds(b * 6 + v, 1), :]
                            rows = h_rows[:, bass.ds(b * NT, NT), :]
                            dve.wait_ge(S["ln_xn"], NT)
                            ch.link(dve.tensor_tensor(rows, xn[:], row(4).to_broadcast([P, NT, P]), ALU.mult))
                            ch.link(dve.tensor_tensor(rows, rows, row(3).to_broadcast([P, NT, P]), ALU.add))
                            dve.wait_ge(S["logits"], 1)
                            ch.did(dve.tensor_copy(logit[:, bass.ds(b * NT, NT), :],
                                                   ps[:, 2, 0:NT * E1].rearrange("p (n e) -> p n e", e=E1)))
                    S.end()

                with ExitStack() as rt:
                    def small(name, *shp, dt=F32):
                        return sb(name, [P, *shp], dt, stack=rt)

                    best = small("best", K, TILES)
                    match = small("match", TILES, E1)
                    first = small("first", TILES)
                    choice = small("choice", K, TILES, E1)
                    choice_bf = small("choice_bf", K, TILES, E1, dt=BF16)
                    others = small("others", TILES, E1)
                    ratio = small("ratio", TILES)
                    through = small("through", CHOICES, E1)
                    place = small("place", CHOICES, E1)
                    loc = small("loc", CHOICES)
                    expert = small("expert", CHOICES)
                    valid = small("valid", CHOICES)
                    target = small("target", CHOICES)
                    clipped = small("clipped", CHOICES)
                    to_slot = small("to_slot", CHOICES, dt=U32)
                    S = phase("t_dve", "t_ratio", "t_exp", "t_choice", "t_pos", "t_to", "t_sent")
                    with nc.Block() as block:
                        @block.vector
                        def _(dve):
                            ch = Chain(dve, S["t_dve"])
                            tt, link = dve.tensor_tensor, ch.link
                            per_expert = lambda ap: ap.unsqueeze(2).to_broadcast([P, TILES, E1])
                            for k in range(K):
                                source = logit if k == 0 else others
                                link(dve.tensor_reduce(best[:, k, :], source[:], axis=AX, op=ALU.max))
                                link(tt(match[:], source[:], per_expert(best[:, k, :]), ALU.is_equal))
                                link(tt(match[:], match[:], priority[:].unsqueeze(1).to_broadcast([P, TILES, E1]), ALU.mult))
                                link(dve.tensor_reduce(first[:], match[:], axis=AX, op=ALU.max))
                                link(tt(choice[:, k], match[:], per_expert(first[:]), ALU.is_equal))
                                if k == 0:
                                    link(dve.scalar_tensor_tensor(others[:].rearrange("p n e -> p (n e)"),
                                                                  choice[:, 0].rearrange("p n e -> p (n e)"), -1e30,
                                                                  logit[:].rearrange("p n e -> p (n e)"), ALU.mult, ALU.add))
                            dve.tensor_copy(choice_bf[:], choice[:]).then_inc(S["t_choice"], 1)
                            tt(ratio[:], best[:, 1, :], best[:, 0, :], ALU.subtract).then_inc(S["t_ratio"], 1)
                            dve.wait_ge(S["t_pos"], 1)
                            flat = choice[:].rearrange("p k n e -> p (k n) e")
                            totals = ps[:, 1, :].rearrange("p (n e) -> p n e", e=E1)
                            for e in range(E1):
                                ch.did(dve.tensor_tensor_scan(through[:, :, e], scan_ones[:], totals[:, :, e], 0.0,
                                                              ALU.mult, ALU.add))
                            ch.wait()
                            link(tt(place[:], through[:], totals, ALU.subtract))
                            link(tt(place[:], place[:], ps[:, 0, :].rearrange("p (n e) -> p n e", e=E1), ALU.add))
                            link(tt(place[:], place[:], flat, ALU.mult))
                            link(dve.tensor_reduce(loc[:], place[:], axis=AX, op=ALU.add))
                            link(tt(place[:], flat, expert_id[:].unsqueeze(1).to_broadcast([P, CHOICES, E1]), ALU.mult))
                            link(dve.tensor_reduce(expert[:], place[:], axis=AX, op=ALU.add))
                            link(dve.tensor_scalar(valid[:], loc[:], float(ROOM), None, ALU.is_lt))
                            link(dve.tensor_scalar(clipped[:], loc[:], float(ROOM - 1), None, ALU.min))
                            link(dve.scalar_tensor_tensor(clipped[:], expert[:], float(ROOM), clipped[:], ALU.mult, ALU.add))
                            ch.did(dve.tensor_copy(from_slot[:], clipped[:]))
                            link(dve.tensor_scalar(target[:], spill[:], float(SLOTS), None, ALU.add))
                            link(tt(clipped[:], clipped[:], target[:], ALU.subtract))
                            link(tt(clipped[:], clipped[:], valid[:], ALU.mult))
                            link(tt(clipped[:], clipped[:], target[:], ALU.add))
                            dve.tensor_copy(to_slot[:], clipped[:]).then_inc(S["t_to"], 1)
                            dve.wait_ge(S["t_exp"], 1)
                            link(dve.tensor_scalar(first[:], ratio[:], 1.0, None, ALU.add))
                            link(dve.reciprocal(gates[:, 0, :], first[:]))
                            link(tt(gates[:, 1, :], gates[:, 0, :], ratio[:], ALU.mult))
                            link(tt(gates[:].rearrange("p k n -> p (k n)"), gates[:].rearrange("p k n -> p (k n)"), valid[:], ALU.mult))

                        @block.scalar
                        def _(act):
                            act.wait_ge(S["t_ratio"], 1)
                            act.activation(ratio[:], ratio[:], ACT.Exp).then_inc(S["t_exp"], 1)

                        @block.tensor
                        def _(pe):
                            pe.wait_ge(S["t_choice"], 1)
                            flat = choice_bf[:].rearrange("p k n e -> p (k n e)")
                            pe.matmul(ps[:, 0, :], before[:], flat, start=True, stop=True)
                            pe.matmul(ps[:, 1, :], ones[:], flat, start=True, stop=True).then_inc(S["t_pos"], 1)

                        @block.gpsimd
                        def _(pool):
                            pool.wait_ge(S["t_to"], 1)
                            for i in range(CHOICES):
                                pool.indirect_dma_start(
                                    slots_dram, bass.IndirectOffsetOnAxis(ap=to_slot[:, i:i + 1], axis=0),
                                    h_rows[:, i % TILES, :], None).then_inc(S["t_sent"], 16)
                            pool.wait_ge(S["t_sent"], 16 * CHOICES)
                    S.end()

            w1 = [sb(f"w1_{i}", [P, HID], stack=own) for i in range(2)]
            w2 = [sb(f"w2_{i}", [P, HT, P], stack=own) for i in range(2)]
            b1 = sb("b1", [P, E1, HT], stack=own)
            b2 = sb("b2", [P, E1, P], stack=own)
            cur_b1 = [sb(f"cur_b1_{i}", [P, HT], stack=own) for i in range(2)]
            slots = [sb(f"slots{i}", [P, ST, P], stack=own) for i in range(2)]
            slotsT = [sb(f"slotsT{i}", [P, ROOM], stack=own) for i in range(2)]
            hid = [sb(f"hid{i}", [P, HT, ROOM], stack=own) for i in range(2)]
            slot_out = [sb(f"slot_out{i}", [P, ST, P], stack=own) for i in range(2)]
            S = phase("b_in")
            with nc.Block() as block:
                @block.sync
                def _(sp):
                    sp.dma_start(b1[:], t["b1"]).then_inc(S["b_in"], 16)
                    sp.dma_start(b2[:], t["b2"]).then_inc(S["b_in"], 16)
                    sp.wait_ge(S["b_in"], 32)
            S.end()

            S = phase("e_in0", "e_in1", "e_b1", "e_turned", "e_slotsT", "e_hid_ps", "e_hid", "e_out_ps", "e_out", "e_stored")
            with nc.Fori(0, E1 // 2) as e2:
                with nc.Block() as block:
                    @block.sync
                    def _(sp):
                        for i in range(2):
                            e = e2 * 2 + i
                            sp.dma_start(slots[i][:], slots_dram[bass.ds(e * ROOM, ROOM)].rearrange("(n p) d -> p n d", p=P)) \
                                .then_inc(S[f"e_in{i}"], 16)
                            sp.dma_start(w1[i][:], t["w1"][e]).then_inc(S[f"e_in{i}"], 16)
                            sp.dma_start(w2[i][:], t["w2"][e].rearrange("(j p) d -> p j d", p=P)).then_inc(S[f"e_in{i}"], 16)
                        for i in range(2):
                            sp.wait_ge(S["e_out"], 2 * i + 2)
                            sp.dma_start(outs_dram[bass.ds((e2 * 2 + i) * ROOM, ROOM)].rearrange("(n p) d -> p n d", p=P),
                                         slot_out[i][:]).then_inc(S["e_stored"], 16)
                        sp.wait_ge(S["e_stored"], 32)

                    @block.tensor
                    def _(pe):
                        for i in range(2):
                            pe.wait_ge(S[f"e_in{i}"], 48)
                            for n in range(ST):
                                last = pe.transpose(ps[:, n // 4, (n % 4) * P:(n % 4 + 1) * P], slots[i][:, n, :], ident[:])
                            last.then_inc(S["e_turned"], 1)
                            pe.wait_ge(S["e_slotsT"], i + 1)
                            for j in range(HT):
                                q = i * HT + j
                                if q >= 2:
                                    pe.wait_ge(S["e_hid"], q - 1)
                                for c in range(2):
                                    last = pe.matmul(ps[:, 2 + 2 * (q % 2) + c, :], w1[i][:, j * P:(j + 1) * P],
                                                     slotsT[i][:, c * BANK:(c + 1) * BANK], start=True, stop=True)
                                last.then_inc(S["e_hid_ps"], 1)
                            pe.wait_ge(S["e_hid"], (i + 1) * HT)
                            for n in range(ST):
                                if i and n % 4 == 0:
                                    pe.wait_ge(S["e_out"], n // 4 + 1)
                                for j in range(HT):
                                    last = pe.matmul(ps[:, 6 + n // 4, (n % 4) * P:(n % 4 + 1) * P],
                                                     hid[i][:, j, n * P:(n + 1) * P], w2[i][:, j, :],
                                                     start=(j == 0), stop=(j == HT - 1))
                                if n % 4 == 3:
                                    last.then_inc(S["e_out_ps"], 1)

                    @block.scalar
                    def _(act):
                        for i in range(2):
                            act.wait_ge(S["e_turned"], i + 1)
                            act.activation(slotsT[i][:], ps[:, 0:2, :].rearrange("p a n -> p (a n)"), ACT.Copy) \
                                .then_inc(S["e_slotsT"], 1)
                            act.wait_ge(S["e_b1"], i + 1)
                            for j in range(HT):
                                q = i * HT + j
                                act.wait_ge(S["e_hid_ps"], q + 1)
                                act.activation(hid[i][:, j, :], ps[:, 2 + 2 * (q % 2):4 + 2 * (q % 2), :].rearrange("p a n -> p (a n)"),
                                               ACT.Relu, bias=cur_b1[i][:, j:j + 1]).then_inc(S["e_hid"], 1)

                    @block.vector
                    def _(dve):
                        for i in range(2):
                            dve.tensor_copy(cur_b1[i][:].unsqueeze(1), b1[:, bass.ds(e2 * 2 + i, 1), :]).then_inc(S["e_b1"], 1)
                        for i in range(2):
                            for c in range(2):
                                dve.wait_ge(S["e_out_ps"], 2 * i + c + 1)
                                dve.tensor_tensor(slot_out[i][:, 4 * c:4 * c + 4, :], ps[:, 6 + c, :].rearrange("p (n d) -> p n d", d=P),
                                                  b2[:, bass.ds(e2 * 2 + i, 1), :].to_broadcast([P, 4, P]), ALU.add) \
                                    .then_inc(S["e_out"], 1)
                S.end()

            S = phase(*[f"g_got{b}" for b in range(B)], "g_dve")
            got = [sb(f"got{i}", [P, K, NT, P], stack=own) for i in range(2)]
            with nc.Block() as block:
                @block.gpsimd
                def _(pool):
                    for b in range(B):
                        if b >= 2:
                            pool.wait_ge(S["g_dve"], 4 * (b - 1))
                        for k in range(K):
                            for n in range(NT):
                                i = k * TILES + b * NT + n
                                pool.indirect_dma_start(
                                    got[b % 2][:, k, n, :], None, outs_dram,
                                    bass.IndirectOffsetOnAxis(ap=from_slot[:, i:i + 1], axis=0)).then_inc(S[f"g_got{b}"], 16)

                @block.vector
                def _(dve):
                    ch = Chain(dve, S["g_dve"])
                    for b in range(B):
                        dve.wait_ge(S[f"g_got{b}"], 16 * K * NT)
                        r = got[b % 2]
                        ch.link(dve.tensor_tensor(r[:], r[:], gates[:, :, b * NT:(b + 1) * NT].unsqueeze(3)
                                                  .to_broadcast([P, K, NT, P]), ALU.mult))
                        ch.link(dve.tensor_tensor(r[:, 0], r[:, 0], r[:, 1], ALU.add))
                        ch.link(dve.tensor_tensor(r[:, 0], r[:, 0], mod1_rows[:, b, 5:6, :].to_broadcast([P, NT, P]), ALU.mult))
                        dst = x_all[:, b * NT:(b + 1) * NT, :]
                        ch.link(dve.tensor_tensor(dst, dst, r[:, 0], ALU.add))
            S.end()

        S = phase("out_stored")
        with nc.Block() as block:
            @block.sync
            def _(sp):
                sp.dma_start(t["out"].rearrange("b (n p) d -> p (b n) d", p=P), x_all[:]).then_inc(S["out_stored"], 16)
                sp.wait_ge(S["out_stored"], 16)


def kernel(**inputs):
    import concourse.bacc as bacc
    from concourse.bass_utils import run_bass_kernel_spmd

    f = {n: np.asarray(a) for n, a in inputs.items()}
    B, T, _ = f["L0_attn_x"].shape
    E0, I, _ = f["L0_ffn_gate_proj"].shape
    E1, _, HID = f["L1_ffn_w1"].shape
    p = np.arange(P)
    expert_of = np.arange(E0 * I) // I
    owner_rows = np.zeros((3 * 32, E0 * I), np.float32)
    for w in range(3):
        owner_rows[32 * w:32 * w + E0] = expert_of[None, :] == np.arange(E0)[:, None]
    below = np.broadcast_to((np.arange(E0)[None, :] < np.arange(E0)[:, None]).astype(np.float32), (P, E0, E0))
    distance = np.maximum(p[:, None] - p[None, :] - 1, 0).astype(np.float32)
    later = (p[:, None] > p[None, :]).astype(np.float32) / np.sqrt(np.float32(P))
    to_end = np.broadcast_to((P - 1 - p).astype(np.float32), (P, P))
    from_start = p[:, None].astype(np.float32)
    before = (p[:, None] < p[None, :]).astype(np.float32)
    expert_id = np.broadcast_to(np.arange(E1, dtype=np.float32), (P, E1))
    spill = np.arange(2 * B * T, dtype=np.float32).reshape(-1, P).T
    arrays = {
        "x": f["L0_attn_x"], "ident": np.eye(P, dtype=np.float32),
        "cT0": f["L0_c"].T, "cT1": f["L1_c"].T, "wmod0": f["L0_wmod"], "wmod1": f["L1_wmod"],
        "wq0": f["L0_attn_Wq"].T, "wk0": f["L0_attn_Wk"].T, "wv0": f["L0_attn_Wv"].T,
        "router0": f["L0_ffn_gate_w"].T, "bias0": np.broadcast_to(f["L0_ffn_gate_bias"], (P, E0)),
        "gate0": np.concatenate([f["L0_ffn_gate_proj"].reshape(E0 * I, P), f["L0_ffn_shared_gate_w"]]).T,
        "up0": np.concatenate([f["L0_ffn_up_proj"].reshape(E0 * I, P), f["L0_ffn_shared_up_w"]]).T,
        "down0": np.concatenate([f["L0_ffn_down_proj"].transpose(0, 2, 1).reshape(E0 * I, P),
                                 f["L0_ffn_shared_down_w"].T]),
        "owner": owner_rows, "below": below,
        "wq1": f["L1_attn_Wq"], "wk1": f["L1_attn_Wk"], "wv1": f["L1_attn_Wv"], "wo1": f["L1_attn_Wo"].T,
        "decay": np.broadcast_to(f["L1_attn_decay_logit"].reshape(1, 1), (P, 1)),
        "out_scale": np.broadcast_to(f["L1_attn_out_scale"].reshape(1, 1), (P, 1)),
        "distance": distance, "later": later, "to_end": to_end, "from_start": from_start,
        "router1": f["L1_ffn_wg"], "w1": f["L1_ffn_w1"], "b1": f["L1_ffn_b1"].reshape(E1, HID // P, P).transpose(2, 0, 1),
        "w2": f["L1_ffn_w2"], "b2": np.broadcast_to(f["L1_ffn_b2"], (P, E1, P)),
        "before": before, "expert_id": expert_id, "spill": spill,
    }
    arrays = {f"in_{n}_dram": np.ascontiguousarray(a) for n, a in arrays.items()}
    nc = bacc.Bacc("TRN2", target_bir_lowering=False, num_devices=1)
    t = {n[3:-5]: nc.dram_tensor(n, a.shape, mybir.dt.from_np(a.dtype), kind="ExternalInput").ap()
         for n, a in arrays.items()}
    t["out"] = nc.dram_tensor("out_0_dram", (B, T, P), F32, kind="ExternalOutput").ap()
    adaln_program(nc, t, {"B": B, "T": T, "E0": E0, "I": f["L0_ffn_gate_proj"].shape[1],
                          "E1": f["L1_ffn_w1"].shape[0], "HID": f["L1_ffn_w1"].shape[2]})
    r = run_bass_kernel_spmd(nc, [arrays], core_ids=[0])
    return r.results[0]["out_0_dram"]
```

```python
from contextlib import ExitStack

import numpy as np
import concourse.bass as bass
from concourse import mybir

F32 = mybir.dt.float32
F32R = mybir.dt.float32r
BF16 = mybir.dt.bfloat16
U16 = mybir.dt.uint16
U32 = mybir.dt.uint32
ALU = mybir.AluOpType
ACT = mybir.ActivationFunctionType
AX = mybir.AxisListType.X

P = 128
BANK = 512
EPS = 1e-5


class Phase:

    def __init__(self, nc, ctx, names):
        self.nc = nc
        handles = [ctx.enter_context(nc.semaphore(n)) for n in names]
        self.by_name = dict(zip(names, handles))
        nums = [h.num for h in handles]
        assert nums == list(range(nums[0], nums[0] + len(nums)))
        self.nums = range(nums[0], nums[-1] + 1)

    def __getitem__(self, name):
        return self.by_name[name]

    def end(self):
        self.nc.all_engine_barrier(sems_to_clear=self.nums)


class Chain:

    def __init__(self, eng, sem):
        self.eng, self.sem, self.n = eng, sem, 0

    def did(self, ins):
        self.n += 1
        ins.then_inc(self.sem, 1)
        return self.n

    def wait(self):
        self.eng.wait_ge(self.sem, self.n)

    def link(self, ins):
        self.did(ins)
        self.wait()


class NormBuffers:

    def __init__(self, name, cols, xb, xn, hT, stats, mv, ln):
        self.name, self.cols, self.xb, self.xn, self.hT = name, cols, xb, xn, hT
        self.stats, self.mv, self.ln = stats, mv, ln


def adaln_program(nc, t, shape):
    B, T = shape["B"], shape["T"]
    NT = T // P
    TILES = B * NT
    HEADS, HD = 16, P // 16
    GROUPS = 4
    GH = HEADS // GROUPS
    QUAD = P // GH
    PARTS = 3
    TERMS = PARTS * PARTS
    KROWS = TERMS * HD
    SROWS = KROWS + PARTS
    HALF = T // 2
    STEPS = 2 * NT
    assert HALF == BANK and GH * QUAD == P

    with ExitStack() as ctx:
        def sb(name, shp, dt=F32, stack=ctx):
            return stack.enter_context(nc.sbuf_tensor(name, shp, dt))

        def phase(*names):
            return Phase(nc, ctx, names)

        ps = ctx.enter_context(nc.psum_tensor("psum", [P, 8, BANK], F32))

        def product(pe, out, lhs, rhs, start=True, stop=True):
            (lh, ll), (rh, rl) = lhs, rhs
            pe.matmul(out, lh, rh, start=start, stop=False)
            pe.matmul(out, lh, rl, start=False, stop=False)
            return pe.matmul(out, ll, rh, start=False, stop=stop)

        def minus_high(eng, low, full, high):
            return eng.tensor_tensor(low, full, high.bitcast(F32), ALU.subtract)

        x_all = sb("x_all", [P, TILES, P])
        ident = sb("ident", [P, P])
        silu_cT = sb("silu_cT", [P, 2, B])
        mod_cols = sb("mod_cols", [P, 2, B, 6])
        ga0_rows = sb("ga0_rows", [P, B, P])
        mod1_rows = sb("mod1_rows", [P, B, 6, P])
        cur_cols = sb("cur_cols", [P, 6])
        xb = sb("xb", [P, NT, P])
        xn = sb("xn", [P, NT, P])
        hT = sb("hT", [P, T])
        stats = sb("stats", [P, NT, 6])
        mv = sb("mv", [P, NT, 2])
        ln = sb("ln", [P, 8, NT])

        q_dram = nc.dram_tensor("q_parts", [B, PARTS, P, T], BF16, kind="Internal").ap()
        k_dram = nc.dram_tensor("k_parts", [B, PARTS, P, T], BF16, kind="Internal").ap()
        v_dram = nc.dram_tensor("v_padded", [B, P, NT, HEADS * QUAD], F32, kind="Internal").ap()

        qk_w = sb("qk_w", [P, P])
        vo_w = sb("vo_w", [P, P])
        out_scale = sb("out_scale", [P, 1])
        mask = sb("mask", [P, P])
        end_powers = sb("end_powers", [P, P])
        start_powers = sb("start_powers", [P, 1])
        chunk_power = sb("chunk_power", [P, 1])

        STORES = 16 * (2 * PARTS + 1)
        qkv_free = ctx.enter_context(nc.semaphore("qkv_free"))
        qkv_own = ctx.enter_context(ExitStack())
        wqkv = sb("wqkv", [P, 3, P], stack=qkv_own)
        v_pad = sb("v_pad", [P, NT, HEADS, QUAD], stack=qkv_own)

        with ExitStack() as own:
            w1q = sb("w1q", [P, 4, P], stack=own)
            decay = sb("decay", [P, 8], stack=own)
            distance = sb("distance", [P, P], stack=own)
            later = sb("later", [P, P], stack=own)
            to_end = sb("to_end", [P, P], stack=own)
            from_start = sb("from_start", [P, 1], stack=own)
            powers = sb("powers", [P, P], stack=own)
            S = phase("m_later", "m_ones", "m_in", "m_sig", "m_silu", "m_bc", "m_cols", "m_rows", "m_gate", "m_done")
            cT = sb("cT", [P, 2, B], stack=own)
            sig = sb("sig", [P, 2, B], stack=own)
            silu_bc = sb("silu_bc", [P, 2, B, P], stack=own)
            wmod = sb("wmod", [P, 2, 6 * P], stack=own)
            sgn = sb("sgn", [P, B, P], stack=own)
            sgc = sb("sgc", [P, 2, B, 2], stack=own)
            mag = sb("mag", [P, B, P], stack=own)
            magc = sb("magc", [P, 2, B, 2], stack=own)
            with nc.Block() as block:
                @block.sync
                def _(sp):
                    for i in range(2):
                        sp.dma_start(cT[:, i, :], t[f"cT{i}"]).then_inc(S["m_in"], 16)
                    for i in range(2):
                        sp.dma_start(wmod[:, i, :], t[f"wmod{i}"]).then_inc(S["m_in"], 16)
                    sp.dma_start(x_all[:], t["x"].rearrange("b (n p) d -> p (b n) d", p=P)).then_inc(S["m_later"], 16)
                    sp.dma_start(ident[:], t["ident"]).then_inc(S["m_later"], 16)
                    for i, w in enumerate(("wq0", "wk0", "wv0")):
                        sp.dma_start(wqkv[:, i, :], t[w]).then_inc(S["m_later"], 16)
                    for i, n in enumerate(("wq1", "wk1", "wv1", "wo1")):
                        sp.dma_start(w1q[:, i, :], t[n]).then_inc(S["m_later"], 16)
                    for dst, n in ((decay[:, 0:1], "decay"), (out_scale[:], "out_scale"), (distance[:], "distance"),
                                   (later[:], "later"), (to_end[:], "to_end"), (from_start[:], "from_start")):
                        sp.dma_start(dst, t[n]).then_inc(S["m_later"], 16)
                    sp.wait_ge(S["m_later"], 16 * 15)

                @block.gpsimd
                def _(pool):
                    pool.memset(v_pad[:], 0.0).then_inc(S["m_ones"], 1)
                    pool.wait_ge(S["m_ones"], 1)
                    pool.memset(v_pad[:, :, :, HD:HD + 1], 1.0).then_inc(qkv_free, 1)

                @block.scalar
                def _(act):
                    act.wait_ge(S["m_in"], 16 * 4)
                    act.activation(sig[:], cT[:], ACT.Sigmoid).then_inc(S["m_sig"], 1)

                @block.vector
                def _(dve):
                    own_steps = Chain(dve, S["m_done"])

                    def keep_from_zero(g, sign, size):
                        own_steps.did(dve.tensor_scalar(sign, g, 0.0, 2.0, ALU.is_ge, ALU.mult))
                        own_steps.link(dve.scalar_tensor_tensor(size, g, -1.0, g, ALU.mult, ALU.max))
                        own_steps.link(dve.tensor_scalar(size, size, 0.25, None, ALU.max))
                        own_steps.link(dve.scalar_tensor_tensor(g, sign, 1.0, size, ALU.subtract, ALU.mult))

                    dve.wait_ge(S["m_sig"], 1)
                    dve.tensor_tensor(silu_cT[:], cT[:], sig[:], ALU.mult).then_inc(S["m_silu"], 1)
                    dve.wait_ge(S["m_silu"], 1)
                    for i in range(2):
                        dve.tensor_copy(silu_bc[:, i], silu_cT[:, i, :].unsqueeze(2).to_broadcast([P, B, P])) \
                            .then_inc(S["m_bc"], 1)
                    dve.wait_ge(S["m_cols"], 1)
                    own_steps.link(dve.tensor_copy(
                        mod_cols[:], ps[:, 0, 0:2 * 6 * B].rearrange("p (i v b) -> p i b v", i=2, v=6)))
                    for v in (1, 4):
                        own_steps.did(dve.tensor_scalar(mod_cols[:, :, :, v], mod_cols[:, :, :, v], 1.0, None, ALU.add))
                    g = mod_cols[:].rearrange("p i b (w v) -> p i b w v", w=2)[:, :, :, :, 2]
                    keep_from_zero(g.rearrange("p i b w -> p (i b w)"), sgc[:].rearrange("p i b w -> p (i b w)"),
                                   magc[:].rearrange("p i b w -> p (i b w)"))
                    dve.wait_ge(S["m_rows"], 1)
                    own_steps.did(dve.tensor_copy(ga0_rows[:], ps[:, 1, :].rearrange("p (b d) -> p b d", b=B)))
                    own_steps.link(dve.tensor_copy(mod1_rows[:].rearrange("p b v d -> p (b v d)"),
                                                   ps[:, 2:8, :].rearrange("p a n -> p (a n)")))
                    for v in (1, 4):
                        own_steps.did(dve.tensor_scalar(mod1_rows[:, :, v, :], mod1_rows[:, :, v, :], 1.0, None, ALU.add))
                    keep_from_zero(ga0_rows[:], sgn[:], mag[:])
                    for v in (2, 5):
                        keep_from_zero(mod1_rows[:, :, v, :], sgn[:], mag[:])

                @block.tensor
                def _(pe):
                    pe.wait_ge(S["m_silu"], 1)
                    for i in range(2):
                        for v in range(6):
                            o = (i * 6 + v) * B
                            last = pe.matmul(ps[:, 0, o:o + B], wmod[:, i, v * P:(v + 1) * P], silu_cT[:, i, :],
                                             start=True, stop=True)
                    last.then_inc(S["m_cols"], 1)
                    pe.wait_ge(S["m_bc"], 2)
                    for b in range(B):
                        pe.matmul(ps[:, 1, b * P:(b + 1) * P], silu_bc[:, 0, b, :], wmod[:, 0, 2 * P:3 * P],
                                  start=True, stop=True)
                    for b in range(B):
                        for v in range(6):
                            q = b * 6 + v
                            last = pe.matmul(ps[:, 2 + q // 4, (q % 4) * P:(q % 4 + 1) * P], silu_bc[:, 1, b, :],
                                             wmod[:, 1, v * P:(v + 1) * P], start=True, stop=True)
                    last.then_inc(S["m_rows"], 1)
            S.end()

            S = phase("l_dve", "l_act", "l_pe", "l_copied")
            with nc.Block() as block:
                @block.tensor
                def _(pe):
                    pe.matmul(ps[:, 0, 0:P], w1q[:, 0, :], w1q[:, 1, :], start=True, stop=True)
                    pe.matmul(ps[:, 1, 0:P], w1q[:, 2, :], w1q[:, 3, :], start=True, stop=True).then_inc(S["l_pe"], 1)

                @block.vector
                def _(dve):
                    ch = Chain(dve, S["l_dve"])
                    ch.link(dve.scalar_tensor_tensor(decay[:, 1:2], decay[:, 0:1], -1.0, decay[:, 0:1], ALU.mult, ALU.min))
                    dve.wait_ge(S["l_act"], 2)
                    ch.link(dve.scalar_tensor_tensor(decay[:, 4:5], decay[:, 0:1], 0.0, decay[:, 3:4], ALU.min, ALU.subtract))
                    dve.wait_ge(S["l_act"], 6)
                    ch.did(dve.tensor_tensor(mask[:], powers[:], later[:], ALU.mult))
                    ch.did(dve.tensor_scalar(end_powers[:], end_powers[:], float(np.float32(P) ** -0.5), None, ALU.mult))
                    dve.wait_ge(S["l_pe"], 1)
                    ch.did(dve.tensor_copy(qk_w[:], ps[:, 0, 0:P]))
                    ch.did(dve.tensor_copy(vo_w[:], ps[:, 1, 0:P]))

                @block.scalar
                def _(act):
                    ch = Chain(act, S["l_act"])
                    act.wait_ge(S["l_dve"], 1)
                    ch.link(act.activation(decay[:, 2:3], decay[:, 1:2], ACT.Exp))
                    ch.link(act.activation(decay[:, 3:4], decay[:, 2:3], ACT.Ln, bias=1.0))
                    act.wait_ge(S["l_dve"], 2)
                    log = decay[:, 4:5]
                    ch.did(act.activation(powers[:], distance[:], ACT.Exp, scale=log))
                    ch.did(act.activation(end_powers[:], to_end[:], ACT.Exp, scale=log))
                    ch.did(act.activation(start_powers[:], from_start[:], ACT.Exp, scale=log))
                    ch.did(act.activation(chunk_power[:], log, ACT.Exp, scale=float(P)))
            S.end()

        first = NormBuffers("ln", cur_cols, xb, xn, hT, stats, mv, ln)

        def norm_vector(dve, S, b, layer, N=first):
            for _ in norm_steps(dve, S, b, layer, N):
                pass

        def norm_steps(dve, S, b, layer, N=first):
            c = Chain(dve, S[N.name + "_dve"])
            c.did(dve.tensor_copy(N.cols[:], mod_cols[:, layer, b, :] if isinstance(b, int) else
                                  mod_cols[:, layer].rearrange("p b v -> p (b v)")[:, bass.ds(b * 6, 6)]))
            c.link(dve.tensor_copy(N.xb[:], x_all[:, bass.ds(b * NT, NT), :]))
            yield
            for n in range(NT):
                c.did(dve.bn_stats(N.stats[:, n, :], N.xb[:, n, :]))
                if n % 4 == 3:
                    yield
            c.wait()
            for n in range(NT):
                c.did(dve.bn_aggr(N.mv[:, n, :], N.stats[:, n, :]))
            c.wait()
            step = [N.ln[:, i, :] for i in range(7)]
            dve.tensor_scalar(step[0], N.mv[:, :, 1], EPS, None, ALU.add).then_inc(S[N.name + "_var"], 1)
            yield
            yield
            dve.wait_ge(S[N.name + "_std"], 1)
            c.link(dve.reciprocal(step[2], step[1]))
            c.link(dve.tensor_tensor(step[3], step[2], step[2], ALU.mult))
            c.link(dve.tensor_tensor(step[4], step[3], step[0], ALU.mult))
            c.link(dve.tensor_scalar(step[5], step[4], -0.5, 1.5, ALU.mult, ALU.add))
            c.link(dve.tensor_tensor(step[6], step[5], step[2], ALU.mult))
            for n in range(NT):
                if n % 2 == 0:
                    yield
                dve.tensor_scalar(N.xn[:, n, :], N.xb[:, n, :], N.mv[:, n, 0:1], N.ln[:, 6, n:n + 1],
                                  ALU.subtract, ALU.mult).then_inc(S[N.name + "_xn"], 1)

        def norm_scalar(act, S, shift, scale, N=first, bank=0):
            act.wait_ge(S[N.name + "_var"], 1)
            act.activation(N.ln[:, 1, :], N.ln[:, 0, :], ACT.Sqrt).then_inc(S[N.name + "_std"], 1)
            act.wait_ge(S[N.name + "_xT"], NT)
            act.activation(N.hT[:], ps[:, bank:bank + 2, :].rearrange("p a n -> p (a n)"), ACT.Identity,
                           bias=N.cols[:, shift:shift + 1], scale=N.cols[:, scale:scale + 1]) \
                .then_inc(S[N.name + "_hT"], 1)

        def norm_tensor(pe, S, N=first, bank=0):
            for n in range(NT):
                pe.wait_ge(S[N.name + "_xn"], n + 1)
                pe.transpose(ps[:, bank + n // 4, (n % 4) * P:(n % 4 + 1) * P], N.xn[:, n, :], ident[:]) \
                    .then_inc(S[N.name + "_xT"], 1)

        def batch_phase(prefix, *names):
            S = phase(*[f"{prefix}_{n}" for n in LN], *[f"{prefix}_{n}" for n in names])
            S.by_name = {n[len(prefix) + 1:]: h for n, h in S.by_name.items()}
            return S

        LN = ("ln_dve", "ln_var", "ln_std", "ln_xn", "ln_xT", "ln_hT")

        with ExitStack() as own:
            part = [[sb(f"part{w}{i}", [P, T], BF16, stack=own) for i in range(PARTS)] for w in "qk"]
            rest = [sb(f"rest{w}", [P, T], stack=own) for w in "qk"]

            S = batch_phase("qkv", "q", "k", "v", "high0", "high1", "rest0", "rest1", "mid0", "mid1", "low", "vpad")
            with nc.Fori(0, B) as b:
                with nc.Block() as block:
                    @block.vector
                    def _(dve):
                        norm_vector(dve, S, b, 0)
                        dve.wait_ge(qkv_free, b * STORES + 1)
                        for w in range(2):
                            dve.wait_ge(S[f"high{w}"], 1)
                            dve.tensor_tensor(rest[w][:], ps[:, 2 + 2 * w:4 + 2 * w, :].rearrange("p a n -> p (a n)"),
                                              part[w][0][:], ALU.subtract).then_inc(S[f"rest{w}"], 1)
                        gate = ga0_rows[:, bass.ds(b, 1), :].to_broadcast([P, 4, P])
                        for c in range(2):
                            dve.wait_ge(S["v"], 4 * (c + 1))
                            dve.tensor_tensor(
                                v_pad[:, 4 * c:4 * c + 4, :, 0:HD],
                                ps[:, 6 + c, :].rearrange("p (n h d) -> p n h d", n=4, d=HD),
                                gate.rearrange("p n (h d) -> p n h d", d=HD), ALU.mult).then_inc(S["vpad"], 1)
                        for w in range(2):
                            dve.wait_ge(S[f"mid{w}"], 1)
                            dve.tensor_tensor(part[w][2][:], rest[w][:], part[w][1][:], ALU.subtract) \
                                .then_inc(S["low"], 1)

                    @block.scalar
                    def _(act):
                        norm_scalar(act, S, 0, 1)
                        act.wait_ge(qkv_free, b * STORES + 1)
                        for w in range(2):
                            act.wait_ge(S["q" if w == 0 else "k"], 1)
                            act.activation(part[w][0][:], ps[:, 2 + 2 * w:4 + 2 * w, :].rearrange("p a n -> p (a n)"),
                                           ACT.Copy).then_inc(S[f"high{w}"], 1)
                        for w in range(2):
                            act.wait_ge(S[f"rest{w}"], 1)
                            act.activation(part[w][1][:], rest[w][:], ACT.Copy).then_inc(S[f"mid{w}"], 1)

                    @block.tensor
                    def _(pe):
                        norm_tensor(pe, S)
                        pe.wait_ge(S["ln_hT"], 1)
                        for w in range(2):
                            for c in range(2):
                                last = pe.matmul(ps[:, 2 + 2 * w + c, :], wqkv[:, w, :], hT[:, c * BANK:(c + 1) * BANK],
                                                 start=True, stop=True)
                            last.then_inc(S["q" if w == 0 else "k"], 1)
                        for n in range(NT):
                            pe.matmul(ps[:, 6 + n // 4, (n % 4) * P:(n % 4 + 1) * P], hT[:, n * P:(n + 1) * P],
                                      wqkv[:, 2, :], start=True, stop=True).then_inc(S["v"], 1)

                    @block.sync
                    def _(sp):
                        for i, (s, n) in enumerate((("high", 1), ("mid", 1))):
                            for w, dram in enumerate((q_dram, k_dram)):
                                sp.wait_ge(S[f"{s}{w}"], n)
                                sp.dma_start(dram[b, i], part[w][i][:]).then_inc(qkv_free, 16)
                        sp.wait_ge(S["vpad"], 2)
                        sp.dma_start(v_dram[b], v_pad[:].rearrange("p n h d -> p n (h d)")).then_inc(qkv_free, 16)
                        for w, dram in enumerate((q_dram, k_dram)):
                            sp.wait_ge(S["low"], w + 1)
                            sp.dma_start(dram[b, 2], part[w][2][:]).then_inc(qkv_free, 16)
                S.end()

        qkv_own.close()

        E0, I = shape["E0"], shape["I"]
        FEATS = E0 * I
        ALL = t["gate0"].shape[1]
        ROUTED = FEATS // P
        FT = -(-ALL // P)
        rows_of = [min(P, ALL - j * P) for j in range(FT)]
        full = ALL // P
        ffn_own = ctx.enter_context(ExitStack())
        gate_raw = sb("gate_raw", [P, ALL], stack=ffn_own)
        up_raw = sb("up_raw", [P, ALL], stack=ffn_own)
        down_raw = sb("down_raw", [P, FT, P], stack=ffn_own)
        router = sb("router0", [P, E0], stack=ffn_own)
        bias = sb("bias0", [P, E0], stack=ffn_own)
        below = sb("below", [P, E0, E0], stack=ffn_own)
        owner = sb("owner", [3 * 32, FEATS], BF16, stack=ffn_own)
        E1, HID = shape["E1"], shape["HID"]
        K = 2
        TOKENS = B * T
        ROOM = K * (-(-TOKENS // E1))
        SLOTS = E1 * ROOM
        ST = ROOM // P
        slots_dram = nc.dram_tensor("slots", [SLOTS + K * TOKENS, P], F32, kind="Internal").ap()

        with ExitStack() as own:
            S = phase("a_load0", "a_load1", "a_load2", "a_load3", "a_scores", "a_exp", "a_maxmm", "a_max",
                      "a_rowT", "a_neg", "a_negrows", "a_pv", "a_oT", "a_turned", "a_free7", "a_dve", "a_ones", "a_zeros",
                      "a_other")
            q_ops = [sb(f"q_ops{g}", [P, GH, T], BF16, stack=own) for g in range(GROUPS)]
            k_ops = [sb(f"k_ops{g}", [P, GH, T], BF16, stack=own) for g in range(GROUPS)]
            v_ops = [sb(f"v_ops{g}", [P, NT, P], stack=own) for g in range(GROUPS)]
            prob = [sb(f"prob{i}", [P, GH, BANK], stack=own) for i in range(2)]
            row_max = [sb(f"row_max{i}", [P, GH * NT], stack=own) for i in range(2)]
            neg = sb("neg", [GH * NT, P], stack=own)
            neg_rest = sb("neg_rest", [GH * NT, P], stack=own)
            neg_part = [sb(f"neg_part{i}", [GH * NT, P], BF16, stack=own) for i in range(PARTS)]
            oT = sb("oT", [P, 2, BANK], stack=own)
            recip = sb("recip", [P, 4, GH], stack=own)
            head_out = sb("head_out", [P, 4, GH * HD], stack=own)
            zeros = sb("zeros", [P, ST, P], stack=own)

            def load_unit(sp, b, g):
                sem = S[f"a_load{g}"]
                rows = slice(g * GH * HD, (g + 1) * GH * HD)
                for i in range(PARTS):
                    for j in range(PARTS):
                        r = (i * PARTS + j) * HD
                        sp.dma_start(q_ops[g][r:r + HD],
                                     q_dram[b, i, rows, :].rearrange("(h d) t -> d h t", d=HD)).then_inc(sem, 16)
                        sp.dma_start(k_ops[g][r:r + HD],
                                     k_dram[b, j, rows, :].rearrange("(h d) t -> d h t", d=HD)).then_inc(sem, 16)
                sp.dma_start(v_ops[g][:], v_dram[b, :, :, g * P:(g + 1) * P]).then_inc(sem, 16)

            LOADED = 16 * (2 * TERMS + 1)

            ROWS = GH * NT
            PER_STEP = ROWS // STEPS
            AHEAD = 4 * PER_STEP

            def max_scores(pe, g, i, asked):
                h, n = divmod(i, NT)
                if asked >= 2:
                    pe.wait_ge(S["a_max"], asked - 1)
                for c in range(2):
                    last = pe.matmul(ps[:, 2 + 2 * (i % 2) + c, :], q_ops[g][0:KROWS, h, n * P:(n + 1) * P],
                                     k_ops[g][0:KROWS, h, c * BANK:(c + 1) * BANK], start=True, stop=True)
                last.then_inc(S["a_maxmm"], 1)

            def reduce_max(dve, rows, i, asked):
                dve.wait_ge(S["a_maxmm"], asked + 1)
                dve.tensor_reduce(rows[:, i:i + 1], ps[:, 2 + 2 * (i % 2):4 + 2 * (i % 2), :].rearrange("p a n -> p (a n)"),
                                  axis=AX, op=ALU.max).then_inc(S["a_max"], 1)

            def store_neg(sp, g, count):
                sp.wait_ge(S["a_neg"], count)
                for i in range(PARTS):
                    sp.dma_start(q_ops[g][KROWS + i:KROWS + i + 1].rearrange("p h (n q) -> p (h n) q", q=P),
                                 neg_part[i][:]).then_inc(S["a_negrows"], 16)

            def split_neg(dve, ch):
                ch.link(dve.tensor_copy(neg_part[0][:], neg[:]))
                ch.link(dve.tensor_tensor(neg_rest[:], neg[:], neg_part[0][:], ALU.subtract))
                ch.link(dve.tensor_copy(neg_part[1][:], neg_rest[:]))
                dve.tensor_tensor(neg_part[2][:], neg_rest[:], neg_part[1][:], ALU.subtract).then_inc(S["a_neg"], 1)

            with nc.Block() as block:
                @block.vector
                def _(dve):
                    c = Chain(dve, S["a_dve"])
                    for i in range(ROWS):
                        reduce_max(dve, row_max[1], i, i)
                    dve.wait_ge(S["a_rowT"], 1)
                    c.link(dve.tensor_scalar(neg[:], ps[0:ROWS, 7, 0:P], -1.0, None, ALU.mult))
                    split_neg(dve, c)
                    for i in range(AHEAD):
                        reduce_max(dve, row_max[0], i, ROWS + i)

                @block.gpsimd
                def _(pool):
                    for g in range(GROUPS):
                        pool.memset(k_ops[g][KROWS // 32 * 32:], 1.0).then_inc(S["a_ones"], 1)
                    pool.wait_ge(S["a_ones"], GROUPS)
                    pool.memset(zeros[:], 0.0).then_inc(S["a_zeros"], 1)

                @block.sync
                def _(sp):
                    sp.wait_ge(qkv_free, B * STORES + 1)
                    for g in range(GROUPS - 1):
                        sp.wait_ge(S["a_ones"], g + 1)
                        load_unit(sp, 0, g)
                    others = 7
                    for dst, n in ((router[:], "router0"), (bias[:], "bias0"), (below[:], "below"), (owner[:].bitcast(U16), "owner")):
                        sp.dma_start(dst, t[n]).then_inc(S["a_other"], 16)
                    sp.dma_start(gate_raw[:], t["gate0"]).then_inc(S["a_other"], 16)
                    sp.dma_start(up_raw[:], t["up0"]).then_inc(S["a_other"], 16)
                    sp.dma_start(down_raw[:, 0:full, :], t["down0"][0:full * P].rearrange("(j p) d -> p j d", p=P)) \
                        .then_inc(S["a_other"], 16)
                    if full < FT:
                        sp.dma_start(down_raw[0:rows_of[-1], full, :], t["down0"][full * P:ALL]) \
                            .then_inc(S["a_other"], 16)
                        others += 1
                    sp.wait_ge(S["a_zeros"], 1)
                    for e in range(E1):
                        sp.dma_start(slots_dram[e * ROOM:(e + 1) * ROOM].rearrange("(n p) d -> p n d", p=P), zeros[:]) \
                            .then_inc(S["a_other"], 16)
                    others += E1
                    store_neg(sp, 0, 1)
                    sp.wait_ge(S["a_negrows"], 48)
                    for g in range(GROUPS - 1):
                        sp.wait_ge(S[f"a_load{g}"], LOADED)
                    sp.wait_ge(S["a_other"], 16 * others)

                @block.tensor
                def _(pe):
                    pe.wait_ge(S["a_load0"], LOADED)
                    for i in range(ROWS):
                        max_scores(pe, 0, i, i)
                    pe.wait_ge(S["a_max"], ROWS)
                    pe.transpose(ps[0:ROWS, 7, 0:P], row_max[1][:], ident[:]).then_inc(S["a_rowT"], 1)
                    pe.wait_ge(S["a_load1"], LOADED)
                    for i in range(AHEAD):
                        max_scores(pe, 1, i, ROWS + i)
            S.end()

            def attention(b, last_batch):
                stop = ROWS * (GROUPS - 1) if last_batch else ROWS * GROUPS + AHEAD
                to_negate = GROUPS - 1 if last_batch else GROUPS
                turns = []
                for k in range(GROUPS * STEPS):
                    g, s = divmod(k, STEPS)
                    if k % NT == 3 and k > NT:
                        turns.append(("out", (k - 3) // NT - 1))
                    if s == STEPS - 3 and g < to_negate:
                        turns.append(("max", g))
                turns.append(("out", 2 * GROUPS - 1))
                order = {u: i for i, u in enumerate(turns)}

                def asked_for(k):
                    for i in range(AHEAD + k * PER_STEP, AHEAD + (k + 1) * PER_STEP):
                        if i < stop:
                            yield i - AHEAD, i // ROWS, i % ROWS

                with nc.Block() as block:
                    @block.tensor
                    def _(pe):
                        def scores(k, h):
                            g, s = divmod(k, STEPS)
                            c, n = divmod(s, NT)
                            if k or h >= 2:
                                pe.wait_ge(S["a_exp"], 4 * k + h - 1)
                            pe.matmul(ps[:, h % 2, :], k_ops[g][0:SROWS, h, n * P:(n + 1) * P],
                                      q_ops[g][0:SROWS, h, c * BANK:(c + 1) * BANK], start=True, stop=True) \
                                .then_inc(S["a_scores"], 1)

                        def values(k):
                            g, s = divmod(k, STEPS)
                            pe.wait_ge(S["a_exp"], 4 * k + 4)
                            if s % NT == 0 and k:
                                pe.wait_ge(S["a_oT"], k // NT)
                            for h in range(GH):
                                last = pe.matmul(ps[h * QUAD:(h + 1) * QUAD, 6, :], v_ops[g][:, s % NT, h * QUAD:(h + 1) * QUAD],
                                                 prob[k % 2][:, h, :], start=(s % NT == 0), stop=(s % NT == NT - 1))
                            last.then_inc(S["a_pv"], 1)

                        def turn_out(m):
                            pe.wait_ge(S["a_oT"], m + 1)
                            if order["out", m]:
                                pe.wait_ge(S["a_free7"], order["out", m])
                            for i in range(4):
                                last = pe.transpose(ps[:, 7, i * P:(i + 1) * P], oT[:, m % 2, i * P:(i + 1) * P], ident[:])
                            last.then_inc(S["a_turned"], 1)

                        for k in range(GROUPS * STEPS):
                            g, s = divmod(k, STEPS)
                            if s == 0 and g:
                                pe.wait_ge(S["a_negrows"], 48 * g)
                            for h in range(GH):
                                scores(k, h)
                                for i, u, row in (asked_for(k) if h == 1 else ()):
                                    if u == GROUPS - 2 and row == 0:
                                        pe.wait_ge(S["a_load3"], LOADED)
                                    if u >= GROUPS - 1 and row == 0:
                                        pe.wait_ge(S[f"a_load{u - GROUPS + 1}"], LOADED)
                                    max_scores(pe, (u + 1) % GROUPS, row, i)
                            if k:
                                values(k - 1)
                            if k % NT == 3 and k > NT:
                                turn_out((k - 3) // NT - 1)
                            if s == STEPS - 3 and g < to_negate:
                                pe.wait_ge(S["a_max"], ROWS * (g + 1) - AHEAD)
                                if order["max", g]:
                                    pe.wait_ge(S["a_free7"], order["max", g])
                                pe.transpose(ps[0:ROWS, 7, 0:P], row_max[g % 2][:], ident[:]).then_inc(S["a_rowT"], 1)
                        values(GROUPS * STEPS - 1)
                        turn_out(2 * GROUPS - 1)

                    @block.scalar
                    def _(act):
                        def copy_out(m):
                            act.wait_ge(S["a_pv"], (m + 1) * NT)
                            if m >= 2:
                                act.wait_ge(S["a_turned"], m - 1)
                            act.activation(oT[:, m % 2, :], ps[:, 6, :], ACT.Copy).then_inc(S["a_oT"], 1)

                        for k in range(GROUPS * STEPS):
                            if k >= 2:
                                act.wait_ge(S["a_pv"], k - 1)
                            for h in range(GH):
                                act.wait_ge(S["a_scores"], 4 * k + h + 1)
                                act.activation(prob[k % 2][:, h, :], ps[:, h % 2, :], ACT.Exp).then_inc(S["a_exp"], 1)
                                if h == 1 and k > NT and k % NT == 1:
                                    copy_out(k // NT - 1)
                        copy_out(2 * GROUPS - 1)

                    @block.vector
                    def _(dve):
                        ch = Chain(dve, S["a_dve"])

                        def add_out(m):
                            g, c = divmod(m, 2)
                            turned = ps[:, 7, :].rearrange("p (n h d) -> p n h d", n=4, h=GH)
                            dve.wait_ge(S["a_turned"], m + 1)
                            ch.link(dve.reciprocal(recip[:], turned[:, :, :, HD]))
                            dve.tensor_tensor(
                                head_out[:].rearrange("p n (h d) -> p (n h) d", d=HD),
                                ps[:, 7, :].rearrange("p (a d) -> p a d", d=QUAD)[:, :, 0:HD],
                                recip[:].rearrange("p n h -> p (n h)").unsqueeze(2).to_broadcast([P, 4 * GH, HD]),
                                ALU.mult).then_inc(S["a_free7"], 1)
                            dve.wait_ge(S["a_free7"], order["out", m] + 1)
                            dst = x_all[:, bass.ds(b * NT + 4 * c, 4), g * GH * HD:(g + 1) * GH * HD]
                            ch.link(dve.tensor_tensor(dst, dst, head_out[:], ALU.add))

                        for k in range(GROUPS * STEPS):
                            g, s = divmod(k, STEPS)
                            for i, u, row in asked_for(k):
                                reduce_max(dve, row_max[u % 2], row, i)
                            if s == STEPS - 3 and g < to_negate:
                                dve.wait_ge(S["a_rowT"], g + 1)
                                if g:
                                    dve.wait_ge(S["a_negrows"], 48 * g)
                                dve.tensor_scalar(neg[:], ps[0:ROWS, 7, 0:P], -1.0, None, ALU.mult) \
                                    .then_inc(S["a_free7"], 1)
                                dve.wait_ge(S["a_free7"], order["max", g] + 1)
                                split_neg(dve, ch)
                            if k % NT == 4 and k > NT:
                                add_out((k - 4) // NT - 1)
                        add_out(2 * GROUPS - 1)

                    @block.sync
                    def _(sp):
                        load_unit(sp, b, GROUPS - 1)
                        for g in range(GROUPS):
                            if g < to_negate:
                                store_neg(sp, (g + 1) % GROUPS, g + 1)
                            if not last_batch and g < GROUPS - 1:
                                sp.wait_ge(S["a_pv"], STEPS * (g + 1))
                                load_unit(sp, b + 1, g)
                        sp.wait_ge(S["a_negrows"], 48 * to_negate)
                        for g in range(GROUPS):
                            if g == GROUPS - 1 or not last_batch:
                                sp.wait_ge(S[f"a_load{g}"], LOADED)
                S.end()

            with nc.Fori(0, B - 1) as b:
                attention(b, False)
            attention(B - 1, True)

        EG = 4
        NG = E0 // EG
        TOP_GROUPS, TOP = 2, 4
        assert FEATS % P == 0
        with ExitStack() as own:
            gate_w = [sb(f"gate_w{i}", [P, ALL], F32R, stack=own) for i in range(2)]
            up_w = [sb(f"up_w{i}", [P, ALL], F32R, stack=own) for i in range(2)]
            down_w = [sb(f"down_w{i}", [P, FT, P], F32R, stack=own) for i in range(2)]
            c_next = sb("c_next", [3 * 32, T], BF16, stack=own)

            pieces = [(raw[:], high[:], low[:]) for raw, (high, low) in ((gate_raw, gate_w), (up_raw, up_w))]
            pieces.append([w[:, 0:full, :] for w in (down_raw, *down_w)])
            if full < FT:
                pieces.append([w[0:rows_of[-1], full, :] for w in (down_raw, *down_w)])

            scores = sb("scores", [P, NT, E0], stack=own)
            biased = sb("biased", [P, NT, E0], stack=own)
            pair_max = sb("pair_max", [P, NT * NG, 2], stack=own)
            pair_sum = sb("pair_sum", [P, NT * NG, 2], stack=own)
            top_a = sb("top_a", [P, NT * NG], stack=own)
            top_b = sb("top_b", [P, NT * NG], stack=own)
            group_score = sb("group_score", [P, NT, NG], stack=own)
            ahead = sb("ahead", [P, 2, E0, E0], stack=own)
            tied = sb("tied", [P, 2, E0, E0], stack=own)
            rank = sb("rank", [P, NT, E0], stack=own)
            chosen = sb("chosen", [P, NT, E0], stack=own)
            masked = sb("masked", [P, NT, E0], stack=own)
            total = sb("total", [P, NT], stack=own)
            inverse = sb("inverse", [P, NT], stack=own)
            combine = sb("combine", [P, NT, E0], stack=own)
            c_rest = sb("c_rest", [E0, T], stack=own)
            c_mid = sb("c_mid", [E0, T], BF16, stack=own)
            c_parts = sb("c_parts", [3 * 32, T], BF16, stack=own)
            h_parts = [sb(f"h_parts{i}", [P, T], F32R, stack=own) for i in range(2)]
            gb_col = sb("gb_col", [P, 1], stack=own)
            spare = [gate_raw[:, i * BANK:(i + 1) * BANK] for i in range(6)]
            gated, prod, acts = spare[0:2], spare[2:4], spare[4:6]
            act_high = [sb(f"act_high{i}", [P, BANK], F32R, stack=own) for i in range(3)]
            act_low = [sb(f"act_low{i}", [P, BANK], F32R, stack=own) for i in range(3)]
            yT = up_raw[:, 0:2 * BANK].rearrange("p (c n) -> p c n", c=2)

            TILES_ALL = 2 * FT

            def experts(b, ahead_of):
                prep, main = ahead_of is not None, b is not None
                CUT_NEXT = FT + 3
                uses = ([("rows", 0), ("rows", 1), ("logits", 0), ("weights", 0), ("weights", 1)] if prep else [])
                slots = {("rows", 0): 9, ("rows", 1): 11, ("logits", 0): 13, ("weights", 0): 2 * FT - 9, ("weights", 1): 2 * FT - 5,
                         ("out", 0): FT + 4, ("out", 1): TILES_ALL + 2}
                if main:
                    uses = sorted(uses + [("out", 0), ("out", 1)], key=lambda u: slots[u])
                before = dict(zip(uses[1:], uses))
                read_out = {"rows": "ln_hT", "logits": "scores", "weights": "c_rest", "out": "added"}
                bank7 = ps[:, 7, :]

                with nc.Block() as block:
                    @block.tensor
                    def _(pe):
                        def gate_up(i):
                            c, j = divmod(i, FT)
                            m = rows_of[j]
                            cols, tokens = slice(j * P, j * P + m), slice(c * BANK, (c + 1) * BANK)
                            h = [x[:, tokens] for x in h_parts]
                            if i == FT:
                                pe.wait_ge(S["h_low"], 1)
                            if i >= 2:
                                pe.wait_ge(S["silu"], i - 1)
                            product(pe, ps[0:m, i % 2, :], [w[:, cols] for w in gate_w], h).then_inc(S["gate"], 1)
                            if i >= 2:
                                pe.wait_ge(S["act"], i - 1)
                            last = product(pe, ps[0:m, 2 + i % 2, :], [w[:, cols] for w in up_w], h)
                            if j < ROUTED:
                                if i == 0:
                                    pe.wait_ge(S["c_parts"], 1)
                                last = pe.matmul(ps[:, 4 + i % 2, :], owner[:, j * P:(j + 1) * P], c_parts[:, tokens],
                                                 start=True, stop=True)
                            last.then_inc(S["up"], 1)

                        def down(i):
                            c, j = divmod(i, FT)
                            m = rows_of[j]
                            pe.wait_ge(S["low"], i + 1)
                            if j == 0 and c:
                                pe.wait_ge(S["yT"], c)
                            product(pe, ps[:, 6, :], [w[0:m, j, :] for w in down_w],
                                    (act_high[i % 3][0:m, :], act_low[i % 3][0:m, :]),
                                    start=(j == 0), stop=(j == FT - 1)).then_inc(S["down"], 1)

                        def use_bank7(use):
                            what, c = use
                            if use in before:
                                pe.wait_ge(S[read_out[before[use][0]]], before[use][1] + 1)
                            if what == "out":
                                pe.wait_ge(S["yT"], c + 1)
                            if what == "logits":
                                pe.wait_ge(S["ln_hT"], 2)
                                for n in range(NT):
                                    last = pe.matmul(ps[:, 7, n * E0:(n + 1) * E0], hT[:, n * P:(n + 1) * P], router[:],
                                                     start=True, stop=True)
                                last.then_inc(S["logits"], 1)
                                return
                            if what == "weights":
                                pe.wait_ge(S["combine"], 1)
                            for n in range(4):
                                cols = slice(n * P, (n + 1) * P)
                                if what == "rows":
                                    pe.wait_ge(S["ln_xn"], 4 * c + n + 1)
                                    last = pe.transpose(ps[:, 7, cols], xn[:, 4 * c + n, :], ident[:])
                                if what == "weights":
                                    last = pe.transpose(ps[0:E0, 7, cols], combine[:, 4 * c + n, :], ident[:])
                                if what == "out":
                                    last = pe.transpose(ps[:, 7, cols], yT[:, c, cols], ident[:])
                            last.then_inc(S[{"rows": "ln_xT", "weights": "cT", "out": "turned"}[what]], 1)

                        for i in range(TILES_ALL + 3):
                            if main and i < TILES_ALL:
                                gate_up(i)
                            if main and 2 <= i < TILES_ALL + 2:
                                down(i - 2)
                            for use in uses:
                                if slots[use] == i:
                                    use_bank7(use)

                    def at(i, *what):
                        return [u for u in uses if u[0] in what and slots[u] == i]

                    @block.scalar
                    def _(act):
                        def rows_high(c):
                            cols = slice(c * BANK, (c + 1) * BANK)
                            act.activation(h_parts[0][:, cols], hT[:, cols], ACT.Copy).then_inc(S["h_high"], 1)

                        def weights_high(some):
                            for raw, high, _ in some:
                                act.activation(high, raw, ACT.Copy).then_inc(S["w_high"], 1)

                        if main:
                            rows_high(1)
                        else:
                            weights_high(pieces[:1])
                        for i in range(TILES_ALL + 4):
                            if main and i < TILES_ALL:
                                m = rows_of[i % FT]
                                act.wait_ge(S["gate"], i + 1)
                                if i >= 2:
                                    act.wait_ge(S["act"], i - 1)
                                act.activation(gated[i % 2][0:m, :], ps[0:m, i % 2, :], ACT.Silu).then_inc(S["silu"], 1)
                            if main and 1 <= i <= TILES_ALL:
                                m = rows_of[(i - 1) % FT]
                                act.wait_ge(S["act"], i)
                                if i >= 4:
                                    act.wait_ge(S["down"], i - 3)
                                act.activation(act_high[(i - 1) % 3][0:m, :], acts[(i - 1) % 2][0:m, :], ACT.Copy) \
                                    .then_inc(S["high"], 1)
                            if prep and i == 4:
                                act.wait_ge(S["ln_var"], 1)
                                act.activation(ln[:, 1, :], ln[:, 0, :], ACT.Sqrt).then_inc(S["ln_std"], 1)
                            for what, c in at(i, "rows"):
                                act.wait_ge(S["ln_xT"], c + 1)
                                if main:
                                    act.wait_ge(S["h_low"], 1)
                                act.activation(hT[:, c * BANK:(c + 1) * BANK], bank7, ACT.Identity, bias=cur_cols[:, 3:4],
                                               scale=cur_cols[:, 4:5]).then_inc(S["ln_hT"], 1)
                            if prep and i == CUT_NEXT:
                                act.wait_ge(S["ln_hT"], 1)
                                if main:
                                    act.wait_ge(S["up"], FT)
                                rows_high(0)
                            for _ in at(i, "logits"):
                                act.wait_ge(S["logits"], 1)
                                act.activation(scores[:].rearrange("p n e -> p (n e)"), ps[:, 7, 0:NT * E0], ACT.Sigmoid) \
                                    .then_inc(S["scores"], 1)
                            if main and i == FT + 1 or main and i == TILES_ALL + 1:
                                c = i // TILES_ALL
                                act.wait_ge(S["down"], FT * (c + 1))
                                act.activation(yT[:, c, :], ps[:, 6, :], ACT.Copy, scale=gb_col[:]).then_inc(S["yT"], 1)
                            if not main and i == slots["logits", 0]:
                                weights_high(pieces[1:])

                    @block.gpsimd
                    def _(pool):
                        def rows_low(c, count):
                            cols = slice(c * BANK, (c + 1) * BANK)
                            pool.wait_ge(S["h_high"], count)
                            minus_high(pool, h_parts[1][:, cols], hT[:, cols], h_parts[0][:, cols]).then_inc(S["h_low"], 1)

                        if main:
                            rows_low(1, 1)
                        else:
                            pool.memset(c_next[:], 0.0).then_inc(S["c_parts"], 1)
                        for i in range(TILES_ALL):
                            if prep and i == CUT_NEXT:
                                rows_low(0, 2 if main else 1)
                            if main:
                                m = rows_of[i % FT]
                                pool.wait_ge(S["high"], i + 1)
                                minus_high(pool, act_low[i % 3][0:m, :], acts[i % 2][0:m, :], act_high[i % 3][0:m, :]) \
                                    .then_inc(S["low"], 1)
                        if not main:
                            for n, (raw, high, low) in enumerate(pieces):
                                pool.wait_ge(S["w_high"], n + 1)
                                minus_high(pool, low, raw, high).then_inc(S["w_low"], 1)

                    @block.vector
                    def _(dve):
                        ch = Chain(dve, S["dve"])
                        tt, link = dve.tensor_tensor, ch.link

                        def rank_of(out, v, count):
                            for some in (slice(n, n + 2) for n in range(0, NT, 2)):
                                a, q = ahead[:, :, 0:count, 0:count], tied[:, :, 0:count, 0:count]
                                shape4 = [P, 2, count, count]
                                other = v[:, some].unsqueeze(2).to_broadcast(shape4)
                                mine = v[:, some].unsqueeze(3).to_broadcast(shape4)
                                yield ch.did(tt(a, other, mine, ALU.is_gt))
                                yield link(tt(q, other, mine, ALU.is_equal))
                                yield link(tt(q, q, below[:, 0:count, 0:count].unsqueeze(1).to_broadcast(shape4), ALU.mult))
                                yield link(tt(a, a, q, ALU.add))
                                yield link(dve.tensor_reduce(out[:, some], a, axis=AX, op=ALU.add))

                        def routes():
                            dve.wait_ge(S["scores"], 1)
                            link(tt(biased[:], scores[:], bias[:].unsqueeze(1).to_broadcast([P, NT, E0]), ALU.add))
                            v = biased[:].rearrange("p n (g w v) -> p (n g) w v", g=NG, v=2)
                            ch.did(tt(pair_max[:], v[:, :, :, 0], v[:, :, :, 1], ALU.max))
                            yield link(tt(pair_sum[:], v[:, :, :, 0], v[:, :, :, 1], ALU.add))
                            ch.did(tt(top_a[:], pair_max[:, :, 0], pair_max[:, :, 1], ALU.add))
                            link(tt(top_b[:], pair_sum[:, :, 0], pair_sum[:, :, 1], ALU.max))
                            yield link(tt(group_score[:].rearrange("p n g -> p (n g)"), top_a[:], top_b[:], ALU.max))
                            for _ in rank_of(rank[:, :, 0:NG], group_score[:], NG):
                                pass
                            link(dve.tensor_scalar(chosen[:, :, 0:NG], rank[:, :, 0:NG], float(TOP_GROUPS), None, ALU.is_lt))
                            yield link(tt(masked[:].rearrange("p n (g w) -> p n g w", g=NG),
                                          biased[:].rearrange("p n (g w) -> p n g w", g=NG),
                                          chosen[:, :, 0:NG].unsqueeze(3).to_broadcast([P, NT, NG, EG]), ALU.mult))
                            yield from rank_of(rank[:], masked[:], E0)
                            link(dve.tensor_scalar(chosen[:], rank[:], float(TOP), None, ALU.is_lt))
                            yield link(tt(masked[:], scores[:], chosen[:], ALU.mult))
                            link(dve.tensor_reduce(total[:], masked[:], axis=AX, op=ALU.add))
                            yield link(dve.tensor_scalar(total[:], total[:], 1e-20, None, ALU.add))
                            link(dve.reciprocal(inverse[:], total[:]))
                            tt(combine[:], masked[:], inverse[:].unsqueeze(2).to_broadcast([P, NT, E0]), ALU.mult) \
                                .then_inc(S["combine"], 1)

                        def cut_weights():
                            if not main:
                                dve.wait_ge(S["c_parts"], 1)
                            for c in range(2):
                                cols = slice(c * BANK, (c + 1) * BANK)
                                dve.wait_ge(S["cT"], c + 1)
                                yield link(dve.tensor_copy(c_next[0:E0, cols], ps[0:E0, 7, :]))
                                yield tt(c_rest[:, cols], ps[0:E0, 7, :], c_next[0:E0, cols], ALU.subtract) \
                                    .then_inc(S["c_rest"], 1)
                                dve.wait_ge(S["c_rest"], c + 1)
                                yield link(dve.tensor_copy(c_mid[:, cols], c_rest[:, cols]))
                                ch.did(dve.tensor_copy(c_next[32:32 + E0, cols], c_mid[:, cols]))
                                yield ch.did(tt(c_next[64:64 + E0, cols], c_rest[:, cols], c_mid[:, cols], ALU.subtract))

                        def add_y(c):
                            dve.wait_ge(S["turned"], c + 1)
                            dst = x_all[:, bass.ds(b * NT + 4 * c, 4), :]
                            tt(dst, dst, ps[:, 7, :].rearrange("p (n d) -> p n d", d=P), ALU.add).then_inc(S["added"], 1)

                        if main:
                            dve.tensor_copy(c_parts[:], c_next[:]).then_inc(S["c_parts"], 1)
                            dve.wait_ge(S["c_parts"], 1)
                            link(dve.tensor_copy(gb_col[:], cur_cols[:, 5:6]))
                        normed = norm_steps(dve, S, ahead_of, 0) if prep else iter(())
                        routed_steps = routes() if prep else iter(())
                        weight_steps = cut_weights() if prep else iter(())
                        if not main:
                            for _ in normed:
                                pass
                        routed = 0
                        for i in range(TILES_ALL + 4):
                            if main and i < TILES_ALL:
                                j = i % FT
                                m = rows_of[j]
                                dve.wait_ge(S["silu"], i + 1)
                                dve.wait_ge(S["up"], i + 1)
                                if i >= 2:
                                    dve.wait_ge(S["low"], i - 1)
                                if j < ROUTED:
                                    tt(prod[i % 2][:], gated[i % 2][:], ps[:, 2 + i % 2, :], ALU.mult).then_inc(S["prod"], 1)
                                    routed += 1
                                    dve.wait_ge(S["prod"], routed)
                                    tt(acts[i % 2][:], prod[i % 2][:], ps[:, 4 + i % 2, :], ALU.mult).then_inc(S["act"], 1)
                                else:
                                    tt(acts[i % 2][0:m, :], gated[i % 2][0:m, :], ps[0:m, 2 + i % 2, :], ALU.mult) \
                                        .then_inc(S["act"], 1)
                            next(normed, None)
                            if i > slots["logits", 0]:
                                next(routed_steps, None)
                            if i == slots["weights", 0]:
                                for _ in routed_steps:
                                    pass
                            if slots["weights", 0] <= i:
                                next(weight_steps, None)
                            for what, c in at(i - 1, "out"):
                                add_y(c)
                S.end()

            S = batch_phase("ffn", "h_high", "h_low", "gate", "up", "silu", "prod", "act", "high", "low", "down", "yT",
                            "turned", "added", "logits", "scores", "combine", "cT", "c_rest", "c_parts", "w_high", "w_low", "dve")
            experts(None, 0)
            with nc.Fori(0, B - 1) as b:
                experts(b, b + 1)
            experts(B - 1, None)

        ffn_own.close()

        HT = HID // P
        CHOICES = K * TILES
        assert ROOM == T and CHOICES * E1 == BANK
        outs_dram = nc.dram_tensor("slot_outs", [SLOTS, P], F32, kind="Internal").ap()
        with ExitStack() as own:
            gates = sb("gates", [P, K, TILES], stack=own)
            from_slot = sb("from_slot", [P, CHOICES], U32, stack=own)

            with ExitStack() as inner:
                qT = sb("qT", [P, T], stack=inner)
                qT_end = sb("qT_end", [P, T], stack=inner)
                h_start = sb("h_start", [P, NT, P], stack=inner)
                gate_row = sb("gate_row", [P, P], stack=inner)
                vals = sb("vals", [P, NT, P], stack=inner)
                near = sb("near", [P, NT, P], stack=inner)
                state = sb("state", [P, NT, P], stack=inner)
                shift_row = sb("shift_row", [P, P], stack=inner)
                second = NormBuffers("ln2", cols=sb("cols2", [P, 6], stack=inner), xb=sb("xb2", [P, NT, P], stack=inner),
                                     xn=sb("xn2", [P, NT, P], stack=inner), hT=sb("hT2", [P, T], stack=inner),
                                     stats=sb("stats2", [P, NT, 6], stack=inner), mv=sb("mv2", [P, NT, 2], stack=inner),
                                     ln=sb("ln2", [P, 8, NT], stack=inner))

                def small(name, *shp, dt=F32):
                    return sb(name, [P, *shp], dt, stack=inner)

                router1 = small("router1", E1)
                h_rows = small("h_rows", TILES, P)
                h_now = small("h_now", NT, P)
                to_slot_now = small("to_slot_now", NT, dt=U32)
                logit = small("logit", TILES, E1)
                before32 = small("before32", P)
                before = small("before", P, dt=BF16)
                ones = small("ones", P, dt=BF16)
                expert_id = small("expert_id", E1)
                priority = small("priority", E1)
                spill = small("spill", CHOICES)
                scan_ones = small("scan_ones", TILES)
                taken = small("taken", E1)
                best = small("best", K, TILES)
                match = small("match", TILES, E1)
                lowest = small("lowest", TILES)
                choice = small("choice", K, TILES, E1)
                choice_bf = small("choice_bf", TILES, E1, dt=BF16)
                counts = small("counts", 2, NT, E1)
                others = small("others", TILES, E1)
                ratio = small("ratio", TILES)
                through = small("through", TILES, E1)
                place = small("place", TILES, E1)
                loc = small("loc", TILES)
                expert = small("expert", TILES)
                valid = small("valid", CHOICES)
                target = small("target", TILES)
                clipped = small("clipped", TILES)
                to_slot = small("to_slot", TILES, dt=U32)

                def choose(ch, n, source, largest, chosen):
                    tt, link = ch.eng.tensor_tensor, ch.link
                    link(ch.eng.tensor_reduce(largest, source, axis=AX, op=ALU.max))
                    link(tt(match[:, 0:n], source, largest.unsqueeze(2).to_broadcast([P, n, E1]), ALU.is_equal))
                    link(tt(match[:, 0:n], match[:, 0:n], priority[:].unsqueeze(1).to_broadcast([P, n, E1]), ALU.mult))
                    link(ch.eng.tensor_reduce(lowest[:, 0:n], match[:, 0:n], axis=AX, op=ALU.max))
                    link(tt(chosen, match[:, 0:n], lowest[:, 0:n].unsqueeze(2).to_broadcast([P, n, E1]), ALU.is_equal))

                def put(ch, n, chosen, earlier, totals, columns, targets):
                    tt, ts, link = ch.eng.tensor_tensor, ch.eng.tensor_scalar, ch.link
                    for e in range(E1):
                        ch.did(ch.eng.tensor_tensor_scan(through[:, 0:n, e], scan_ones[:, 0:n], totals[:, :, e], 0.0,
                                                         ALU.mult, ALU.add))
                    ch.wait()
                    link(tt(place[:, 0:n], through[:, 0:n], totals, ALU.subtract))
                    link(tt(place[:, 0:n], place[:, 0:n], earlier, ALU.add))
                    link(tt(place[:, 0:n], place[:, 0:n], taken[:].unsqueeze(1).to_broadcast([P, n, E1]), ALU.add))
                    link(tt(taken[:], taken[:], through[:, n - 1], ALU.add))
                    link(tt(place[:, 0:n], place[:, 0:n], chosen, ALU.mult))
                    link(ch.eng.tensor_reduce(loc[:, 0:n], place[:, 0:n], axis=AX, op=ALU.add))
                    link(tt(place[:, 0:n], chosen, expert_id[:].unsqueeze(1).to_broadcast([P, n, E1]), ALU.mult))
                    link(ch.eng.tensor_reduce(expert[:, 0:n], place[:, 0:n], axis=AX, op=ALU.add))
                    link(ts(valid[:, columns], loc[:, 0:n], float(ROOM), None, ALU.is_lt))
                    link(ts(clipped[:, 0:n], loc[:, 0:n], float(ROOM - 1), None, ALU.min))
                    link(ch.eng.scalar_tensor_tensor(clipped[:, 0:n], expert[:, 0:n], float(ROOM), clipped[:, 0:n],
                                                     ALU.mult, ALU.add))
                    ch.did(ch.eng.tensor_copy(from_slot[:, columns], clipped[:, 0:n]))
                    link(ts(target[:, 0:n], spill[:, columns], float(SLOTS), None, ALU.add))
                    link(tt(clipped[:, 0:n], clipped[:, 0:n], target[:, 0:n], ALU.subtract))
                    link(tt(clipped[:, 0:n], clipped[:, 0:n], valid[:, columns], ALU.mult))
                    link(tt(clipped[:, 0:n], clipped[:, 0:n], target[:, 0:n], ALU.add))
                    return ch.eng.tensor_copy(targets, clipped[:, 0:n])

                S = batch_phase("lin", *[f"ln2_{n[3:]}" for n in LN], "qT", "qT_sb", "dve", "vals", "vals_sb", "near", "near_sb",
                                "pairs", "states", "y", "in", "logits", "chosen", "counts", "h_now", "h_kept", "placed")
                rows_sent = ctx.enter_context(nc.semaphore("rows_sent"))

                def send(pool, source, targets, n):
                    pool.indirect_dma_start(slots_dram, bass.IndirectOffsetOnAxis(ap=targets[:, n:n + 1], axis=0),
                                            source[:, n, :], None).then_inc(rows_sent, 16)

                def place_first(ch, p):
                    tiles = bass.ds(p * NT, NT)
                    return put(ch, NT, choice[:, 0, tiles, :], counts[:, 0], counts[:, 1], tiles, to_slot_now[:])

                def linear(b, m, p):
                    with nc.Block() as block:
                        @block.tensor
                        def _(pe):
                            if b is not None:
                                norm_tensor(pe, S)
                                pe.wait_ge(S["ln_hT"], 1)
                                for c in range(2):
                                    last = pe.matmul(ps[:, 2 + c, :], qk_w[:], hT[:, c * BANK:(c + 1) * BANK], start=True, stop=True)
                                last.then_inc(S["qT"], 1)
                                for n in range(NT):
                                    last = pe.matmul(ps[:, 6 + n // 4, (n % 4) * P:(n % 4 + 1) * P], hT[:, n * P:(n + 1) * P], vo_w[:],
                                                     start=True, stop=True)
                                last.then_inc(S["vals"], 1)
                                pe.wait_ge(S["qT_sb"], 1)
                                for n in range(NT):
                                    cols = slice(n * P, (n + 1) * P)
                                    last = pe.matmul(ps[:, 4 + n // 4, (n % 4) * P:(n % 4 + 1) * P], hT[:, cols], qT[:, cols],
                                                     start=True, stop=True)
                                last.then_inc(S["near"], 1)
                                pe.wait_ge(S["vals_sb"], 1)
                                for n in range(NT):
                                    last = pe.matmul(ps[:, n // 4, (n % 4) * P:(n % 4 + 1) * P], h_start[:, n, :], vals[:, n, :],
                                                     start=True, stop=True)
                                last.then_inc(S["pairs"], 1)
                            if b is not None:
                                pe.wait_ge(S["near_sb"], 1)
                                pe.wait_ge(S["states"], 1)
                                for n in range(NT):
                                    out = ps[:, 2 + n // 4, (n % 4) * P:(n % 4 + 1) * P]
                                    last = pe.matmul(out, near[:, n, :], vals[:, n, :], start=True, stop=(n == NT - 1))
                                    if n < NT - 1:
                                        last = pe.matmul(out, qT_end[:, n * P:(n + 1) * P], state[:, n, :], start=False, stop=True)
                                last.then_inc(S["y"], 1)
                            if m is not None:
                                norm_tensor(pe, S, second, 6)
                                pe.wait_ge(S["ln2_hT"], 1)
                                for n in range(NT):
                                    last = pe.matmul(ps[:, 4, n * E1:(n + 1) * E1], second.hT[:, n * P:(n + 1) * P], router1[:],
                                                     start=True, stop=True)
                                last.then_inc(S["logits"], 1)
                                pe.wait_ge(S["chosen"], 1)
                                flat = choice_bf[:, 0:NT].rearrange("p n e -> p (n e)")
                                pe.matmul(ps[:, 5, 0:NT * E1], before[:], flat, start=True, stop=True)
                                pe.matmul(ps[:, 5, NT * E1:2 * NT * E1], ones[:], flat, start=True, stop=True).then_inc(S["counts"], 1)

                        @block.scalar
                        def _(act):
                            if b is not None:
                                norm_scalar(act, S, 0, 1)
                                act.wait_ge(S["qT"], 1)
                                act.activation(qT[:], ps[:, 2:4, :].rearrange("p a n -> p (a n)"), ACT.Copy).then_inc(S["qT_sb"], 1)
                            if m is not None:
                                norm_scalar(act, S, 3, 4, second, 6)
                                act.wait_ge(S["h_now"], 1)
                                act.activation(h_rows[:, bass.ds(m * NT, NT), :], h_now[:], ACT.Copy).then_inc(S["h_kept"], 1)

                        @block.vector
                        def _(dve):
                            ch = Chain(dve, S["dve"])
                            tt, link = dve.tensor_tensor, ch.link
                            row = lambda i, v: mod1_rows[:].rearrange("p b v d -> p (b v) d")[:, bass.ds(i * 6 + v, 1), :]
                            all_tiles = lambda ap: ap.to_broadcast([P, NT, P])
                            wide = lambda first: ps[:, first:first + 2, :].rearrange("p a (n d) -> p (a n) d", d=P)

                            def some(steps, count=NT + 8):
                                for _ in range(count):
                                    next(steps, None)

                            norm2 = norm_steps(dve, S, m, 1, second) if m is not None else iter(())
                            if b is not None:
                                norm1 = norm_steps(dve, S, b, 1)
                                some(norm1, 4)
                                some(norm2, 3)
                                some(norm1)
                                dve.wait_ge(S["ln_xn"], NT)
                                ch.did(dve.tensor_scalar(gate_row[:].unsqueeze(1), row(b, 2), out_scale[:], None, ALU.mult))
                                ch.did(dve.tensor_scalar(shift_row[:].unsqueeze(1), row(b, 0), start_powers[:], None, ALU.mult))
                                link(dve.scalar_tensor_tensor(h_start[:], xn[:], start_powers[:], all_tiles(row(b, 1)), ALU.mult, ALU.mult))
                                link(tt(h_start[:], h_start[:], all_tiles(shift_row[:].unsqueeze(1)), ALU.add))
                                if p is not None:
                                    place_first(ch, p).then_inc(S["placed"], 1)
                                dve.wait_ge(S["vals"], 1)
                                tt(vals[:], wide(6), all_tiles(gate_row[:].unsqueeze(1)), ALU.mult).then_inc(S["vals_sb"], 1)
                                some(norm2, 1)
                                dve.wait_ge(S["qT_sb"], 1)
                                link(tt(qT_end[:].rearrange("p (n q) -> p n q", q=P), qT[:].rearrange("p (n q) -> p n q", q=P),
                                        all_tiles(end_powers[:].unsqueeze(1)), ALU.mult))
                                dve.wait_ge(S["near"], 1)
                                tt(near[:], wide(4), all_tiles(mask[:].unsqueeze(1)), ALU.mult).then_inc(S["near_sb"], 1)
                                dve.wait_ge(S["pairs"], 1)
                                pair = lambda n: ps[:, n // 4, (n % 4) * P:(n % 4 + 1) * P]
                                link(dve.tensor_copy(state[:, NT - 2, :], pair(NT - 1)))
                                for n in range(NT - 2, 0, -1):
                                    ins = dve.scalar_tensor_tensor(state[:, n - 1, :], state[:, n, :], chunk_power[:], pair(n),
                                                                   ALU.mult, ALU.add)
                                    if n > 1:
                                        link(ins)
                                ins.then_inc(S["states"], 1)
                            elif p is not None:
                                place_first(ch, p).then_inc(S["placed"], 1)
                            some(norm2)
                            if m is not None:
                                dve.wait_ge(S["ln2_xn"], NT)
                                if p is not None:
                                    dve.wait_ge(rows_sent, (p + 1) * (16 * NT))
                                link(tt(h_now[:], second.xn[:], all_tiles(row(m, 4)), ALU.mult))
                                tt(h_now[:], h_now[:], all_tiles(row(m, 3)), ALU.add).then_inc(S["h_now"], 1)
                            if b is not None:
                                dve.wait_ge(S["y"], 1)
                                dst = x_all[:, bass.ds(b * NT, NT), :]
                                link(tt(dst, dst, wide(2), ALU.add))
                            if m is None:
                                ch.did(dve.memset(ones[:], 1.0))
                                ch.did(dve.memset(scan_ones[:], 1.0))
                                ch.did(dve.memset(taken[:], 0.0))
                                dve.wait_ge(S["in"], 64)
                                ch.did(dve.tensor_copy(before[:], before32[:]))
                                ch.did(dve.tensor_scalar(priority[:], expert_id[:], -1.0, float(E1), ALU.mult, ALU.add))
                            else:
                                tiles = bass.ds(m * NT, NT)
                                dve.wait_ge(S["logits"], 1)
                                link(dve.tensor_copy(logit[:, tiles, :], ps[:, 4, 0:NT * E1].rearrange("p (n e) -> p n e", e=E1)))
                                choose(ch, NT, logit[:, tiles, :], best[:, 0, tiles], choice[:, 0, tiles, :])
                                dve.tensor_copy(choice_bf[:, 0:NT], choice[:, 0, tiles, :]).then_inc(S["chosen"], 1)
                                dve.wait_ge(S["counts"], 1)
                                ch.did(dve.tensor_copy(counts[:].rearrange("p k n e -> p (k n e)"), ps[:, 5, 0:2 * NT * E1]))

                        @block.sync
                        def _(sp):
                            if m is None:
                                for dst, n in ((router1, "router1"), (before32, "before"), (expert_id, "expert_id"), (spill, "spill")):
                                    sp.dma_start(dst[:], t[n]).then_inc(S["in"], 16)
                                sp.wait_ge(S["in"], 64)

                        @block.gpsimd
                        def _(pool):
                            if p is not None:
                                pool.wait_ge(S["placed"], 1)
                                for n in range(NT):
                                    send(pool, h_now, to_slot_now, n)
                                pool.wait_ge(rows_sent, (p + 1) * (16 * NT))
                    S.end()

                linear(0, None, None)
                linear(1, 0, None)
                with nc.Fori(2, B) as b:
                    linear(b, b - 1, b - 2)
                linear(None, B - 1, B - 2)

                S = phase("t_dve", "t_ratio", "t_exp", "t_chosen", "t_counts", "t_first", "t_placed")
                with nc.Block() as block:
                    @block.vector
                    def _(dve):
                        ch = Chain(dve, S["t_dve"])
                        tt, link = dve.tensor_tensor, ch.link
                        place_first(ch, B - 1).then_inc(S["t_first"], 1)
                        dve.wait_ge(S["t_first"], 1)
                        link(dve.scalar_tensor_tensor(others[:].rearrange("p n e -> p (n e)"),
                                                      choice[:, 0].rearrange("p n e -> p (n e)"), -1e30,
                                                      logit[:].rearrange("p n e -> p (n e)"), ALU.mult, ALU.add))
                        choose(ch, TILES, others[:], best[:, 1, :], choice[:, 1])
                        dve.tensor_copy(choice_bf[:], choice[:, 1]).then_inc(S["t_chosen"], 1)
                        tt(ratio[:], best[:, 1, :], best[:, 0, :], ALU.subtract).then_inc(S["t_ratio"], 1)
                        dve.wait_ge(S["t_counts"], 1)
                        in_tile = lambda bank: ps[:, bank, 0:TILES * E1].rearrange("p (n e) -> p n e", e=E1)
                        put(ch, TILES, choice[:, 1], in_tile(0), in_tile(1), slice(TILES, CHOICES), to_slot[:]) \
                            .then_inc(S["t_placed"], 1)
                        dve.wait_ge(S["t_exp"], 1)
                        link(dve.tensor_scalar(lowest[:], ratio[:], 1.0, None, ALU.add))
                        link(dve.reciprocal(gates[:, 0, :], lowest[:]))
                        link(tt(gates[:, 1, :], gates[:, 0, :], ratio[:], ALU.mult))
                        link(tt(gates[:].rearrange("p k n -> p (k n)"), gates[:].rearrange("p k n -> p (k n)"), valid[:], ALU.mult))

                    @block.scalar
                    def _(act):
                        act.wait_ge(S["t_ratio"], 1)
                        act.activation(ratio[:], ratio[:], ACT.Exp).then_inc(S["t_exp"], 1)

                    @block.tensor
                    def _(pe):
                        pe.wait_ge(S["t_chosen"], 1)
                        flat = choice_bf[:].rearrange("p n e -> p (n e)")
                        pe.matmul(ps[:, 0, 0:TILES * E1], before[:], flat, start=True, stop=True)
                        pe.matmul(ps[:, 1, 0:TILES * E1], ones[:], flat, start=True, stop=True).then_inc(S["t_counts"], 1)

                    @block.gpsimd
                    def _(pool):
                        pool.wait_ge(S["t_first"], 1)
                        for n in range(NT):
                            send(pool, h_now, to_slot_now, n)
                        pool.wait_ge(S["t_placed"], 1)
                        for n in range(TILES):
                            send(pool, h_rows, to_slot, n)
                        pool.wait_ge(rows_sent, 16 * CHOICES)
                S.end()

            w_raw = [sb(f"w_raw{i}", [P, 2, HID], stack=own) for i in range(2)]
            slots_raw = [sb(f"slots_raw{i}", [P, ST, P], stack=own) for i in range(2)]
            w_parts = [[sb(f"w_parts{i}{h}", [P, 2, HID], F32R, stack=own) for h in range(2)] for i in range(2)]
            slotsT = [[sb(f"slotsT{i}{h}", [P, ROOM], F32R, stack=own) for h in range(2)] for i in range(2)]
            hid = sb("hid", [P, HT, ROOM], stack=own)
            hid_parts = [sb(f"hid_parts{h}", [P, HT, ROOM], F32R, stack=own) for h in range(2)]
            outT = [sb(f"outT{i}", [P, ROOM], stack=own) for i in range(2)]
            slot_out = [sb(f"slot_out{i}", [P, ST, P], stack=own) for i in range(2)]
            b1 = sb("b1", [P, E1, HT], stack=own)
            b2 = sb("b2", [P, E1], stack=own)
            cur_b1 = [sb(f"cur_b1_{i}", [P, HT], stack=own) for i in range(2)]
            cur_b2 = [sb(f"cur_b2_{i}", [P, 1], stack=own) for i in range(2)]
            turned_ps = ps[:, 0:2, :].rearrange("p a n -> p (a n)")

            def load_expert(sp, e, i, sem):
                sp.dma_start(w_raw[i][:, 0, :], t["w1"][e]).then_inc(sem, 16)
                sp.dma_start(w_raw[i][:, 1, :].rearrange("p (j d) -> p j d", d=P), t["w2"][e].rearrange("(j p) d -> p j d", p=P)) \
                    .then_inc(sem, 16)
                sp.dma_start(slots_raw[i][:], slots_dram[bass.ds(e * ROOM, ROOM)].rearrange("(n p) d -> p n d", p=P)) \
                    .then_inc(sem, 16)

            def turn(pe, tiles):
                for n, tile in enumerate(tiles):
                    last = pe.transpose(ps[:, n // 4, (n % 4) * P:(n % 4 + 1) * P], tile, ident[:])
                return last

            E_SEMS = ("in1", "in0", "bias", "slots_turned", "out_turned", "w_high", "w_low", "slots_high", "slots_low",
                      "hid_ps", "hid_high", "hid", "low_even", "low_odd", "out_ps", "outT", "out_copied", "stored")
            S = phase(*[f"e_{n}" for n in E_SEMS])
            S.by_name = {n[2:]: h for n, h in S.by_name.items()}

            def low_done(i, j):
                return S[("low_even", "low_odd")[j % 2]], i * (HT // 2) + j // 2 + 1

            def cut_hidden(eng, i, j):
                eng.wait_ge(S["hid_high"], i * HT + j + 1)
                minus_high(eng, hid_parts[1][:, j, :], hid[:, j, :], hid_parts[0][:, j, :]).then_inc(low_done(i, j)[0], 1)

            def expert_pass(e0, first, last):
                with nc.Block() as block:
                    @block.sync
                    def _(sp):
                        load_expert(sp, e0 + 1, 1, S["in1"])
                        if not last:
                            load_expert(sp, e0 + 2, 0, S["in0"])
                        stores = ([(e0 - 1, 1)] if not first else []) + [(e0, 0)]
                        for n, (e, i) in enumerate(stores):
                            sp.wait_ge(S["out_copied"], n + 1)
                            sp.dma_start(outs_dram[bass.ds(e * ROOM, ROOM)].rearrange("(n p) d -> p n d", p=P), slot_out[i][:]) \
                                .then_inc(S["stored"], 16)
                        sp.wait_ge(S["stored"], 16 * len(stores))

                    @block.tensor
                    def _(pe):
                        def hidden(i, j):
                            q = i * HT + j
                            if q >= 2:
                                pe.wait_ge(S["hid"], q - 1)
                            for c in range(2):
                                last_one = product(pe, ps[:, 2 + 2 * (q % 2) + c, :], [w[:, 0, j * P:(j + 1) * P] for w in w_parts[i]],
                                                   [s[:, c * BANK:(c + 1) * BANK] for s in slotsT[i]])
                            last_one.then_inc(S["hid_ps"], 1)

                        def outputs(i):
                            for j in range(HT):
                                pe.wait_ge(*low_done(i, j))
                                if i and j == 0:
                                    pe.wait_ge(S["outT"], 2)
                                for c in range(2):
                                    ins = product(pe, ps[:, 6 + c, :], [w[:, 1, j * P:(j + 1) * P] for w in w_parts[i]],
                                                  [h[:, j, c * BANK:(c + 1) * BANK] for h in hid_parts],
                                                  start=(j == 0), stop=(j == HT - 1))
                                    if j == HT - 1:
                                        ins.then_inc(S["out_ps"], 1)

                        def turn_slots(i):
                            turn(pe, [slots_raw[i][:, n, :] for n in range(ST)]).then_inc(S["slots_turned"], 1)

                        def turn_out(i):
                            turn(pe, [outT[i][:, n * P:(n + 1) * P] for n in range(ST)]).then_inc(S["out_turned"], 1)

                        before = 0 if first else 1
                        if not first:
                            turn_out(1)
                        for j in range(HT):
                            hidden(0, j)
                        pe.wait_ge(S["in1"], 48)
                        if not first:
                            pe.wait_ge(S["out_copied"], 1)
                        turn_slots(1)
                        outputs(0)
                        pe.wait_ge(S["w_low"], 1)
                        pe.wait_ge(S["slots_low"], 1)
                        hidden(1, 0)
                        hidden(1, 1)
                        pe.wait_ge(S["outT"], 2)
                        turn_out(0)
                        hidden(1, 2)
                        hidden(1, 3)
                        if not last:
                            pe.wait_ge(S["in0"], 48)
                            pe.wait_ge(S["out_copied"], before + 1)
                            turn_slots(0)
                        pe.wait_ge(S["w_low"], 2)
                        outputs(1)

                    @block.scalar
                    def _(act):
                        def hid_high(i, j):
                            q = i * HT + j
                            act.wait_ge(S["hid"], q + 1)
                            if i:
                                act.wait_ge(S["out_ps"], 2)
                            act.activation(hid_parts[0][:, j, :], hid[:, j, :], ACT.Copy).then_inc(S["hid_high"], 1)

                        def weights_high(i, w):
                            act.activation(w_parts[i][0][:, w, :], w_raw[i][:, w, :], ACT.Copy).then_inc(S["w_high"], 1)

                        def slots_high(i, count):
                            act.wait_ge(S["slots_turned"], count)
                            act.activation(slotsT[i][0][:], turned_ps, ACT.Copy).then_inc(S["slots_high"], 1)

                        def copy_out(i):
                            for c in range(2):
                                act.wait_ge(S["out_ps"], 2 * i + c + 1)
                                act.activation(outT[i][:, c * BANK:(c + 1) * BANK], ps[:, 6 + c, :], ACT.Identity, bias=cur_b2[i][:]) \
                                    .then_inc(S["outT"], 1)

                        act.wait_ge(S["bias"], 4)
                        hid_high(0, 0)
                        hid_high(0, 1)
                        act.wait_ge(S["in1"], 48)
                        weights_high(1, 0)
                        hid_high(0, 2)
                        hid_high(0, 3)
                        weights_high(1, 1)
                        slots_high(1, 1)
                        copy_out(0)
                        hid_high(1, 0)
                        hid_high(1, 1)
                        if not last:
                            act.wait_ge(S["in0"], 48)
                            weights_high(0, 0)
                        hid_high(1, 2)
                        hid_high(1, 3)
                        if not last:
                            weights_high(0, 1)
                            slots_high(0, 2)
                        copy_out(1)

                    @block.vector
                    def _(dve):
                        def hid_full(i, j):
                            q = i * HT + j
                            dve.wait_ge(S["hid_ps"], q + 1)
                            if i:
                                dve.wait_ge(*low_done(0, j))
                            dve.tensor_scalar(hid[:, j, :], ps[:, 2 + 2 * (q % 2):4 + 2 * (q % 2), :].rearrange("p a n -> p (a n)"),
                                              cur_b1[i][:, j:j + 1], 0.0, ALU.add, ALU.max).then_inc(S["hid"], 1)

                        def weights_low(i, w, count):
                            dve.wait_ge(S["w_high"], count)
                            minus_high(dve, w_parts[i][1][:, w, :], w_raw[i][:, w, :], w_parts[i][0][:, w, :]).then_inc(S["w_low"], 1)

                        def slots_low(i, count):
                            dve.wait_ge(S["slots_high"], count)
                            minus_high(dve, slotsT[i][1][:], turned_ps, slotsT[i][0][:]).then_inc(S["slots_low"], 1)

                        def copy_turned(i, count):
                            dve.wait_ge(S["out_turned"], count)
                            dve.tensor_copy(slot_out[i][:].rearrange("p n d -> p (n d)"), turned_ps).then_inc(S["out_copied"], 1)

                        for i in range(2):
                            dve.tensor_copy(cur_b1[i][:].unsqueeze(1), b1[:, bass.ds(e0 + i, 1), :]).then_inc(S["bias"], 1)
                            dve.tensor_copy(cur_b2[i][:], b2[:, bass.ds(e0 + i, 1)]).then_inc(S["bias"], 1)
                        if not first:
                            copy_turned(1, 1)
                        dve.wait_ge(S["bias"], 4)
                        hid_full(0, 0)
                        hid_full(0, 1)
                        weights_low(1, 0, 1)
                        hid_full(0, 2)
                        cut_hidden(dve, 0, 1)
                        hid_full(0, 3)
                        cut_hidden(dve, 0, 3)
                        weights_low(1, 1, 2)
                        slots_low(1, 1)
                        hid_full(1, 0)
                        hid_full(1, 1)
                        copy_turned(0, 1 if first else 2)
                        if not last:
                            weights_low(0, 0, 3)
                        hid_full(1, 2)
                        cut_hidden(dve, 1, 1)
                        hid_full(1, 3)
                        cut_hidden(dve, 1, 3)
                        if not last:
                            weights_low(0, 1, 4)
                            slots_low(0, 2)

                    @block.gpsimd
                    def _(pool):
                        for i in range(2):
                            for j in range(0, HT, 2):
                                cut_hidden(pool, i, j)
                S.end()

            with nc.Block() as block:
                @block.sync
                def _(sp):
                    load_expert(sp, 0, 0, S["in0"])
                    sp.dma_start(b1[:], t["b1"]).then_inc(S["bias"], 16)
                    sp.dma_start(b2[:], t["b2"]).then_inc(S["bias"], 16)
                    sp.wait_ge(S["bias"], 32)

                @block.tensor
                def _(pe):
                    pe.wait_ge(S["in0"], 48)
                    turn(pe, [slots_raw[0][:, n, :] for n in range(ST)]).then_inc(S["slots_turned"], 1)

                @block.scalar
                def _(act):
                    act.wait_ge(S["in0"], 48)
                    act.activation(w_parts[0][0][:], w_raw[0][:], ACT.Copy).then_inc(S["w_high"], 1)
                    act.wait_ge(S["slots_turned"], 1)
                    act.activation(slotsT[0][0][:], turned_ps, ACT.Copy).then_inc(S["slots_high"], 1)

                @block.vector
                def _(dve):
                    dve.wait_ge(S["w_high"], 1)
                    minus_high(dve, w_parts[0][1][:], w_raw[0][:], w_parts[0][0][:]).then_inc(S["w_low"], 1)
                    dve.wait_ge(S["slots_high"], 1)
                    minus_high(dve, slotsT[0][1][:], turned_ps, slotsT[0][0][:]).then_inc(S["slots_low"], 1)
            S.end()

            assert HT == 4 and E1 >= 4 and ST * P == 2 * BANK
            expert_pass(0, True, False)
            with nc.Fori(1, E1 // 2 - 1) as e2:
                expert_pass(e2 * 2, False, False)
            expert_pass(E1 - 2, False, True)

            with nc.Block() as block:
                @block.tensor
                def _(pe):
                    turn(pe, [outT[1][:, n * P:(n + 1) * P] for n in range(ST)]).then_inc(S["out_turned"], 1)

                @block.vector
                def _(dve):
                    dve.wait_ge(S["out_turned"], 1)
                    dve.tensor_copy(slot_out[1][:].rearrange("p n d -> p (n d)"), turned_ps).then_inc(S["out_copied"], 1)

                @block.sync
                def _(sp):
                    sp.wait_ge(S["out_copied"], 1)
                    sp.dma_start(outs_dram[(E1 - 1) * ROOM:E1 * ROOM].rearrange("(n p) d -> p n d", p=P), slot_out[1][:]) \
                        .then_inc(S["stored"], 16)
                    sp.wait_ge(S["stored"], 16)
            S.end()

            S = phase(*[f"g_got{b}" for b in range(B)], "g_dve", "g_stored")
            got = [sb(f"got{i}", [P, K, NT, P], stack=own) for i in range(2)]
            with nc.Block() as block:
                @block.gpsimd
                def _(pool):
                    for b in range(B):
                        if b >= 2:
                            pool.wait_ge(S["g_dve"], 4 * (b - 1))
                        for k in range(K):
                            for n in range(NT):
                                i = k * TILES + b * NT + n
                                pool.indirect_dma_start(
                                    got[b % 2][:, k, n, :], None, outs_dram,
                                    bass.IndirectOffsetOnAxis(ap=from_slot[:, i:i + 1], axis=0)).then_inc(S[f"g_got{b}"], 16)

                @block.vector
                def _(dve):
                    ch = Chain(dve, S["g_dve"])
                    for b in range(B):
                        dve.wait_ge(S[f"g_got{b}"], 16 * K * NT)
                        r = got[b % 2]
                        ch.link(dve.tensor_tensor(r[:], r[:], gates[:, :, b * NT:(b + 1) * NT].unsqueeze(3)
                                                  .to_broadcast([P, K, NT, P]), ALU.mult))
                        ch.link(dve.tensor_tensor(r[:, 0], r[:, 0], r[:, 1], ALU.add))
                        ch.link(dve.tensor_tensor(r[:, 0], r[:, 0], mod1_rows[:, b, 5:6, :].to_broadcast([P, NT, P]), ALU.mult))
                        dst = x_all[:, b * NT:(b + 1) * NT, :]
                        ch.link(dve.tensor_tensor(dst, dst, r[:, 0], ALU.add))

                @block.sync
                def _(sp):
                    for b in range(B):
                        sp.wait_ge(S["g_dve"], 4 * (b + 1))
                        sp.dma_start(t["out"][b].rearrange("(n p) d -> p n d", p=P), x_all[:, b * NT:(b + 1) * NT, :]) \
                            .then_inc(S["g_stored"], 16)
                    sp.wait_ge(S["g_stored"], 16 * B)
            S.end()


def kernel(**inputs):
    import concourse.bacc as bacc
    from concourse.bass_utils import run_bass_kernel_spmd

    f = {n: np.asarray(a) for n, a in inputs.items()}
    B, T, _ = f["L0_attn_x"].shape
    E0, I, _ = f["L0_ffn_gate_proj"].shape
    E1, _, HID = f["L1_ffn_w1"].shape
    p = np.arange(P)
    expert_of = np.arange(E0 * I) // I
    owner_rows = np.zeros((3 * 32, E0 * I), np.uint16)
    for w in range(3):
        owner_rows[32 * w:32 * w + E0][expert_of[None, :] == np.arange(E0)[:, None]] = 0x3F80
    below = np.broadcast_to((np.arange(E0)[None, :] < np.arange(E0)[:, None]).astype(np.float32), (P, E0, E0))
    distance = np.maximum(p[:, None] - p[None, :] - 1, 0).astype(np.float32)
    later = (p[:, None] > p[None, :]).astype(np.float32) / np.sqrt(np.float32(P))
    to_end = np.broadcast_to((P - 1 - p).astype(np.float32), (P, P))
    from_start = p[:, None].astype(np.float32)
    before = (p[:, None] < p[None, :]).astype(np.float32)
    expert_id = np.broadcast_to(np.arange(E1, dtype=np.float32), (P, E1))
    spill = np.arange(2 * B * T, dtype=np.float32).reshape(-1, P).T
    arrays = {
        "x": f["L0_attn_x"], "ident": np.eye(P, dtype=np.float32),
        "cT0": f["L0_c"].T, "cT1": f["L1_c"].T, "wmod0": f["L0_wmod"], "wmod1": f["L1_wmod"],
        "wq0": f["L0_attn_Wq"].T, "wk0": f["L0_attn_Wk"].T, "wv0": f["L0_attn_Wv"].T,
        "router0": f["L0_ffn_gate_w"].T, "bias0": np.broadcast_to(f["L0_ffn_gate_bias"], (P, E0)),
        "gate0": np.concatenate([f["L0_ffn_gate_proj"].reshape(E0 * I, P), f["L0_ffn_shared_gate_w"]]).T,
        "up0": np.concatenate([f["L0_ffn_up_proj"].reshape(E0 * I, P), f["L0_ffn_shared_up_w"]]).T,
        "down0": np.concatenate([f["L0_ffn_down_proj"].transpose(0, 2, 1).reshape(E0 * I, P),
                                 f["L0_ffn_shared_down_w"].T]),
        "owner": owner_rows, "below": below,
        "wq1": f["L1_attn_Wq"], "wk1": f["L1_attn_Wk"], "wv1": f["L1_attn_Wv"], "wo1": f["L1_attn_Wo"].T,
        "decay": np.broadcast_to(f["L1_attn_decay_logit"].reshape(1, 1), (P, 1)),
        "out_scale": np.broadcast_to(f["L1_attn_out_scale"].reshape(1, 1), (P, 1)),
        "distance": distance, "later": later, "to_end": to_end, "from_start": from_start,
        "router1": f["L1_ffn_wg"], "w1": f["L1_ffn_w1"], "b1": f["L1_ffn_b1"].reshape(E1, HID // P, P).transpose(2, 0, 1),
        "w2": f["L1_ffn_w2"], "b2": f["L1_ffn_b2"].T,
        "before": before, "expert_id": expert_id, "spill": spill,
    }
    arrays = {f"in_{n}_dram": np.ascontiguousarray(a) for n, a in arrays.items()}
    nc = bacc.Bacc("TRN2", target_bir_lowering=False, num_devices=1)
    t = {n[3:-5]: nc.dram_tensor(n, a.shape, mybir.dt.from_np(a.dtype), kind="ExternalInput").ap()
         for n, a in arrays.items()}
    t["out"] = nc.dram_tensor("out_0_dram", (B, T, P), F32, kind="ExternalOutput").ap()
    adaln_program(nc, t, {"B": B, "T": T, "E0": E0, "I": f["L0_ffn_gate_proj"].shape[1],
                          "E1": f["L1_ffn_w1"].shape[0], "HID": f["L1_ffn_w1"].shape[2]})
    r = run_bass_kernel_spmd(nc, [arrays], core_ids=[0])
    return r.results[0]["out_0_dram"]
```

```python
from contextlib import ExitStack

import numpy as np
import concourse.bass as bass
from concourse import mybir

F32 = mybir.dt.float32
F32R = mybir.dt.float32r
BF16 = mybir.dt.bfloat16
U16 = mybir.dt.uint16
U32 = mybir.dt.uint32
ALU = mybir.AluOpType
ACT = mybir.ActivationFunctionType
AX = mybir.AxisListType.X

P = 128
BANK = 512
EPS = 1e-5


class Phase:

    def __init__(self, nc, ctx, names):
        self.nc = nc
        handles = [ctx.enter_context(nc.semaphore(n)) for n in names]
        self.by_name = dict(zip(names, handles))
        nums = [h.num for h in handles]
        assert nums == list(range(nums[0], nums[0] + len(nums)))
        self.nums = range(nums[0], nums[-1] + 1)

    def __getitem__(self, name):
        return self.by_name[name]

    def end(self):
        self.nc.all_engine_barrier(sems_to_clear=self.nums)


class Chain:

    def __init__(self, eng, sem):
        self.eng, self.sem, self.n = eng, sem, 0

    def did(self, ins):
        self.n += 1
        ins.then_inc(self.sem, 1)
        return self.n

    def wait(self):
        self.eng.wait_ge(self.sem, self.n)

    def link(self, ins):
        self.did(ins)
        self.wait()


class NormBuffers:

    def __init__(self, name, cols, xb, xn, hT, stats, mv, ln):
        self.name, self.cols, self.xb, self.xn, self.hT = name, cols, xb, xn, hT
        self.stats, self.mv, self.ln = stats, mv, ln


def adaln_program(nc, t, shape):
    B, T = shape["B"], shape["T"]
    NT = T // P
    TILES = B * NT
    HEADS, HD = 16, P // 16
    GROUPS = 4
    GH = HEADS // GROUPS
    QUAD = P // GH
    PARTS = 3
    TERMS = PARTS * PARTS
    KROWS = TERMS * HD
    SROWS = KROWS + PARTS
    HALF = T // 2
    STEPS = 2 * NT
    assert HALF == BANK and GH * QUAD == P

    with ExitStack() as ctx:
        def sb(name, shp, dt=F32, stack=ctx):
            return stack.enter_context(nc.sbuf_tensor(name, shp, dt))

        def phase(*names):
            return Phase(nc, ctx, names)

        ps = ctx.enter_context(nc.psum_tensor("psum", [P, 8, BANK], F32))

        def product(pe, out, lhs, rhs, start=True, stop=True):
            (lh, ll), (rh, rl) = lhs, rhs
            pe.matmul(out, lh, rh, start=start, stop=False)
            pe.matmul(out, lh, rl, start=False, stop=False)
            return pe.matmul(out, ll, rh, start=False, stop=stop)

        def minus_high(eng, low, full, high):
            return eng.tensor_tensor(low, full, high.bitcast(F32), ALU.subtract)

        x_all = sb("x_all", [P, TILES, P])
        ident = sb("ident", [P, P])
        silu_cT = sb("silu_cT", [P, 2, B])
        mod_cols = sb("mod_cols", [P, 2, B, 6])
        ga0_rows = sb("ga0_rows", [P, B, P])
        mod1_rows = sb("mod1_rows", [P, B, 6, P])
        cur_cols = sb("cur_cols", [P, 6])
        xb = sb("xb", [P, NT, P])
        xn = sb("xn", [P, NT, P])
        hT = sb("hT", [P, T])
        stats = sb("stats", [P, NT, 6])
        mv = sb("mv", [P, NT, 2])
        ln = sb("ln", [P, 8, NT])

        q_dram = nc.dram_tensor("q_parts", [B, GROUPS, PARTS, GH * HD, T], BF16, kind="Internal").ap()
        k_dram = nc.dram_tensor("k_parts", [B, GROUPS, PARTS, GH * HD, T], BF16, kind="Internal").ap()
        v_dram = nc.dram_tensor("v_padded", [B, P, NT, HEADS * QUAD], F32, kind="Internal").ap()

        qk_w = sb("qk_w", [P, P])
        vo_w = sb("vo_w", [P, P])
        out_scale = sb("out_scale", [P, 1])
        mask = sb("mask", [P, P])
        end_powers = sb("end_powers", [P, P])
        start_powers = sb("start_powers", [P, 1])
        chunk_power = sb("chunk_power", [P, 1])

        STORES = 16 * (2 * PARTS + 1)
        qkv_free = ctx.enter_context(nc.semaphore("qkv_free"))
        qkv_own = ctx.enter_context(ExitStack())
        wqkv = sb("wqkv", [P, 3, P], stack=qkv_own)
        v_pad = sb("v_pad", [P, NT, HEADS, QUAD], stack=qkv_own)

        def keep_from_zero(steps, g, sign, size):
            eng = steps.eng
            steps.link(eng.tensor_scalar(sign, g, 0.0, 2.0, ALU.is_ge, ALU.mult))
            steps.link(eng.tensor_scalar(sign, sign, 1.0, None, ALU.subtract))
            steps.link(eng.tensor_tensor(size, sign, g, ALU.mult))
            steps.link(eng.tensor_scalar(size, size, 0.25, None, ALU.max))
            steps.link(eng.tensor_tensor(g, sign, size, ALU.mult))

        first = NormBuffers("ln", cur_cols, xb, xn, hT, stats, mv, ln)

        def norm_steps(dve, S, b, layer, N=first):
            c = Chain(dve, S[N.name + "_dve"])
            c.did(dve.tensor_copy(N.cols[:], mod_cols[:, layer, b, :] if isinstance(b, int) else
                                  mod_cols[:, layer].rearrange("p b v -> p (b v)")[:, bass.ds(b * 6, 6)]))
            c.link(dve.tensor_copy(N.xb[:], x_all[:, bass.ds(b * NT, NT), :]))
            yield
            for n in range(NT):
                c.did(dve.bn_stats(N.stats[:, n, :], N.xb[:, n, :]))
                if n % 4 == 3:
                    yield
            c.wait()
            for n in range(NT):
                c.did(dve.bn_aggr(N.mv[:, n, :], N.stats[:, n, :]))
            c.wait()
            step = [N.ln[:, i, :] for i in range(7)]
            dve.tensor_scalar(step[0], N.mv[:, :, 1], EPS, None, ALU.add).then_inc(S[N.name + "_var"], 1)
            yield
            yield
            dve.wait_ge(S[N.name + "_std"], 1)
            c.link(dve.reciprocal(step[2], step[1]))
            c.link(dve.tensor_tensor(step[3], step[2], step[2], ALU.mult))
            c.link(dve.tensor_tensor(step[4], step[3], step[0], ALU.mult))
            c.link(dve.tensor_scalar(step[5], step[4], -0.5, 1.5, ALU.mult, ALU.add))
            c.link(dve.tensor_tensor(step[6], step[5], step[2], ALU.mult))
            for n in range(NT):
                if n % 2 == 0:
                    yield
                dve.tensor_scalar(N.xn[:, n, :], N.xb[:, n, :], N.mv[:, n, 0:1], N.ln[:, 6, n:n + 1],
                                  ALU.subtract, ALU.mult).then_inc(S[N.name + "_xn"], 1)

        def norm_root(act, S, N=first):
            act.wait_ge(S[N.name + "_var"], 1)
            act.activation(N.ln[:, 1, :], N.ln[:, 0, :], ACT.Sqrt).then_inc(S[N.name + "_std"], 1)

        def norm_rows(act, S, shift, scale, N=first, bank=0):
            act.wait_ge(S[N.name + "_xT"], NT)
            act.activation(N.hT[:], ps[:, bank:bank + 2, :].rearrange("p a n -> p (a n)"), ACT.Identity,
                           bias=N.cols[:, shift:shift + 1], scale=N.cols[:, scale:scale + 1]) \
                .then_inc(S[N.name + "_hT"], 1)

        def norm_tensor(pe, S, N=first, bank=0):
            for n in range(NT):
                pe.wait_ge(S[N.name + "_xn"], n + 1)
                pe.transpose(ps[:, bank + n // 4, (n % 4) * P:(n % 4 + 1) * P], N.xn[:, n, :], ident[:]) \
                    .then_inc(S[N.name + "_xT"], 1)

        def batch_phase(prefix, *names):
            S = phase(*[f"{prefix}_{n}" for n in LN], *[f"{prefix}_{n}" for n in names])
            S.by_name = {n[len(prefix) + 1:]: h for n, h in S.by_name.items()}
            return S

        LN = ("ln_dve", "ln_var", "ln_std", "ln_xn", "ln_xT", "ln_hT")

        with ExitStack() as own:
            S = batch_phase("m", "x", "later", "ones", "in", "sig", "silu", "bc", "cols", "gate", "rows", "kept", "done")
            cT = sb("cT", [P, 2, B], stack=own)
            sig = sb("sig", [P, 2, B], stack=own)
            silu_bc = sb("silu_bc", [P, 2, B, P], stack=own)
            wmod = sb("wmod", [P, 2, 6 * P], stack=own)
            sgn = sb("sgn", [P, B, P], stack=own)
            sgc = sb("sgc", [P, 2, B, 2], stack=own)
            mag = sb("mag", [P, B, P], stack=own)
            magc = sb("magc", [P, 2, B, 2], stack=own)
            with nc.Block() as block:
                @block.sync
                def _(sp):
                    for i in range(2):
                        sp.dma_start(cT[:, i, :], t[f"cT{i}"]).then_inc(S["in"], 16)
                    for i in range(2):
                        sp.dma_start(wmod[:, i, :], t[f"wmod{i}"]).then_inc(S["in"], 16)
                    sp.dma_start(x_all[:], t["x"].rearrange("b (n p) d -> p (b n) d", p=P)).then_inc(S["x"], 16)
                    sp.dma_start(ident[:], t["ident"]).then_inc(S["x"], 16)
                    for i, w in enumerate(("wq0", "wk0", "wv0")):
                        sp.dma_start(wqkv[:, i, :], t[w]).then_inc(S["later"], 16)
                    sp.wait_ge(S["later"], 16 * 3)

                @block.gpsimd
                def _(pool):
                    pool.memset(v_pad[:], 0.0).then_inc(S["ones"], 1)
                    pool.wait_ge(S["ones"], 1)
                    pool.memset(v_pad[:, :, :, HD:HD + 1], 1.0).then_inc(qkv_free, 1)

                @block.scalar
                def _(act):
                    act.wait_ge(S["in"], 16 * 4)
                    act.activation(sig[:], cT[:], ACT.Sigmoid).then_inc(S["sig"], 1)
                    norm_root(act, S)
                    norm_rows(act, S, 0, 1)
                    act.wait_ge(S["rows"], 1)
                    act.activation(mod1_rows[:].rearrange("p b v d -> p (b v d)"), ps[:, 2:8, :].rearrange("p a n -> p (a n)"),
                                   ACT.Copy).then_inc(S["kept"], 1)

                @block.vector
                def _(dve):
                    own_steps = Chain(dve, S["done"])

                    dve.wait_ge(S["sig"], 1)
                    dve.tensor_tensor(silu_cT[:], cT[:], sig[:], ALU.mult).then_inc(S["silu"], 1)
                    dve.wait_ge(S["silu"], 1)
                    for i in range(2):
                        dve.tensor_copy(silu_bc[:, i], silu_cT[:, i, :].unsqueeze(2).to_broadcast([P, B, P])) \
                            .then_inc(S["bc"], 1)
                    dve.wait_ge(S["cols"], 1)
                    own_steps.link(dve.tensor_copy(
                        mod_cols[:], ps[:, 0, 0:2 * 6 * B].rearrange("p (i v b) -> p i b v", i=2, v=6)))
                    for v in (1, 4):
                        own_steps.did(dve.tensor_scalar(mod_cols[:, :, :, v], mod_cols[:, :, :, v], 1.0, None, ALU.add))
                    g = mod_cols[:].rearrange("p i b (w v) -> p i b w v", w=2)[:, :, :, :, 2]
                    keep_from_zero(own_steps, g.rearrange("p i b w -> p (i b w)"), sgc[:].rearrange("p i b w -> p (i b w)"),
                                   magc[:].rearrange("p i b w -> p (i b w)"))
                    own_steps.wait()
                    dve.wait_ge(S["x"], 32)
                    steps = norm_steps(dve, S, 0, 0)
                    for _ in range(4):
                        next(steps, None)
                    dve.wait_ge(S["gate"], 1)
                    own_steps.did(dve.tensor_copy(ga0_rows[:], ps[:, 1, :].rearrange("p (b d) -> p b d", b=B)))
                    own_steps.wait()
                    for _ in steps:
                        pass
                    keep_from_zero(own_steps, ga0_rows[:], sgn[:], mag[:])

                @block.tensor
                def _(pe):
                    pe.wait_ge(S["silu"], 1)
                    for i in range(2):
                        for v in range(6):
                            o = (i * 6 + v) * B
                            last = pe.matmul(ps[:, 0, o:o + B], wmod[:, i, v * P:(v + 1) * P], silu_cT[:, i, :],
                                             start=True, stop=True)
                    last.then_inc(S["cols"], 1)
                    pe.wait_ge(S["bc"], 2)
                    for b in range(B):
                        last = pe.matmul(ps[:, 1, b * P:(b + 1) * P], silu_bc[:, 0, b, :], wmod[:, 0, 2 * P:3 * P],
                                         start=True, stop=True)
                    last.then_inc(S["gate"], 1)
                    for b in range(B):
                        for v in range(6):
                            q = b * 6 + v
                            last = pe.matmul(ps[:, 2 + q // 4, (q % 4) * P:(q % 4 + 1) * P], silu_bc[:, 1, b, :],
                                             wmod[:, 1, v * P:(v + 1) * P], start=True, stop=True)
                    last.then_inc(S["rows"], 1)
                    norm_tensor(pe, S)
            S.end()

        with ExitStack() as own:
            part = [[sb(f"part{w}{i}", [P, T], BF16, stack=own) for i in range(PARTS)] for w in "qk"]
            rest = [sb(f"rest{w}", [P, T], stack=own) for w in "qk"]

            S = batch_phase("qkv", "qk", "v", "high0", "high1", "rest0", "rest1", "mid0", "mid1", "low", "vpad")

            def project(b, n):
                wide = lambda first: ps[:, first:first + 2, :].rearrange("p a n -> p (a n)")
                with nc.Block() as block:
                    @block.vector
                    def _(dve):
                        steps = norm_steps(dve, S, n, 0) if n is not None else iter(())
                        for _ in range(4):
                            next(steps, None)
                        if b is not None:
                            dve.wait_ge(qkv_free, b * STORES + 1)
                            for w in range(2):
                                dve.wait_ge(S[f"high{w}"], 1)
                                dve.tensor_tensor(rest[w][:], wide(2 + 2 * w), part[w][0][:], ALU.subtract) \
                                    .then_inc(S[f"rest{w}"], 1)
                        for _ in steps:
                            pass
                        if b is not None:
                            gate = ga0_rows[:, bass.ds(b, 1), :].to_broadcast([P, 4, P])
                            for c in range(2):
                                dve.wait_ge(S["v"], c + 1)
                                dve.tensor_tensor(
                                    v_pad[:, 4 * c:4 * c + 4, :, 0:HD],
                                    ps[:, 6 + c, :].rearrange("p (n h d) -> p n h d", n=4, d=HD),
                                    gate.rearrange("p n (h d) -> p n h d", d=HD), ALU.mult).then_inc(S["vpad"], 1)
                            for w in range(2):
                                dve.wait_ge(S[f"mid{w}"], 1)
                                dve.tensor_tensor(part[w][2][:], rest[w][:], part[w][1][:], ALU.subtract) \
                                    .then_inc(S["low"], 1)

                    @block.scalar
                    def _(act):
                        def high(w):
                            act.wait_ge(S["qk"], w + 1)
                            act.activation(part[w][0][:], wide(2 + 2 * w), ACT.Copy).then_inc(S[f"high{w}"], 1)

                        if b is not None:
                            act.wait_ge(qkv_free, b * STORES + 1)
                            high(0)
                        if n is not None:
                            norm_root(act, S)
                        if b is not None:
                            high(1)
                            for w in range(2):
                                act.wait_ge(S[f"rest{w}"], 1)
                                act.activation(part[w][1][:], rest[w][:], ACT.Copy).then_inc(S[f"mid{w}"], 1)
                        if n is not None:
                            norm_rows(act, S, 0, 1)

                    @block.tensor
                    def _(pe):
                        if b is not None:
                            for w in range(2):
                                for c in range(2):
                                    last = pe.matmul(ps[:, 2 + 2 * w + c, :], wqkv[:, w, :], hT[:, c * BANK:(c + 1) * BANK],
                                                     start=True, stop=True)
                                last.then_inc(S["qk"], 1)
                            for i in range(NT):
                                last = pe.matmul(ps[:, 6 + i // 4, (i % 4) * P:(i % 4 + 1) * P], hT[:, i * P:(i + 1) * P],
                                                 wqkv[:, 2, :], start=True, stop=True)
                                if i % 4 == 3:
                                    last.then_inc(S["v"], 1)
                        if n is not None:
                            norm_tensor(pe, S)

                    @block.sync
                    def _(sp):
                        if b is None:
                            return
                        for i, name in enumerate(("high", "mid")):
                            for w, dram in enumerate((q_dram, k_dram)):
                                sp.wait_ge(S[f"{name}{w}"], 1)
                                sp.dma_start(dram[b, :, i], part[w][i][:]).then_inc(qkv_free, 16)
                        sp.wait_ge(S["vpad"], 2)
                        sp.dma_start(v_dram[b], v_pad[:].rearrange("p n h d -> p n (h d)")).then_inc(qkv_free, 16)
                        for w, dram in enumerate((q_dram, k_dram)):
                            sp.wait_ge(S["low"], w + 1)
                            sp.dma_start(dram[b, :, 2], part[w][2][:]).then_inc(qkv_free, 16)
                S.end()

            with nc.Fori(0, B - 1) as b:
                project(b, b + 1)
            project(B - 1, None)

        qkv_own.close()

        E0, I = shape["E0"], shape["I"]
        FEATS = E0 * I
        ALL = t["gate0"].shape[1]
        ROUTED = FEATS // P
        FT = -(-ALL // P)
        rows_of = [min(P, ALL - j * P) for j in range(FT)]
        full = ALL // P
        ffn_own = ctx.enter_context(ExitStack())
        gate_raw = sb("gate_raw", [P, ALL], stack=ffn_own)
        up_raw = sb("up_raw", [P, ALL], stack=ffn_own)
        down_raw = sb("down_raw", [P, FT, P], stack=ffn_own)
        router = sb("router0", [P, E0], stack=ffn_own)
        bias = sb("bias0", [P, E0], stack=ffn_own)
        below = sb("below", [P, E0, E0], stack=ffn_own)
        owner = sb("owner", [3 * 32, FEATS], BF16, stack=ffn_own)
        E1, HID = shape["E1"], shape["HID"]
        K = 2
        TOKENS = B * T
        ROOM = K * (-(-TOKENS // E1))
        SLOTS = E1 * ROOM
        ST = ROOM // P
        NUMBER = P
        ROW = P + 16
        slots_dram = nc.dram_tensor("slots", [SLOTS + K * TOKENS, ROW], F32, kind="Internal").ap()
        outs_dram = nc.dram_tensor("choice_outs", [K * TOKENS + SLOTS, P], F32, kind="Internal").ap()

        with ExitStack() as own:
            S = phase("a_load0", "a_load1", "a_load2", "a_load3", "a_scores", "a_exp", "a_maxmm", "a_max",
                      "a_rowT", "a_neg", "a_negrows", "a_pv", "a_oT", "a_turned", "a_free7", "a_dve", "a_ones", "a_zeros",
                      "a_other",
                      "a_l1", "a_l1_dve", "a_l1_act", "a_l1_pe", "a_rows")
            q_ops = [sb(f"q_ops{g}", [P, GH, T], BF16, stack=own) for g in range(GROUPS)]
            k_ops = [sb(f"k_ops{g}", [P, GH, T], BF16, stack=own) for g in range(GROUPS)]
            v_ops = [sb(f"v_ops{g}", [P, NT, P], stack=own) for g in range(GROUPS)]
            prob = [sb(f"prob{i}", [P, GH, BANK], stack=own) for i in range(2)]
            row_max = [sb(f"row_max{i}", [P, GH * NT], stack=own) for i in range(2)]
            neg = sb("neg", [GH * NT, P], stack=own)
            neg_rest = sb("neg_rest", [GH * NT, P], stack=own)
            neg_part = [sb(f"neg_part{i}", [GH * NT, P], BF16, stack=own) for i in range(PARTS)]
            oT = sb("oT", [P, 2, BANK], stack=own)
            recip = sb("recip", [P, 4, GH], stack=own)
            head_out = sb("head_out", [P, 4, GH * HD], stack=own)
            zeros = sb("zeros", [P, ST, ROW], stack=own)
            sgn = sb("sgn1", [P, B, P], stack=own)
            mag = sb("mag1", [P, B, P], stack=own)
            w1q = sb("w1q", [P, 4, P], stack=own)
            decay = sb("decay", [P, 8], stack=own)
            distance = sb("distance", [P, P], stack=own)
            later = sb("later", [P, P], stack=own)
            to_end = sb("to_end", [P, P], stack=own)
            from_start = sb("from_start", [P, 1], stack=own)
            powers = sb("powers", [P, P], stack=own)

            def load_unit(sp, b, g, ones=None):
                sem = S[f"a_load{g}"]
                if ones:
                    sp.wait_ge(ones, g + 1)
                sp.dma_start(k_ops[g][0:KROWS].rearrange("r h t -> r (h t)"),
                             k_dram[b, g].rearrange("j (d h) t -> (j d) (h t)", d=HD).unsqueeze(0)
                             .to_broadcast([PARTS, PARTS * HD, GH * T])).then_inc(sem, 16)
                for i in range(PARTS):
                    sp.dma_start(q_ops[g][i * PARTS * HD:(i + 1) * PARTS * HD].rearrange("r h t -> r (h t)"),
                                 q_dram[b, g, i:i + 1].rearrange("i (d h) t -> i d (h t)", d=HD)
                                 .to_broadcast([PARTS, HD, GH * T])).then_inc(sem, 16)
                sp.dma_start(v_ops[g][:], v_dram[b, :, :, g * P:(g + 1) * P]).then_inc(sem, 16)

            LOADED = 16 * (1 + PARTS + 1)

            ROWS = GH * NT
            PER_STEP = ROWS // STEPS
            AHEAD = 4 * PER_STEP

            def max_scores(pe, g, i, asked):
                h, n = divmod(i, NT)
                if asked >= 2:
                    pe.wait_ge(S["a_max"], asked - 1)
                for c in range(2):
                    last = pe.matmul(ps[:, 2 + 2 * (i % 2) + c, :], q_ops[g][0:KROWS, h, n * P:(n + 1) * P],
                                     k_ops[g][0:KROWS, h, c * BANK:(c + 1) * BANK], start=True, stop=True)
                last.then_inc(S["a_maxmm"], 1)

            def reduce_max(dve, rows, i, asked):
                dve.wait_ge(S["a_maxmm"], asked + 1)
                dve.tensor_reduce(rows[:, i:i + 1], ps[:, 2 + 2 * (i % 2):4 + 2 * (i % 2), :].rearrange("p a n -> p (a n)"),
                                  axis=AX, op=ALU.max).then_inc(S["a_max"], 1)

            def store_neg(sp, g, count):
                sp.wait_ge(S["a_neg"], count)
                for i in range(PARTS):
                    sp.dma_start(q_ops[g][KROWS + i:KROWS + i + 1].rearrange("p h (n q) -> p (h n) q", q=P),
                                 neg_part[i][:]).then_inc(S["a_negrows"], 16)

            def split_neg(dve, ch):
                ch.link(dve.tensor_copy(neg_part[0][:], neg[:]))
                ch.link(dve.tensor_tensor(neg_rest[:], neg[:], neg_part[0][:], ALU.subtract))
                ch.link(dve.tensor_copy(neg_part[1][:], neg_rest[:]))
                dve.tensor_tensor(neg_part[2][:], neg_rest[:], neg_part[1][:], ALU.subtract).then_inc(S["a_neg"], 1)

            with nc.Block() as block:
                @block.vector
                def _(dve):
                    c = Chain(dve, S["a_dve"])
                    l1 = Chain(dve, S["a_l1_dve"])
                    for i in range(ROWS):
                        reduce_max(dve, row_max[1], i, i)
                        if i == ROWS // 2:
                            dve.wait_ge(S["a_l1"], 160)
                            l1.did(dve.scalar_tensor_tensor(decay[:, 1:2], decay[:, 0:1], -1.0, decay[:, 0:1], ALU.mult, ALU.min))
                        if i == ROWS // 2 + 6:
                            dve.wait_ge(S["a_l1_act"], 2)
                            l1.did(dve.scalar_tensor_tensor(decay[:, 4:5], decay[:, 0:1], 0.0, decay[:, 3:4], ALU.min, ALU.subtract))
                    dve.wait_ge(S["a_rowT"], 1)
                    c.link(dve.tensor_scalar(neg[:], ps[0:ROWS, 7, 0:P], -1.0, None, ALU.mult))
                    split_neg(dve, c)
                    for i in range(AHEAD):
                        reduce_max(dve, row_max[0], i, ROWS + i)
                    dve.wait_ge(S["a_l1_act"], 6)
                    l1.did(dve.tensor_tensor(mask[:], powers[:], later[:], ALU.mult))
                    l1.did(dve.tensor_scalar(end_powers[:], end_powers[:], float(np.float32(P) ** -0.5), None, ALU.mult))
                    dve.wait_ge(S["a_l1_pe"], 1)
                    l1.did(dve.tensor_copy(qk_w[:], ps[:, 0, 0:P]))
                    l1.did(dve.tensor_copy(vo_w[:], ps[:, 1, 0:P]))

                @block.scalar
                def _(act):
                    ch = Chain(act, S["a_l1_act"])
                    act.wait_ge(S["a_l1_dve"], 1)
                    ch.link(act.activation(decay[:, 2:3], decay[:, 1:2], ACT.Exp))
                    ch.link(act.activation(decay[:, 3:4], decay[:, 2:3], ACT.Ln, bias=1.0))
                    act.wait_ge(S["a_l1_dve"], 2)
                    log = decay[:, 4:5]
                    ch.did(act.activation(powers[:], distance[:], ACT.Exp, scale=log))
                    ch.did(act.activation(end_powers[:], to_end[:], ACT.Exp, scale=log))
                    ch.did(act.activation(start_powers[:], from_start[:], ACT.Exp, scale=log))
                    ch.did(act.activation(chunk_power[:], log, ACT.Exp, scale=float(P)))

                @block.gpsimd
                def _(pool):
                    for g in range(GROUPS):
                        pool.memset(k_ops[g][KROWS // 32 * 32:], 1.0).then_inc(S["a_ones"], 1)
                    pool.wait_ge(S["a_ones"], GROUPS)
                    pool.memset(zeros[:], 0.0).then_inc(S["a_zeros"], 1)
                    pool.wait_ge(S["a_zeros"], 1)
                    rows = Chain(pool, S["a_rows"])
                    for v in (1, 4):
                        rows.link(pool.tensor_scalar(mod1_rows[:, :, v, :], mod1_rows[:, :, v, :], 1.0, None, ALU.add))
                    for v in (2, 5):
                        keep_from_zero(rows, mod1_rows[:, :, v, :], sgn[:], mag[:])

                @block.sync
                def _(sp):
                    sp.wait_ge(qkv_free, B * STORES + 1)
                    for g in range(GROUPS - 1):
                        load_unit(sp, 0, g, S["a_ones"])
                    for i, n in enumerate(("wq1", "wk1", "wv1", "wo1")):
                        sp.dma_start(w1q[:, i, :], t[n]).then_inc(S["a_l1"], 16)
                    for dst, n in ((decay[:, 0:1], "decay"), (out_scale[:], "out_scale"), (distance[:], "distance"),
                                   (later[:], "later"), (to_end[:], "to_end"), (from_start[:], "from_start")):
                        sp.dma_start(dst, t[n]).then_inc(S["a_l1"], 16)
                    others = 7
                    for dst, n in ((router[:], "router0"), (bias[:], "bias0"), (below[:], "below"), (owner[:].bitcast(U16), "owner")):
                        sp.dma_start(dst, t[n]).then_inc(S["a_other"], 16)
                    sp.dma_start(gate_raw[:], t["gate0"]).then_inc(S["a_other"], 16)
                    sp.dma_start(up_raw[:], t["up0"]).then_inc(S["a_other"], 16)
                    sp.dma_start(down_raw[:, 0:full, :], t["down0"][0:full * P].rearrange("(j p) d -> p j d", p=P)) \
                        .then_inc(S["a_other"], 16)
                    if full < FT:
                        sp.dma_start(down_raw[0:rows_of[-1], full, :], t["down0"][full * P:ALL]) \
                            .then_inc(S["a_other"], 16)
                        others += 1
                    sp.wait_ge(S["a_zeros"], 1)
                    for e in range(E1):
                        sp.dma_start(slots_dram[e * ROOM:(e + 1) * ROOM].rearrange("(n p) d -> p n d", p=P), zeros[:]) \
                            .then_inc(S["a_other"], 16)
                        sp.dma_start(outs_dram[e * ROOM:(e + 1) * ROOM].rearrange("(n p) d -> p n d", p=P), zeros[:, :, 0:P]) \
                            .then_inc(S["a_other"], 16)
                    others += 2 * E1
                    store_neg(sp, 0, 1)
                    sp.wait_ge(S["a_negrows"], 48)
                    for g in range(GROUPS - 1):
                        sp.wait_ge(S[f"a_load{g}"], LOADED)
                    sp.wait_ge(S["a_other"], 16 * others)

                @block.tensor
                def _(pe):
                    pe.wait_ge(S["a_load0"], LOADED)
                    for i in range(ROWS):
                        max_scores(pe, 0, i, i)
                    pe.wait_ge(S["a_l1"], 160)
                    pe.matmul(ps[:, 0, 0:P], w1q[:, 0, :], w1q[:, 1, :], start=True, stop=True)
                    pe.matmul(ps[:, 1, 0:P], w1q[:, 2, :], w1q[:, 3, :], start=True, stop=True).then_inc(S["a_l1_pe"], 1)
                    pe.wait_ge(S["a_max"], ROWS)
                    pe.transpose(ps[0:ROWS, 7, 0:P], row_max[1][:], ident[:]).then_inc(S["a_rowT"], 1)
                    pe.wait_ge(S["a_load1"], LOADED)
                    for i in range(AHEAD):
                        max_scores(pe, 1, i, ROWS + i)
            S.end()

            def attention(b, last_batch):
                stop = ROWS * (GROUPS - 1) if last_batch else ROWS * GROUPS + AHEAD
                to_negate = GROUPS - 1 if last_batch else GROUPS
                turns = []
                for k in range(GROUPS * STEPS):
                    g, s = divmod(k, STEPS)
                    if k % NT == 3 and k > NT:
                        turns.append(("out", (k - 3) // NT - 1))
                    if s == STEPS - 3 and g < to_negate:
                        turns.append(("max", g))
                turns.append(("out", 2 * GROUPS - 1))
                order = {u: i for i, u in enumerate(turns)}

                def asked_for(k):
                    for i in range(AHEAD + k * PER_STEP, AHEAD + (k + 1) * PER_STEP):
                        if i < stop:
                            yield i - AHEAD, i // ROWS, i % ROWS

                with nc.Block() as block:
                    @block.tensor
                    def _(pe):
                        def scores(k, h):
                            g, s = divmod(k, STEPS)
                            c, n = divmod(s, NT)
                            if k or h >= 2:
                                pe.wait_ge(S["a_exp"], 4 * k + h - 1)
                            pe.matmul(ps[:, h % 2, :], k_ops[g][0:SROWS, h, n * P:(n + 1) * P],
                                      q_ops[g][0:SROWS, h, c * BANK:(c + 1) * BANK], start=True, stop=True) \
                                .then_inc(S["a_scores"], 1)

                        def values(k):
                            g, s = divmod(k, STEPS)
                            pe.wait_ge(S["a_exp"], 4 * k + 4)
                            if s % NT == 0 and k:
                                pe.wait_ge(S["a_oT"], k // NT)
                            for h in range(GH):
                                last = pe.matmul(ps[h * QUAD:(h + 1) * QUAD, 6, :], v_ops[g][:, s % NT, h * QUAD:(h + 1) * QUAD],
                                                 prob[k % 2][:, h, :], start=(s % NT == 0), stop=(s % NT == NT - 1))
                            last.then_inc(S["a_pv"], 1)

                        def turn_out(m):
                            pe.wait_ge(S["a_oT"], m + 1)
                            if order["out", m]:
                                pe.wait_ge(S["a_free7"], order["out", m])
                            for i in range(4):
                                last = pe.transpose(ps[:, 7, i * P:(i + 1) * P], oT[:, m % 2, i * P:(i + 1) * P], ident[:])
                            last.then_inc(S["a_turned"], 1)

                        for k in range(GROUPS * STEPS):
                            g, s = divmod(k, STEPS)
                            if s == 0 and g:
                                pe.wait_ge(S["a_negrows"], 48 * g)
                            for h in range(GH):
                                scores(k, h)
                                for i, u, row in (asked_for(k) if h == 1 else ()):
                                    if u == GROUPS - 2 and row == 0:
                                        pe.wait_ge(S["a_load3"], LOADED)
                                    if u >= GROUPS - 1 and row == 0:
                                        pe.wait_ge(S[f"a_load{u - GROUPS + 1}"], LOADED)
                                    max_scores(pe, (u + 1) % GROUPS, row, i)
                            if k:
                                values(k - 1)
                            if k % NT == 3 and k > NT:
                                turn_out((k - 3) // NT - 1)
                            if s == STEPS - 3 and g < to_negate:
                                pe.wait_ge(S["a_max"], ROWS * (g + 1) - AHEAD)
                                if order["max", g]:
                                    pe.wait_ge(S["a_free7"], order["max", g])
                                pe.transpose(ps[0:ROWS, 7, 0:P], row_max[g % 2][:], ident[:]).then_inc(S["a_rowT"], 1)
                        values(GROUPS * STEPS - 1)
                        turn_out(2 * GROUPS - 1)

                    @block.scalar
                    def _(act):
                        def copy_out(m):
                            act.wait_ge(S["a_pv"], (m + 1) * NT)
                            if m >= 2:
                                act.wait_ge(S["a_turned"], m - 1)
                            act.activation(oT[:, m % 2, :], ps[:, 6, :], ACT.Copy).then_inc(S["a_oT"], 1)

                        for k in range(GROUPS * STEPS):
                            if k >= 2:
                                act.wait_ge(S["a_pv"], k - 1)
                            for h in range(GH):
                                act.wait_ge(S["a_scores"], 4 * k + h + 1)
                                act.activation(prob[k % 2][:, h, :], ps[:, h % 2, :], ACT.Exp).then_inc(S["a_exp"], 1)
                                if h == 1 and k > NT and k % NT == 1:
                                    copy_out(k // NT - 1)
                        copy_out(2 * GROUPS - 1)

                    @block.vector
                    def _(dve):
                        ch = Chain(dve, S["a_dve"])

                        def add_out(m):
                            g, c = divmod(m, 2)
                            turned = ps[:, 7, :].rearrange("p (n h d) -> p n h d", n=4, h=GH)
                            dve.wait_ge(S["a_turned"], m + 1)
                            ch.link(dve.reciprocal(recip[:], turned[:, :, :, HD]))
                            dve.tensor_tensor(
                                head_out[:].rearrange("p n (h d) -> p (n h) d", d=HD),
                                ps[:, 7, :].rearrange("p (a d) -> p a d", d=QUAD)[:, :, 0:HD],
                                recip[:].rearrange("p n h -> p (n h)").unsqueeze(2).to_broadcast([P, 4 * GH, HD]),
                                ALU.mult).then_inc(S["a_free7"], 1)
                            dve.wait_ge(S["a_free7"], order["out", m] + 1)
                            dst = x_all[:, bass.ds(b * NT + 4 * c, 4), g * GH * HD:(g + 1) * GH * HD]
                            ch.link(dve.tensor_tensor(dst, dst, head_out[:], ALU.add))

                        for k in range(GROUPS * STEPS):
                            g, s = divmod(k, STEPS)
                            for i, u, row in asked_for(k):
                                reduce_max(dve, row_max[u % 2], row, i)
                            if s == STEPS - 3 and g < to_negate:
                                dve.wait_ge(S["a_rowT"], g + 1)
                                if g:
                                    dve.wait_ge(S["a_negrows"], 48 * g)
                                dve.tensor_scalar(neg[:], ps[0:ROWS, 7, 0:P], -1.0, None, ALU.mult) \
                                    .then_inc(S["a_free7"], 1)
                                dve.wait_ge(S["a_free7"], order["max", g] + 1)
                                split_neg(dve, ch)
                            if k % NT == 4 and k > NT:
                                add_out((k - 4) // NT - 1)
                        add_out(2 * GROUPS - 1)

                    @block.sync
                    def _(sp):
                        load_unit(sp, b, GROUPS - 1)
                        for g in range(GROUPS):
                            if g < to_negate:
                                store_neg(sp, (g + 1) % GROUPS, g + 1)
                            if not last_batch and g < GROUPS - 1:
                                sp.wait_ge(S["a_pv"], STEPS * (g + 1))
                                load_unit(sp, b + 1, g)
                        sp.wait_ge(S["a_negrows"], 48 * to_negate)
                        for g in range(GROUPS):
                            if g == GROUPS - 1 or not last_batch:
                                sp.wait_ge(S[f"a_load{g}"], LOADED)
                S.end()

            with nc.Fori(0, B - 1) as b:
                attention(b, False)
            attention(B - 1, True)

        EG = 4
        NG = E0 // EG
        TOP_GROUPS, TOP = 2, 4
        assert FEATS % P == 0
        with ExitStack() as own:
            gate_w = [sb(f"gate_w{i}", [P, ALL], F32R, stack=own) for i in range(2)]
            up_w = [sb(f"up_w{i}", [P, ALL], F32R, stack=own) for i in range(2)]
            down_w = [sb(f"down_w{i}", [P, FT, P], F32R, stack=own) for i in range(2)]
            c_next = sb("c_next", [3 * 32, T], BF16, stack=own)

            pieces = [(raw[:], high[:], low[:]) for raw, (high, low) in ((gate_raw, gate_w), (up_raw, up_w))]
            pieces.append([w[:, 0:full, :] for w in (down_raw, *down_w)])
            if full < FT:
                pieces.append([w[0:rows_of[-1], full, :] for w in (down_raw, *down_w)])

            scores = sb("scores", [P, NT, E0], stack=own)
            biased = sb("biased", [P, NT, E0], stack=own)
            pair_max = sb("pair_max", [P, NT * NG, 2], stack=own)
            pair_sum = sb("pair_sum", [P, NT * NG, 2], stack=own)
            top_a = sb("top_a", [P, NT * NG], stack=own)
            top_b = sb("top_b", [P, NT * NG], stack=own)
            group_score = sb("group_score", [P, NT, NG], stack=own)
            ahead = sb("ahead", [P, 2 * E0 * E0], stack=own)
            tied = sb("tied", [P, 2 * E0 * E0], stack=own)
            rank = sb("rank", [P, NT, E0], stack=own)
            chosen = sb("chosen", [P, NT, E0], stack=own)
            masked = sb("masked", [P, NT, E0], stack=own)
            total = sb("total", [P, NT], stack=own)
            inverse = sb("inverse", [P, NT], stack=own)
            combine = sb("combine", [P, NT, E0], stack=own)
            c_rest = sb("c_rest", [E0, T], stack=own)
            c_mid = sb("c_mid", [E0, T], BF16, stack=own)
            c_parts = sb("c_parts", [3 * 32, T], BF16, stack=own)
            h_parts = [sb(f"h_parts{i}", [P, T], F32R, stack=own) for i in range(2)]
            gb_col = sb("gb_col", [P, 1], stack=own)
            spare = [gate_raw[:, i * BANK:(i + 1) * BANK] for i in range(6)]
            gated, prod, acts = spare[0:2], spare[2:4], spare[4:6]
            act_high = [sb(f"act_high{i}", [P, BANK], F32R, stack=own) for i in range(3)]
            act_low = [sb(f"act_low{i}", [P, BANK], F32R, stack=own) for i in range(3)]
            yT = up_raw[:, 0:2 * BANK].rearrange("p (c n) -> p c n", c=2)

            TILES_ALL = 2 * FT

            def experts(b, ahead_of):
                prep, main = ahead_of is not None, b is not None
                CUT_NEXT = FT + 3
                uses = ([("rows", 0), ("rows", 1), ("logits", 0), ("weights", 0), ("weights", 1)] if prep else [])
                slots = {("rows", 0): 9, ("rows", 1): 11, ("logits", 0): 13, ("weights", 0): 2 * FT - 9, ("weights", 1): 2 * FT - 5,
                         ("out", 0): FT + 4, ("out", 1): TILES_ALL + 2}
                if main:
                    uses = sorted(uses + [("out", 0), ("out", 1)], key=lambda u: slots[u])
                before = dict(zip(uses[1:], uses))
                read_out = {"rows": "ln_hT", "logits": "scores", "weights": "c_rest", "out": "added"}
                bank7 = ps[:, 7, :]

                with nc.Block() as block:
                    @block.tensor
                    def _(pe):
                        def gate_up(i):
                            c, j = divmod(i, FT)
                            m = rows_of[j]
                            cols, tokens = slice(j * P, j * P + m), slice(c * BANK, (c + 1) * BANK)
                            h = [x[:, tokens] for x in h_parts]
                            if i == FT:
                                pe.wait_ge(S["h_low"], 1)
                            if i >= 2:
                                pe.wait_ge(S["silu"], i - 1)
                            product(pe, ps[0:m, i % 2, :], [w[:, cols] for w in gate_w], h).then_inc(S["gate"], 1)
                            if i >= 2:
                                pe.wait_ge(S["act"], i - 1)
                            last = product(pe, ps[0:m, 2 + i % 2, :], [w[:, cols] for w in up_w], h)
                            if j < ROUTED:
                                if i == 0:
                                    pe.wait_ge(S["c_parts"], 1)
                                last = pe.matmul(ps[:, 4 + i % 2, :], owner[:, j * P:(j + 1) * P], c_parts[:, tokens],
                                                 start=True, stop=True)
                            last.then_inc(S["up"], 1)

                        def down(i):
                            c, j = divmod(i, FT)
                            m = rows_of[j]
                            pe.wait_ge(S["low"], i + 1)
                            if j == 0 and c:
                                pe.wait_ge(S["yT"], c)
                            product(pe, ps[:, 6, :], [w[0:m, j, :] for w in down_w],
                                    (act_high[i % 3][0:m, :], act_low[i % 3][0:m, :]),
                                    start=(j == 0), stop=(j == FT - 1)).then_inc(S["down"], 1)

                        def use_bank7(use):
                            what, c = use
                            if use in before:
                                pe.wait_ge(S[read_out[before[use][0]]], before[use][1] + 1)
                            if what == "out":
                                pe.wait_ge(S["yT"], c + 1)
                            if what == "logits":
                                pe.wait_ge(S["ln_hT"], 2)
                                for n in range(NT):
                                    last = pe.matmul(ps[:, 7, n * E0:(n + 1) * E0], hT[:, n * P:(n + 1) * P], router[:],
                                                     start=True, stop=True)
                                last.then_inc(S["logits"], 1)
                                return
                            if what == "weights":
                                pe.wait_ge(S["combine"], 1)
                            for n in range(4):
                                cols = slice(n * P, (n + 1) * P)
                                if what == "rows":
                                    pe.wait_ge(S["ln_xn"], 4 * c + n + 1)
                                    last = pe.transpose(ps[:, 7, cols], xn[:, 4 * c + n, :], ident[:])
                                if what == "weights":
                                    last = pe.transpose(ps[0:E0, 7, cols], combine[:, 4 * c + n, :], ident[:])
                                if what == "out":
                                    last = pe.transpose(ps[:, 7, cols], yT[:, c, cols], ident[:])
                            last.then_inc(S[{"rows": "ln_xT", "weights": "cT", "out": "turned"}[what]], 1)

                        for i in range(TILES_ALL + 3):
                            if main and i < TILES_ALL:
                                gate_up(i)
                            if main and 2 <= i < TILES_ALL + 2:
                                down(i - 2)
                            for use in uses:
                                if slots[use] == i:
                                    use_bank7(use)

                    def at(i, *what):
                        return [u for u in uses if u[0] in what and slots[u] == i]

                    @block.scalar
                    def _(act):
                        def rows_high(c):
                            cols = slice(c * BANK, (c + 1) * BANK)
                            act.activation(h_parts[0][:, cols], hT[:, cols], ACT.Copy).then_inc(S["h_high"], 1)

                        def weights_high(some):
                            for raw, high, _ in some:
                                act.activation(high, raw, ACT.Copy).then_inc(S["w_high"], 1)

                        if main:
                            rows_high(1)
                        else:
                            weights_high(pieces[:1])
                        for i in range(TILES_ALL + 4):
                            if main and i < TILES_ALL:
                                m = rows_of[i % FT]
                                act.wait_ge(S["gate"], i + 1)
                                if i >= 2:
                                    act.wait_ge(S["act"], i - 1)
                                act.activation(gated[i % 2][0:m, :], ps[0:m, i % 2, :], ACT.Silu).then_inc(S["silu"], 1)
                            if main and 1 <= i <= TILES_ALL:
                                m = rows_of[(i - 1) % FT]
                                act.wait_ge(S["act"], i)
                                if i >= 4:
                                    act.wait_ge(S["down"], i - 3)
                                act.activation(act_high[(i - 1) % 3][0:m, :], acts[(i - 1) % 2][0:m, :], ACT.Copy) \
                                    .then_inc(S["high"], 1)
                            if prep and i == 4:
                                norm_root(act, S)
                            for what, c in at(i, "rows"):
                                act.wait_ge(S["ln_xT"], c + 1)
                                if main:
                                    act.wait_ge(S["h_low"], 1)
                                act.activation(hT[:, c * BANK:(c + 1) * BANK], bank7, ACT.Identity, bias=cur_cols[:, 3:4],
                                               scale=cur_cols[:, 4:5]).then_inc(S["ln_hT"], 1)
                            if prep and i == CUT_NEXT:
                                act.wait_ge(S["ln_hT"], 1)
                                if main:
                                    act.wait_ge(S["up"], FT)
                                rows_high(0)
                            for _ in at(i, "logits"):
                                act.wait_ge(S["logits"], 1)
                                act.activation(scores[:].rearrange("p n e -> p (n e)"), ps[:, 7, 0:NT * E0], ACT.Sigmoid) \
                                    .then_inc(S["scores"], 1)
                            if main and i == FT + 1 or main and i == TILES_ALL + 1:
                                c = i // TILES_ALL
                                act.wait_ge(S["down"], FT * (c + 1))
                                act.activation(yT[:, c, :], ps[:, 6, :], ACT.Copy, scale=gb_col[:]).then_inc(S["yT"], 1)
                            if not main and i == slots["logits", 0]:
                                weights_high(pieces[1:])

                    @block.gpsimd
                    def _(pool):
                        def rows_low(c, count):
                            cols = slice(c * BANK, (c + 1) * BANK)
                            pool.wait_ge(S["h_high"], count)
                            minus_high(pool, h_parts[1][:, cols], hT[:, cols], h_parts[0][:, cols]).then_inc(S["h_low"], 1)

                        def weights_low(some):
                            for i in some:
                                raw, high, low = pieces[i]
                                pool.wait_ge(S["w_high"], i + 1)
                                minus_high(pool, low, raw, high).then_inc(S["w_low"], 1)

                        if main:
                            rows_low(1, 1)
                        else:
                            pool.memset(c_next[:], 0.0).then_inc(S["c_parts"], 1)
                            weights_low([0, 1])
                        for i in range(TILES_ALL):
                            if prep and i == CUT_NEXT:
                                rows_low(0, 2 if main else 1)
                            if main:
                                m = rows_of[i % FT]
                                pool.wait_ge(S["high"], i + 1)
                                minus_high(pool, act_low[i % 3][0:m, :], acts[i % 2][0:m, :], act_high[i % 3][0:m, :]) \
                                    .then_inc(S["low"], 1)
                        if not main:
                            weights_low(range(2, len(pieces)))

                    @block.vector
                    def _(dve):
                        ch = Chain(dve, S["dve"])
                        tt, link = dve.tensor_tensor, ch.link

                        def rank_of(out, v, count):
                            step = 2 * (E0 // count) ** 2
                            for n in range(0, NT, min(step, NT)):
                                some = slice(n, n + min(step, NT))
                                shape4 = [P, min(step, NT), count, count]
                                a, q = [w[:, 0:shape4[1] * count * count].rearrange("p (n o m) -> p n o m", o=count, m=count)
                                        for w in (ahead, tied)]
                                other = v[:, some].unsqueeze(2).to_broadcast(shape4)
                                mine = v[:, some].unsqueeze(3).to_broadcast(shape4)
                                yield ch.did(tt(a, other, mine, ALU.is_gt))
                                yield link(tt(q, other, mine, ALU.is_equal))
                                yield link(tt(q, q, below[:, 0:count, 0:count].unsqueeze(1).to_broadcast(shape4), ALU.mult))
                                yield link(tt(a, a, q, ALU.add))
                                yield link(dve.tensor_reduce(out[:, some], a, axis=AX, op=ALU.add))

                        def routes():
                            dve.wait_ge(S["scores"], 1)
                            link(tt(biased[:], scores[:], bias[:].unsqueeze(1).to_broadcast([P, NT, E0]), ALU.add))
                            v = biased[:].rearrange("p n (g w v) -> p (n g) w v", g=NG, v=2)
                            ch.did(tt(pair_max[:], v[:, :, :, 0], v[:, :, :, 1], ALU.max))
                            yield link(tt(pair_sum[:], v[:, :, :, 0], v[:, :, :, 1], ALU.add))
                            ch.did(tt(top_a[:], pair_max[:, :, 0], pair_max[:, :, 1], ALU.add))
                            link(tt(top_b[:], pair_sum[:, :, 0], pair_sum[:, :, 1], ALU.max))
                            yield link(tt(group_score[:].rearrange("p n g -> p (n g)"), top_a[:], top_b[:], ALU.max))
                            for _ in rank_of(rank[:, :, 0:NG], group_score[:], NG):
                                pass
                            link(dve.tensor_scalar(chosen[:, :, 0:NG], rank[:, :, 0:NG], float(TOP_GROUPS), None, ALU.is_lt))
                            yield link(tt(masked[:].rearrange("p n (g w) -> p n g w", g=NG),
                                          biased[:].rearrange("p n (g w) -> p n g w", g=NG),
                                          chosen[:, :, 0:NG].unsqueeze(3).to_broadcast([P, NT, NG, EG]), ALU.mult))
                            yield from rank_of(rank[:], masked[:], E0)
                            link(dve.tensor_scalar(chosen[:], rank[:], float(TOP), None, ALU.is_lt))
                            yield link(tt(masked[:], scores[:], chosen[:], ALU.mult))
                            link(dve.tensor_reduce(total[:], masked[:], axis=AX, op=ALU.add))
                            yield link(dve.tensor_scalar(total[:], total[:], 1e-20, None, ALU.add))
                            link(dve.reciprocal(inverse[:], total[:]))
                            tt(combine[:], masked[:], inverse[:].unsqueeze(2).to_broadcast([P, NT, E0]), ALU.mult) \
                                .then_inc(S["combine"], 1)

                        def cut_weights():
                            if not main:
                                dve.wait_ge(S["c_parts"], 1)
                            for c in range(2):
                                cols = slice(c * BANK, (c + 1) * BANK)
                                dve.wait_ge(S["cT"], c + 1)
                                yield link(dve.tensor_copy(c_next[0:E0, cols], ps[0:E0, 7, :]))
                                yield tt(c_rest[:, cols], ps[0:E0, 7, :], c_next[0:E0, cols], ALU.subtract) \
                                    .then_inc(S["c_rest"], 1)
                                dve.wait_ge(S["c_rest"], c + 1)
                                yield link(dve.tensor_copy(c_mid[:, cols], c_rest[:, cols]))
                                ch.did(dve.tensor_copy(c_next[32:32 + E0, cols], c_mid[:, cols]))
                                yield ch.did(tt(c_next[64:64 + E0, cols], c_rest[:, cols], c_mid[:, cols], ALU.subtract))

                        def add_y(c):
                            dve.wait_ge(S["turned"], c + 1)
                            dst = x_all[:, bass.ds(b * NT + 4 * c, 4), :]
                            tt(dst, dst, ps[:, 7, :].rearrange("p (n d) -> p n d", d=P), ALU.add).then_inc(S["added"], 1)

                        if main:
                            dve.tensor_copy(c_parts[:], c_next[:]).then_inc(S["c_parts"], 1)
                            dve.wait_ge(S["c_parts"], 1)
                            link(dve.tensor_copy(gb_col[:], cur_cols[:, 5:6]))
                        normed = norm_steps(dve, S, ahead_of, 0) if prep else iter(())
                        routed_steps = routes() if prep else iter(())
                        weight_steps = cut_weights() if prep else iter(())
                        if not main:
                            for _ in normed:
                                pass
                        routed = 0
                        for i in range(TILES_ALL + 4):
                            if main and i < TILES_ALL:
                                j = i % FT
                                m = rows_of[j]
                                dve.wait_ge(S["silu"], i + 1)
                                dve.wait_ge(S["up"], i + 1)
                                if i >= 2:
                                    dve.wait_ge(S["low"], i - 1)
                                if j < ROUTED:
                                    tt(prod[i % 2][:], gated[i % 2][:], ps[:, 2 + i % 2, :], ALU.mult).then_inc(S["prod"], 1)
                                    routed += 1
                                    dve.wait_ge(S["prod"], routed)
                                    tt(acts[i % 2][:], prod[i % 2][:], ps[:, 4 + i % 2, :], ALU.mult).then_inc(S["act"], 1)
                                else:
                                    tt(acts[i % 2][0:m, :], gated[i % 2][0:m, :], ps[0:m, 2 + i % 2, :], ALU.mult) \
                                        .then_inc(S["act"], 1)
                            next(normed, None)
                            if i > slots["logits", 0]:
                                next(routed_steps, None)
                            if i == slots["weights", 0]:
                                for _ in routed_steps:
                                    pass
                            if slots["weights", 0] <= i:
                                next(weight_steps, None)
                            for what, c in at(i - 1, "out"):
                                add_y(c)
                S.end()

            S = batch_phase("ffn", "h_high", "h_low", "gate", "up", "silu", "prod", "act", "high", "low", "down", "yT",
                            "turned", "added", "logits", "scores", "combine", "cT", "c_rest", "c_parts", "w_high", "w_low", "dve")
            experts(None, 0)
            with nc.Fori(0, B - 1) as b:
                experts(b, b + 1)
            experts(B - 1, None)

        ffn_own.close()

        HT = HID // P
        CHOICES = K * TILES
        assert ROOM == T and CHOICES * E1 == BANK and SLOTS == K * TOKENS
        with ExitStack() as own:
            gates = sb("gates", [P, K, TILES], stack=own)

            with ExitStack() as inner:
                qT = sb("qT", [P, T], stack=inner)
                qT_end = sb("qT_end", [P, T], stack=inner)
                h_start = sb("h_start", [P, NT, P], stack=inner)
                gate_row = sb("gate_row", [P, P], stack=inner)
                vals = sb("vals", [P, NT, P], stack=inner)
                near = sb("near", [P, NT, P], stack=inner)
                state = sb("state", [P, NT, P], stack=inner)
                shift_row = sb("shift_row", [P, P], stack=inner)
                second = NormBuffers("ln2", cols=sb("cols2", [P, 6], stack=inner), xb=sb("xb2", [P, NT, P], stack=inner),
                                     xn=sb("xn2", [P, NT, P], stack=inner), hT=sb("hT2", [P, T], stack=inner),
                                     stats=sb("stats2", [P, NT, 6], stack=inner), mv=sb("mv2", [P, NT, 2], stack=inner),
                                     ln=sb("ln2", [P, 8, NT], stack=inner))

                def small(name, *shp, dt=F32):
                    return sb(name, [P, *shp], dt, stack=inner)

                router1 = small("router1", E1)
                h_rows = small("h_rows", TILES, ROW)
                h_now = small("h_now", NT, ROW)
                to_slot_now = small("to_slot_now", NT, dt=U32)
                logit = small("logit", TILES, E1)
                before32 = small("before32", P)
                before = small("before", P, dt=BF16)
                ones = small("ones", P, dt=BF16)
                expert_id = small("expert_id", E1)
                priority = small("priority", E1)
                spill = small("spill", CHOICES)
                scan_ones = small("scan_ones", TILES)
                taken = small("taken", E1)
                best = small("best", K, TILES)
                match = small("match", TILES, E1)
                lowest = small("lowest", TILES)
                choice = small("choice", K, TILES, E1)
                choice_bf = small("choice_bf", TILES, E1, dt=BF16)
                counts = small("counts", 2, NT, E1)
                others = small("others", TILES, E1)
                ratio = small("ratio", TILES)
                through = small("through", TILES, E1)
                place = small("place", TILES, E1)
                loc = small("loc", TILES)
                expert = small("expert", TILES)
                valid = small("valid", CHOICES)
                target = small("target", TILES)
                clipped = small("clipped", TILES)
                to_slot = small("to_slot", TILES, dt=U32)

                def choose(ch, n, source, largest, chosen):
                    tt, link = ch.eng.tensor_tensor, ch.link
                    link(ch.eng.tensor_reduce(largest, source, axis=AX, op=ALU.max))
                    link(tt(match[:, 0:n], source, largest.unsqueeze(2).to_broadcast([P, n, E1]), ALU.is_equal))
                    link(tt(match[:, 0:n], match[:, 0:n], priority[:].unsqueeze(1).to_broadcast([P, n, E1]), ALU.mult))
                    link(ch.eng.tensor_reduce(lowest[:, 0:n], match[:, 0:n], axis=AX, op=ALU.max))
                    link(tt(chosen, match[:, 0:n], lowest[:, 0:n].unsqueeze(2).to_broadcast([P, n, E1]), ALU.is_equal))

                def put(ch, n, chosen, earlier, totals, columns, targets):
                    tt, ts, link = ch.eng.tensor_tensor, ch.eng.tensor_scalar, ch.link
                    for e in range(E1):
                        ch.did(ch.eng.tensor_tensor_scan(through[:, 0:n, e], scan_ones[:, 0:n], totals[:, :, e], 0.0,
                                                         ALU.mult, ALU.add))
                    ch.wait()
                    link(tt(place[:, 0:n], through[:, 0:n], totals, ALU.subtract))
                    link(tt(place[:, 0:n], place[:, 0:n], earlier, ALU.add))
                    link(tt(place[:, 0:n], place[:, 0:n], taken[:].unsqueeze(1).to_broadcast([P, n, E1]), ALU.add))
                    link(tt(taken[:], taken[:], through[:, n - 1], ALU.add))
                    link(tt(place[:, 0:n], place[:, 0:n], chosen, ALU.mult))
                    link(ch.eng.tensor_reduce(loc[:, 0:n], place[:, 0:n], axis=AX, op=ALU.add))
                    link(tt(place[:, 0:n], chosen, expert_id[:].unsqueeze(1).to_broadcast([P, n, E1]), ALU.mult))
                    link(ch.eng.tensor_reduce(expert[:, 0:n], place[:, 0:n], axis=AX, op=ALU.add))
                    link(ts(valid[:, columns], loc[:, 0:n], float(ROOM), None, ALU.is_lt))
                    link(ts(clipped[:, 0:n], loc[:, 0:n], float(ROOM - 1), None, ALU.min))
                    link(ch.eng.scalar_tensor_tensor(clipped[:, 0:n], expert[:, 0:n], float(ROOM), clipped[:, 0:n],
                                                     ALU.mult, ALU.add))
                    link(ts(target[:, 0:n], spill[:, columns], float(SLOTS), None, ALU.add))
                    link(tt(clipped[:, 0:n], clipped[:, 0:n], target[:, 0:n], ALU.subtract))
                    link(tt(clipped[:, 0:n], clipped[:, 0:n], valid[:, columns], ALU.mult))
                    link(tt(clipped[:, 0:n], clipped[:, 0:n], target[:, 0:n], ALU.add))
                    return ch.eng.tensor_copy(targets, clipped[:, 0:n])

                S = batch_phase("lin", *[f"ln2_{n[3:]}" for n in LN], "qT", "qT_sb", "dve", "vals", "vals_sb", "near", "near_sb",
                                "pairs", "states", "y", "in", "logits", "chosen", "counts", "h_now", "h_kept", "placed")
                rows_sent = ctx.enter_context(nc.semaphore("rows_sent"))

                def send(pool, source, targets, n):
                    pool.indirect_dma_start(slots_dram, bass.IndirectOffsetOnAxis(ap=targets[:, n:n + 1], axis=0),
                                            source[:, n, :], None).then_inc(rows_sent, 16)

                def place_first(ch, p):
                    tiles = bass.ds(p * NT, NT)
                    return put(ch, NT, choice[:, 0, tiles, :], counts[:, 0], counts[:, 1], tiles, to_slot_now[:])

                def linear(n, b, m, p):
                    with nc.Block() as block:
                        @block.tensor
                        def _(pe):
                            if b is not None:
                                for c in range(2):
                                    last = pe.matmul(ps[:, 2 + c, :], qk_w[:], hT[:, c * BANK:(c + 1) * BANK], start=True, stop=True)
                                last.then_inc(S["qT"], 1)
                                for i in range(NT):
                                    last = pe.matmul(ps[:, 6 + i // 4, (i % 4) * P:(i % 4 + 1) * P], hT[:, i * P:(i + 1) * P], vo_w[:],
                                                     start=True, stop=True)
                                last.then_inc(S["vals"], 1)
                                pe.wait_ge(S["qT_sb"], 1)
                                for i in range(NT):
                                    cols = slice(i * P, (i + 1) * P)
                                    last = pe.matmul(ps[:, 4 + i // 4, (i % 4) * P:(i % 4 + 1) * P], hT[:, cols], qT[:, cols],
                                                     start=True, stop=True)
                                last.then_inc(S["near"], 1)
                                pe.wait_ge(S["vals_sb"], 1)
                                for i in range(NT):
                                    last = pe.matmul(ps[:, i // 4, (i % 4) * P:(i % 4 + 1) * P], h_start[:, i, :], vals[:, i, :],
                                                     start=True, stop=True)
                                last.then_inc(S["pairs"], 1)
                            if b is not None:
                                pe.wait_ge(S["near_sb"], 1)
                                pe.wait_ge(S["states"], 1)
                                for i in range(NT):
                                    out = ps[:, 2 + i // 4, (i % 4) * P:(i % 4 + 1) * P]
                                    last = pe.matmul(out, near[:, i, :], vals[:, i, :], start=True, stop=(i == NT - 1))
                                    if i < NT - 1:
                                        last = pe.matmul(out, qT_end[:, i * P:(i + 1) * P], state[:, i, :], start=False, stop=True)
                                last.then_inc(S["y"], 1)
                            if m is not None:
                                norm_tensor(pe, S, second, 6)
                            if n is not None:
                                norm_tensor(pe, S)
                            if m is not None:
                                pe.wait_ge(S["ln2_hT"], 1)
                                for i in range(NT):
                                    last = pe.matmul(ps[:, 4, i * E1:(i + 1) * E1], second.hT[:, i * P:(i + 1) * P], router1[:],
                                                     start=True, stop=True)
                                last.then_inc(S["logits"], 1)
                                pe.wait_ge(S["chosen"], 1)
                                flat = choice_bf[:, 0:NT].rearrange("p n e -> p (n e)")
                                pe.matmul(ps[:, 5, 0:NT * E1], before[:], flat, start=True, stop=True)
                                pe.matmul(ps[:, 5, NT * E1:2 * NT * E1], ones[:], flat, start=True, stop=True).then_inc(S["counts"], 1)

                        @block.scalar
                        def _(act):
                            if b is not None:
                                act.wait_ge(S["qT"], 1)
                                act.activation(qT[:], ps[:, 2:4, :].rearrange("p a n -> p (a n)"), ACT.Copy).then_inc(S["qT_sb"], 1)
                            if m is not None:
                                norm_root(act, S, second)
                            if n is not None:
                                norm_root(act, S)
                            if m is not None:
                                norm_rows(act, S, 3, 4, second, 6)
                                act.wait_ge(S["h_now"], 1)
                                act.activation(h_rows[:, bass.ds(m * NT, NT), :], h_now[:], ACT.Copy).then_inc(S["h_kept"], 1)
                            if n is not None:
                                norm_rows(act, S, 0, 1)

                        @block.vector
                        def _(dve):
                            ch = Chain(dve, S["dve"])
                            tt, link = dve.tensor_tensor, ch.link
                            row = lambda i, v: mod1_rows[:].rearrange("p b v d -> p (b v) d")[:, bass.ds(i * 6 + v, 1), :]
                            all_tiles = lambda ap: ap.to_broadcast([P, NT, P])
                            wide = lambda first: ps[:, first:first + 2, :].rearrange("p a (n d) -> p (a n) d", d=P)

                            def some(steps, count=NT + 8):
                                for _ in range(count):
                                    next(steps, None)

                            norm1 = norm_steps(dve, S, n, 1) if n is not None else iter(())
                            norm2 = norm_steps(dve, S, m, 1, second) if m is not None else iter(())
                            if b is not None:
                                ch.did(dve.tensor_scalar(gate_row[:].unsqueeze(1), row(b, 2), out_scale[:], None, ALU.mult))
                                ch.did(dve.tensor_scalar(shift_row[:].unsqueeze(1), row(b, 0), start_powers[:], None, ALU.mult))
                                link(dve.scalar_tensor_tensor(h_start[:], xn[:], start_powers[:], all_tiles(row(b, 1)), ALU.mult, ALU.mult))
                                link(tt(h_start[:], h_start[:], all_tiles(shift_row[:].unsqueeze(1)), ALU.add))
                                some(norm2, 3)
                                if p is not None:
                                    place_first(ch, p).then_inc(S["placed"], 1)
                                dve.wait_ge(S["vals"], 1)
                                tt(vals[:], wide(6), all_tiles(gate_row[:].unsqueeze(1)), ALU.mult).then_inc(S["vals_sb"], 1)
                                some(norm2, 1)
                                dve.wait_ge(S["qT_sb"], 1)
                                link(tt(qT_end[:].rearrange("p (n q) -> p n q", q=P), qT[:].rearrange("p (n q) -> p n q", q=P),
                                        all_tiles(end_powers[:].unsqueeze(1)), ALU.mult))
                                dve.wait_ge(S["near"], 1)
                                tt(near[:], wide(4), all_tiles(mask[:].unsqueeze(1)), ALU.mult).then_inc(S["near_sb"], 1)
                                some(norm1, 4)
                                dve.wait_ge(S["pairs"], 1)
                                pair = lambda i: ps[:, i // 4, (i % 4) * P:(i % 4 + 1) * P]
                                link(dve.tensor_copy(state[:, NT - 2, :], pair(NT - 1)))
                                for i in range(NT - 2, 0, -1):
                                    ins = dve.scalar_tensor_tensor(state[:, i - 1, :], state[:, i, :], chunk_power[:], pair(i),
                                                                   ALU.mult, ALU.add)
                                    if i > 1:
                                        link(ins)
                                ins.then_inc(S["states"], 1)
                            elif p is not None:
                                place_first(ch, p).then_inc(S["placed"], 1)
                            some(norm2)
                            some(norm1)
                            if m is not None:
                                dve.wait_ge(S["ln2_xn"], NT)
                                if p is not None:
                                    dve.wait_ge(rows_sent, (p + 1) * (16 * NT))
                                ch.did(dve.tensor_scalar(h_now[:, :, NUMBER], spill[:, bass.ds(m * NT, NT)], 1.0, None, ALU.add))
                                link(tt(h_now[:, :, 0:P], second.xn[:], all_tiles(row(m, 4)), ALU.mult))
                                tt(h_now[:, :, 0:P], h_now[:, :, 0:P], all_tiles(row(m, 3)), ALU.add).then_inc(S["h_now"], 1)
                            if b is not None:
                                dve.wait_ge(S["y"], 1)
                                dst = x_all[:, bass.ds(b * NT, NT), :]
                                link(tt(dst, dst, wide(2), ALU.add))
                            if m is None and b is not None:
                                ch.did(dve.memset(ones[:], 1.0))
                                ch.did(dve.memset(h_now[:], 0.0))
                                ch.did(dve.memset(scan_ones[:], 1.0))
                                ch.did(dve.memset(taken[:], 0.0))
                                dve.wait_ge(S["in"], 64)
                                ch.did(dve.tensor_copy(before[:], before32[:]))
                                ch.did(dve.tensor_scalar(priority[:], expert_id[:], -1.0, float(E1), ALU.mult, ALU.add))
                            elif m is not None:
                                tiles = bass.ds(m * NT, NT)
                                dve.wait_ge(S["logits"], 1)
                                link(dve.tensor_copy(logit[:, tiles, :], ps[:, 4, 0:NT * E1].rearrange("p (n e) -> p n e", e=E1)))
                                choose(ch, NT, logit[:, tiles, :], best[:, 0, tiles], choice[:, 0, tiles, :])
                                dve.tensor_copy(choice_bf[:, 0:NT], choice[:, 0, tiles, :]).then_inc(S["chosen"], 1)
                                dve.wait_ge(S["counts"], 1)
                                ch.did(dve.tensor_copy(counts[:].rearrange("p k n e -> p (k n e)"), ps[:, 5, 0:2 * NT * E1]))

                        @block.sync
                        def _(sp):
                            if m is None and b is not None:
                                for dst, n in ((router1, "router1"), (before32, "before"), (expert_id, "expert_id"), (spill, "spill")):
                                    sp.dma_start(dst[:], t[n]).then_inc(S["in"], 16)
                                sp.wait_ge(S["in"], 64)

                        @block.gpsimd
                        def _(pool):
                            if p is not None:
                                pool.wait_ge(S["placed"], 1)
                                for i in range(NT):
                                    send(pool, h_now, to_slot_now, i)
                                pool.wait_ge(rows_sent, (p + 1) * (16 * NT))
                    S.end()

                linear(0, None, None, None)
                linear(1, 0, None, None)
                linear(2, 1, 0, None)
                with nc.Fori(2, B - 1) as b:
                    linear(b + 1, b, b - 1, b - 2)
                linear(None, B - 1, B - 2, B - 3)
                linear(None, None, B - 1, B - 2)

                S = phase("t_dve", "t_ratio", "t_exp", "t_chosen", "t_counts", "t_first", "t_placed")
                with nc.Block() as block:
                    @block.vector
                    def _(dve):
                        ch = Chain(dve, S["t_dve"])
                        tt, link = dve.tensor_tensor, ch.link
                        place_first(ch, B - 1).then_inc(S["t_first"], 1)
                        dve.wait_ge(S["t_first"], 1)
                        ch.did(dve.tensor_scalar(h_rows[:, :, NUMBER], spill[:, TILES:CHOICES], 1.0, None, ALU.add))
                        link(dve.scalar_tensor_tensor(others[:].rearrange("p n e -> p (n e)"),
                                                      choice[:, 0].rearrange("p n e -> p (n e)"), -1e30,
                                                      logit[:].rearrange("p n e -> p (n e)"), ALU.mult, ALU.add))
                        choose(ch, TILES, others[:], best[:, 1, :], choice[:, 1])
                        dve.tensor_copy(choice_bf[:], choice[:, 1]).then_inc(S["t_chosen"], 1)
                        tt(ratio[:], best[:, 1, :], best[:, 0, :], ALU.subtract).then_inc(S["t_ratio"], 1)
                        dve.wait_ge(S["t_counts"], 1)
                        in_tile = lambda bank: ps[:, bank, 0:TILES * E1].rearrange("p (n e) -> p n e", e=E1)
                        put(ch, TILES, choice[:, 1], in_tile(0), in_tile(1), slice(TILES, CHOICES), to_slot[:]) \
                            .then_inc(S["t_placed"], 1)
                        dve.wait_ge(S["t_exp"], 1)
                        link(dve.tensor_scalar(lowest[:], ratio[:], 1.0, None, ALU.add))
                        link(dve.reciprocal(gates[:, 0, :], lowest[:]))
                        link(tt(gates[:, 1, :], gates[:, 0, :], ratio[:], ALU.mult))
                        link(tt(gates[:].rearrange("p k n -> p (k n)"), gates[:].rearrange("p k n -> p (k n)"), valid[:], ALU.mult))

                    @block.scalar
                    def _(act):
                        act.wait_ge(S["t_ratio"], 1)
                        act.activation(ratio[:], ratio[:], ACT.Exp).then_inc(S["t_exp"], 1)

                    @block.tensor
                    def _(pe):
                        pe.wait_ge(S["t_chosen"], 1)
                        flat = choice_bf[:].rearrange("p n e -> p (n e)")
                        pe.matmul(ps[:, 0, 0:TILES * E1], before[:], flat, start=True, stop=True)
                        pe.matmul(ps[:, 1, 0:TILES * E1], ones[:], flat, start=True, stop=True).then_inc(S["t_counts"], 1)

                    @block.gpsimd
                    def _(pool):
                        pool.wait_ge(S["t_first"], 1)
                        for n in range(NT):
                            send(pool, h_now, to_slot_now, n)
                        pool.wait_ge(S["t_placed"], 1)
                        for n in range(TILES):
                            send(pool, h_rows, to_slot, n)
                        pool.wait_ge(rows_sent, 16 * CHOICES)
                S.end()

            w_raw = [sb(f"w_raw{i}", [P, 2, HID], stack=own) for i in range(2)]
            slots_raw = [sb(f"slots_raw{i}", [P, ST, ROW], stack=own) for i in range(2)]
            w_parts = [[sb(f"w_parts{i}{h}", [P, 2, HID], F32R, stack=own) for h in range(2)] for i in range(2)]
            slotsT = [[sb(f"slotsT{i}{h}", [P, ROOM], F32R, stack=own) for h in range(2)] for i in range(2)]
            hid = sb("hid", [P, HT, ROOM], stack=own)
            hid_parts = [sb(f"hid_parts{h}", [P, HT, ROOM], F32R, stack=own) for h in range(2)]
            outT = [sb(f"outT{i}", [P, ROOM], stack=own) for i in range(2)]
            slot_out = [sb(f"slot_out{i}", [P, ST, P], stack=own) for i in range(2)]
            b1 = sb("b1", [P, E1, HT], stack=own)
            b2 = sb("b2", [P, E1], stack=own)
            slot_junk = sb("slot_junk", [P, E1 * ST], stack=own)
            nobody = sb("nobody", [P, ST], stack=own)
            targets_next = [sb(f"targets_next{i}", [P, ST], U32, stack=own) for i in range(2)]
            targets = [sb(f"targets{i}", [P, ST], U32, stack=own) for i in range(2)]
            cur_b1 = [sb(f"cur_b1_{i}", [P, HT], stack=own) for i in range(2)]
            cur_b2 = [sb(f"cur_b2_{i}", [P, 1], stack=own) for i in range(2)]
            turned_ps = ps[:, 0:2, :].rearrange("p a n -> p (a n)")

            def load_expert(sp, e, i, sem):
                sp.dma_start(w_raw[i][:, 0, :], t["w1"][e]).then_inc(sem, 16)
                sp.dma_start(w_raw[i][:, 1, :].rearrange("p (j d) -> p j d", d=P), t["w2"][e].rearrange("(j p) d -> p j d", p=P)) \
                    .then_inc(sem, 16)
                sp.dma_start(slots_raw[i][:], slots_dram[bass.ds(e * ROOM, ROOM)].rearrange("(n p) d -> p n d", p=P)) \
                    .then_inc(sem, 16)

            def find_targets(ch, e, i):
                numbers = slots_raw[i][:, :, NUMBER]
                ch.link(ch.eng.tensor_scalar(nobody[:], numbers, 0.0, None, ALU.is_equal))
                ch.link(ch.eng.tensor_tensor(nobody[:], nobody[:], slot_junk[:, bass.ds(e * ST, ST)], ALU.mult))
                ch.link(ch.eng.tensor_tensor(nobody[:], nobody[:], numbers, ALU.add))
                ch.link(ch.eng.tensor_scalar(targets_next[i][:], nobody[:], 1.0, None, ALU.subtract))

            def send_outputs(pool, i, to, tiles=range(ST)):
                for n in tiles:
                    pool.indirect_dma_start(outs_dram, bass.IndirectOffsetOnAxis(ap=to[i][:, n:n + 1], axis=0),
                                            slot_out[i][:, n, :], None).then_inc(outs_sent, 16)

            def turn(pe, tiles, at=0):
                for n, tile in enumerate(tiles, at):
                    last = pe.transpose(ps[:, n // 4, (n % 4) * P:(n % 4 + 1) * P], tile, ident[:])
                return last

            E_SEMS = ("in1", "in0", "bias", "slots_turned", "out_turned", "w_high", "w_low", "slots_high", "slots_low",
                      "hid_ps", "hid_high", "hid", "low_pool", "low_dve", "out_ps", "outT", "out_copied", "targets", "dve")
            outs_sent = ctx.enter_context(nc.semaphore("outs_sent"))
            S = phase(*[f"e_{n}" for n in E_SEMS])
            S.by_name = {n[2:]: h for n, h in S.by_name.items()}

            BY_POOL = [(0, 1), (1, 0)]
            BY_DVE = [(i, j) for i in range(2) for j in range(HT) if (i, j) not in BY_POOL]

            def low_done(i, j):
                by, name = (BY_POOL, "low_pool") if (i, j) in BY_POOL else (BY_DVE, "low_dve")
                return S[name], by.index((i, j)) + 1

            def cut_hidden(eng, i, j):
                eng.wait_ge(S["hid_high"], i * HT + j + 1)
                minus_high(eng, hid_parts[1][:, j, :], hid[:, j, :], hid_parts[0][:, j, :]).then_inc(low_done(i, j)[0], 1)

            def expert_pass(e0, first, last):
                with nc.Block() as block:
                    @block.sync
                    def _(sp):
                        load_expert(sp, e0 + 1, 1, S["in1"])
                        if not last:
                            load_expert(sp, e0 + 2, 0, S["in0"])

                    @block.tensor
                    def _(pe):
                        def hidden(i, j):
                            q = i * HT + j
                            if q >= 2:
                                pe.wait_ge(S["hid"], q - 1)
                            for c in range(2):
                                last_one = product(pe, ps[:, 2 + 2 * (q % 2) + c, :], [w[:, 0, j * P:(j + 1) * P] for w in w_parts[i]],
                                                   [s[:, c * BANK:(c + 1) * BANK] for s in slotsT[i]])
                            last_one.then_inc(S["hid_ps"], 1)

                        def outputs(i):
                            for j in range(HT):
                                pe.wait_ge(*low_done(i, j))
                                if i and j == 0:
                                    pe.wait_ge(S["outT"], 2)
                                for c in range(2):
                                    ins = product(pe, ps[:, 6 + c, :], [w[:, 1, j * P:(j + 1) * P] for w in w_parts[i]],
                                                  [h[:, j, c * BANK:(c + 1) * BANK] for h in hid_parts],
                                                  start=(j == 0), stop=(j == HT - 1))
                                    if j == HT - 1:
                                        ins.then_inc(S["out_ps"], 1)

                        def turn_slots(i):
                            turn(pe, [slots_raw[i][:, n, 0:P] for n in range(ST)]).then_inc(S["slots_turned"], 1)

                        def turn_out(i):
                            turn(pe, [outT[i][:, n * P:(n + 1) * P] for n in range(ST)]).then_inc(S["out_turned"], 1)

                        before = 0 if first else 1
                        if not first:
                            turn_out(1)
                        for j in range(HT):
                            hidden(0, j)
                        pe.wait_ge(S["in1"], 48)
                        if not first:
                            pe.wait_ge(S["out_copied"], 1)
                        turn_slots(1)
                        outputs(0)
                        pe.wait_ge(S["w_low"], 1)
                        pe.wait_ge(S["slots_low"], 1)
                        hidden(1, 0)
                        hidden(1, 1)
                        pe.wait_ge(S["outT"], 2)
                        turn_out(0)
                        hidden(1, 2)
                        hidden(1, 3)
                        if not last:
                            pe.wait_ge(S["in0"], 48)
                            pe.wait_ge(S["out_copied"], before + 1)
                            turn_slots(0)
                        pe.wait_ge(S["w_low"], 2)
                        outputs(1)

                    @block.scalar
                    def _(act):
                        def hid_high(i, j):
                            q = i * HT + j
                            act.wait_ge(S["hid"], q + 1)
                            if i:
                                act.wait_ge(S["out_ps"], 2)
                            act.activation(hid_parts[0][:, j, :], hid[:, j, :], ACT.Copy).then_inc(S["hid_high"], 1)

                        def weights_high(i, w):
                            act.activation(w_parts[i][0][:, w, :], w_raw[i][:, w, :], ACT.Copy).then_inc(S["w_high"], 1)

                        def slots_high(i, count):
                            act.wait_ge(S["slots_turned"], count)
                            act.activation(slotsT[i][0][:], turned_ps, ACT.Copy).then_inc(S["slots_high"], 1)

                        def copy_out(i):
                            for c in range(2):
                                act.wait_ge(S["out_ps"], 2 * i + c + 1)
                                act.activation(outT[i][:, c * BANK:(c + 1) * BANK], ps[:, 6 + c, :], ACT.Identity, bias=cur_b2[i][:]) \
                                    .then_inc(S["outT"], 1)

                        def copy_turned(i, count):
                            act.wait_ge(S["out_turned"], count)
                            act.activation(slot_out[i][:].rearrange("p n d -> p (n d)"), turned_ps, ACT.Copy) \
                                .then_inc(S["out_copied"], 1)

                        if not first:
                            copy_turned(1, 1)
                        act.wait_ge(S["bias"], 4)
                        hid_high(0, 0)
                        hid_high(0, 1)
                        act.wait_ge(S["in1"], 48)
                        weights_high(1, 0)
                        hid_high(0, 2)
                        hid_high(0, 3)
                        weights_high(1, 1)
                        slots_high(1, 1)
                        copy_out(0)
                        hid_high(1, 0)
                        hid_high(1, 1)
                        copy_turned(0, 1 if first else 2)
                        if not last:
                            act.wait_ge(S["in0"], 48)
                            weights_high(0, 0)
                        hid_high(1, 2)
                        hid_high(1, 3)
                        if not last:
                            weights_high(0, 1)
                            slots_high(0, 2)
                        copy_out(1)

                    @block.vector
                    def _(dve):
                        def hid_full(i, j):
                            q = i * HT + j
                            dve.wait_ge(S["hid_ps"], q + 1)
                            if i:
                                dve.wait_ge(*low_done(0, j))
                            dve.tensor_scalar(hid[:, j, :], ps[:, 2 + 2 * (q % 2):4 + 2 * (q % 2), :].rearrange("p a n -> p (a n)"),
                                              cur_b1[i][:, j:j + 1], 0.0, ALU.add, ALU.max).then_inc(S["hid"], 1)

                        def weights_low(i, w, count):
                            dve.wait_ge(S["w_high"], count)
                            minus_high(dve, w_parts[i][1][:, w, :], w_raw[i][:, w, :], w_parts[i][0][:, w, :]).then_inc(S["w_low"], 1)

                        def slots_low(i, count):
                            dve.wait_ge(S["slots_high"], count)
                            minus_high(dve, slotsT[i][1][:], turned_ps, slotsT[i][0][:]).then_inc(S["slots_low"], 1)

                        for i in range(2):
                            dve.tensor_copy(cur_b1[i][:].unsqueeze(1), b1[:, bass.ds(e0 + i, 1), :]).then_inc(S["bias"], 1)
                            dve.tensor_copy(cur_b2[i][:], b2[:, bass.ds(e0 + i, 1)]).then_inc(S["bias"], 1)
                            dve.tensor_copy(targets[i][:], targets_next[i][:]).then_inc(S["targets"], 1)
                        own_steps = Chain(dve, S["dve"])
                        dve.wait_ge(S["bias"], 4)
                        hid_full(0, 0)
                        hid_full(0, 1)
                        weights_low(1, 0, 1)
                        cut_hidden(dve, 0, 0)
                        hid_full(0, 2)
                        hid_full(0, 3)
                        cut_hidden(dve, 0, 2)
                        cut_hidden(dve, 0, 3)
                        weights_low(1, 1, 2)
                        slots_low(1, 1)
                        hid_full(1, 0)
                        hid_full(1, 1)
                        if not last:
                            weights_low(0, 0, 3)
                        hid_full(1, 2)
                        cut_hidden(dve, 1, 1)
                        hid_full(1, 3)
                        cut_hidden(dve, 1, 2)
                        cut_hidden(dve, 1, 3)
                        if not last:
                            weights_low(0, 1, 4)
                            slots_low(0, 2)
                        dve.wait_ge(S["targets"], 2)
                        dve.wait_ge(S["in1"], 48)
                        find_targets(own_steps, e0 + 1, 1)
                        if not last:
                            dve.wait_ge(S["in0"], 48)
                            find_targets(own_steps, e0 + 2, 0)

                    @block.gpsimd
                    def _(pool):
                        pool.wait_ge(S["targets"], 2)
                        if not first:
                            pool.wait_ge(S["out_copied"], 1)
                            send_outputs(pool, 1, targets, range(ST // 2))
                        cut_hidden(pool, 0, 1)
                        if not first:
                            send_outputs(pool, 1, targets, range(ST // 2, ST))
                        cut_hidden(pool, 1, 0)
                        pool.wait_ge(S["out_copied"], 1 if first else 2)
                        send_outputs(pool, 0, targets)
                        pool.wait_ge(outs_sent, (e0 + 1) * (16 * ST))
                S.end()

            with nc.Block() as block:
                @block.sync
                def _(sp):
                    load_expert(sp, 0, 0, S["in0"])
                    sp.dma_start(b1[:], t["b1"]).then_inc(S["bias"], 16)
                    sp.dma_start(b2[:], t["b2"]).then_inc(S["bias"], 16)
                    sp.dma_start(slot_junk[:], t["slot_junk"]).then_inc(S["bias"], 16)
                    sp.wait_ge(S["bias"], 48)

                @block.tensor
                def _(pe):
                    pe.wait_ge(S["in0"], 48)
                    turn(pe, [slots_raw[0][:, n, 0:P] for n in range(ST)]).then_inc(S["slots_turned"], 1)

                @block.scalar
                def _(act):
                    act.wait_ge(S["in0"], 48)
                    act.activation(w_parts[0][0][:], w_raw[0][:], ACT.Copy).then_inc(S["w_high"], 1)
                    act.wait_ge(S["slots_turned"], 1)
                    act.activation(slotsT[0][0][:], turned_ps, ACT.Copy).then_inc(S["slots_high"], 1)

                @block.vector
                def _(dve):
                    dve.wait_ge(S["w_high"], 1)
                    minus_high(dve, w_parts[0][1][:], w_raw[0][:], w_parts[0][0][:]).then_inc(S["w_low"], 1)
                    dve.wait_ge(S["slots_high"], 1)
                    minus_high(dve, slotsT[0][1][:], turned_ps, slotsT[0][0][:]).then_inc(S["slots_low"], 1)
                    own_steps = Chain(dve, S["dve"])
                    own_steps.did(dve.memset(targets_next[1][:], 0))
                    dve.wait_ge(S["in0"], 48)
                    dve.wait_ge(S["bias"], 48)
                    find_targets(own_steps, 0, 0)
            S.end()

            assert HT == 4 and E1 >= 4 and ST * P == 2 * BANK
            expert_pass(0, True, False)
            with nc.Fori(1, E1 // 2 - 1) as e2:
                expert_pass(e2 * 2, False, False)
            expert_pass(E1 - 2, False, True)

            with nc.Block() as block:
                HALF_ST = ST // 2

                @block.tensor
                def _(pe):
                    for c in range(2):
                        turn(pe, [outT[1][:, n * P:(n + 1) * P] for n in range(c * HALF_ST, (c + 1) * HALF_ST)], c * HALF_ST) \
                            .then_inc(S["out_turned"], 1)

                @block.scalar
                def _(act):
                    for c in range(2):
                        act.wait_ge(S["out_turned"], c + 1)
                        act.activation(slot_out[1][:, c * HALF_ST:(c + 1) * HALF_ST].rearrange("p n d -> p (n d)"), ps[:, c, :],
                                       ACT.Copy).then_inc(S["out_copied"], 1)

                @block.gpsimd
                def _(pool):
                    for c in range(2):
                        pool.wait_ge(S["out_copied"], c + 1)
                        send_outputs(pool, 1, targets_next, range(c * HALF_ST, (c + 1) * HALF_ST))
                    pool.wait_ge(outs_sent, E1 * 16 * ST)
            S.end()

            S = phase(*[f"g_got{b}" for b in range(B)], "g_first", "g_second", "g_dve", "g_stored")
            got = [sb(f"got{b}", [P, K, NT, P], stack=own) for b in range(B)]
            with nc.Block() as block:
                @block.gpsimd
                def _(pool):
                    for b in range(B):
                        pool.wait_ge(S[f"g_got{b}"], 16 * K)
                        r = got[b]
                        pool.tensor_tensor(r[:, 0], r[:, 0], gates[:, 0, b * NT:(b + 1) * NT].unsqueeze(2).to_broadcast([P, NT, P]),
                                           ALU.mult).then_inc(S["g_first"], 1)

                @block.scalar
                def _(act):
                    for b in range(B):
                        act.wait_ge(S[f"g_got{b}"], 16 * K)
                        for n in range(NT):
                            r = got[b][:, 1, n, :]
                            i = b * NT + n
                            act.activation(r, r, ACT.Copy, scale=gates[:, 1, i:i + 1]).then_inc(S["g_second"], 1)

                @block.vector
                def _(dve):
                    ch = Chain(dve, S["g_dve"])
                    for b in range(B):
                        r = got[b]
                        dve.wait_ge(S["g_first"], b + 1)
                        dve.wait_ge(S["g_second"], NT * (b + 1))
                        ch.link(dve.tensor_tensor(r[:, 0], r[:, 0], r[:, 1], ALU.add))
                        ch.link(dve.tensor_tensor(r[:, 0], r[:, 0], mod1_rows[:, b, 5:6, :].to_broadcast([P, NT, P]), ALU.mult))
                        dst = x_all[:, b * NT:(b + 1) * NT, :]
                        ch.link(dve.tensor_tensor(dst, dst, r[:, 0], ALU.add))

                @block.sync
                def _(sp):
                    def load(b):
                        for k in range(K):
                            sp.dma_start(got[b][:, k], outs_dram[k * TOKENS + b * T:k * TOKENS + (b + 1) * T]
                                         .rearrange("(n p) d -> p n d", p=P)).then_inc(S[f"g_got{b}"], 16)

                    for b in range(B):
                        load(b)
                    for b in range(B):
                        sp.wait_ge(S["g_dve"], 3 * (b + 1))
                        sp.dma_start(t["out"][b].rearrange("(n p) d -> p n d", p=P), x_all[:, b * NT:(b + 1) * NT, :]) \
                            .then_inc(S["g_stored"], 16)
                    sp.wait_ge(S["g_stored"], 16 * B)
            S.end()


def kernel(**inputs):
    import concourse.bacc as bacc
    from concourse.bass_utils import run_bass_kernel_spmd

    f = {n: np.asarray(a) for n, a in inputs.items()}
    B, T, _ = f["L0_attn_x"].shape
    E0, I, _ = f["L0_ffn_gate_proj"].shape
    E1, _, HID = f["L1_ffn_w1"].shape
    p = np.arange(P)
    expert_of = np.arange(E0 * I) // I
    owner_rows = np.zeros((3 * 32, E0 * I), np.uint16)
    for w in range(3):
        owner_rows[32 * w:32 * w + E0][expert_of[None, :] == np.arange(E0)[:, None]] = 0x3F80
    below = np.broadcast_to((np.arange(E0)[None, :] < np.arange(E0)[:, None]).astype(np.float32), (P, E0, E0))
    distance = np.maximum(p[:, None] - p[None, :] - 1, 0).astype(np.float32)
    later = (p[:, None] > p[None, :]).astype(np.float32) / np.sqrt(np.float32(P))
    to_end = np.broadcast_to((P - 1 - p).astype(np.float32), (P, P))
    from_start = p[:, None].astype(np.float32)
    before = (p[:, None] < p[None, :]).astype(np.float32)
    expert_id = np.broadcast_to(np.arange(E1, dtype=np.float32), (P, E1))
    slots_of_nobody = 2 * B * T + np.arange(2 * B * T, dtype=np.float32)
    spill = np.arange(2 * B * T, dtype=np.float32).reshape(-1, P).T
    by_index = np.arange(P).reshape(4, 4, P // 16).transpose(0, 2, 1).ravel()
    arrays = {
        "x": f["L0_attn_x"], "ident": np.eye(P, dtype=np.float32),
        "cT0": f["L0_c"].T, "cT1": f["L1_c"].T, "wmod0": f["L0_wmod"], "wmod1": f["L1_wmod"],
        "wq0": f["L0_attn_Wq"].T[:, by_index], "wk0": f["L0_attn_Wk"].T[:, by_index], "wv0": f["L0_attn_Wv"].T,
        "router0": f["L0_ffn_gate_w"].T, "bias0": np.broadcast_to(f["L0_ffn_gate_bias"], (P, E0)),
        "gate0": np.concatenate([f["L0_ffn_gate_proj"].reshape(E0 * I, P), f["L0_ffn_shared_gate_w"]]).T,
        "up0": np.concatenate([f["L0_ffn_up_proj"].reshape(E0 * I, P), f["L0_ffn_shared_up_w"]]).T,
        "down0": np.concatenate([f["L0_ffn_down_proj"].transpose(0, 2, 1).reshape(E0 * I, P),
                                 f["L0_ffn_shared_down_w"].T]),
        "owner": owner_rows, "below": below,
        "wq1": f["L1_attn_Wq"], "wk1": f["L1_attn_Wk"], "wv1": f["L1_attn_Wv"], "wo1": f["L1_attn_Wo"].T,
        "decay": np.broadcast_to(f["L1_attn_decay_logit"].reshape(1, 1), (P, 1)),
        "out_scale": np.broadcast_to(f["L1_attn_out_scale"].reshape(1, 1), (P, 1)),
        "distance": distance, "later": later, "to_end": to_end, "from_start": from_start,
        "router1": f["L1_ffn_wg"], "w1": f["L1_ffn_w1"], "b1": f["L1_ffn_b1"].reshape(E1, HID // P, P).transpose(2, 0, 1),
        "w2": f["L1_ffn_w2"], "b2": f["L1_ffn_b2"].T,
        "slot_junk": 1 + slots_of_nobody.reshape(-1, P).T,
        "before": before, "expert_id": expert_id, "spill": spill,
    }
    arrays = {f"in_{n}_dram": np.ascontiguousarray(a) for n, a in arrays.items()}
    nc = bacc.Bacc("TRN2", target_bir_lowering=False, num_devices=1)
    t = {n[3:-5]: nc.dram_tensor(n, a.shape, mybir.dt.from_np(a.dtype), kind="ExternalInput").ap()
         for n, a in arrays.items()}
    t["out"] = nc.dram_tensor("out_0_dram", (B, T, P), F32, kind="ExternalOutput").ap()
    adaln_program(nc, t, {"B": B, "T": T, "E0": E0, "I": f["L0_ffn_gate_proj"].shape[1],
                          "E1": f["L1_ffn_w1"].shape[0], "HID": f["L1_ffn_w1"].shape[2]})
    r = run_bass_kernel_spmd(nc, [arrays], core_ids=[0])
    return r.results[0]["out_0_dram"]
```
